# Optimizing a Trainium2 kernel written in Bass

```python
import numpy as np
import jax
import jax.numpy as jnp

def _softmax(x, axis=-1):
    return jax.nn.softmax(x, axis=axis)

def _gelu(x):
    return jax.nn.gelu(x, approximate=True)

def _silu(x):
    return jax.nn.silu(x)

def _sigmoid(x):
    return jax.nn.sigmoid(x)

def _layernorm(x, axis=-1, eps=1e-05):
    m = jnp.mean(x, axis=axis, keepdims=True)
    v = jnp.var(x, axis=axis, keepdims=True)
    return (x - m) / jnp.sqrt(v + eps)

def _scatter_add(tgt, idx, src, axis=0):
    return tgt.at[idx].add(src)

def _segment_sum(src, seg, n):
    return jax.ops.segment_sum(src, seg, n)
kernel_name = 'mk_sandwich_d1_jaxref_r8_d91226'

def setup_inputs(seed: int=0):
    np.random.seed(seed)
    _w = jnp.asarray

    def _L0_attn_setup():
        import jax, jax.numpy as jnp
        import numpy as np
        B, S, E = (4, 256, 128)
        H, KVH = (16, 4)
        D = E // H
        QL, KVL = (64, 32)
        ROPE_BASE = 10000.0

        def _rope(x):
            d = x.shape[-1]
            inv_freq = 1.0 / ROPE_BASE ** (jnp.arange(0, d, 2, dtype=jnp.float32) / d)
            t = jnp.arange(x.shape[1], dtype=jnp.float32)
            freqs = jnp.outer(t, inv_freq)
            cos = jnp.cos(freqs)[None, :, None, :].astype(x.dtype)
            sin = jnp.sin(freqs)[None, :, None, :].astype(x.dtype)
            x1, x2 = (x[..., ::2], x[..., 1::2])
            r1 = x1 * cos - x2 * sin
            r2 = x1 * sin + x2 * cos
            return jnp.stack([r1, r2], axis=-1).reshape(x.shape)
        key = jax.random.key(seed)
        ks = jax.random.split(key, 7)
        s = 0.02
        return {'x': jax.random.normal(ks[0], (B, S, E), dtype=jnp.float32), 'Wqa': jax.random.normal(ks[1], (E, QL), dtype=jnp.float32) * s, 'Wqb': jax.random.normal(ks[2], (QL, E), dtype=jnp.float32) * s, 'Wkva': jax.random.normal(ks[3], (E, KVL), dtype=jnp.float32) * s, 'Wkvb': jax.random.normal(ks[4], (KVL, KVH * D * 2), dtype=jnp.float32) * s, 'Wout': jax.random.normal(ks[5], (E, E), dtype=jnp.float32) * s, 'bout': jax.random.normal(ks[6], (E,), dtype=jnp.float32) * s}
    _L0_attn_in = _L0_attn_setup()

    def _L0_ffn_setup():
        import jax, jax.numpy as jnp
        import numpy as np
        DIM = 128
        DEPTH = 2
        HEADS = 8
        DIM_HEAD = 64
        WINDOW = 64
        INNER = HEADS * DIM_HEAD
        HID = int(DIM * 4 * 2 / 3)
        B, N = (2, 1024)
        QK_SCALE = 8.0

        def shift_token(t):
            t1, t2 = jnp.split(t, 2, axis=-1)
            t2 = jnp.pad(t2, ((0, 0), (1, 0), (0, 0)))[:, :-1]
            return jnp.concatenate([t1, t2], axis=-1)

        def l2norm(t):
            return t / jnp.clip(jnp.linalg.norm(t, axis=-1, keepdims=True), 1e-12)

        def rotate_half(x):
            x1, x2 = jnp.split(x, 2, axis=-1)
            return jnp.concatenate([-x2, x1], axis=-1)

        def rotary_xpos(q, k):
            n = q.shape[-2]
            half_idx = jnp.arange(0, DIM_HEAD, 2, dtype=jnp.float32)
            inv_freq = 1.0 / 10000.0 ** (half_idx / DIM_HEAD)
            t = jnp.arange(n, dtype=jnp.float32)
            freqs = t[:, None] * inv_freq[None, :]
            freqs = jnp.concatenate([freqs, freqs], axis=-1)
            base = (half_idx + 0.4 * DIM_HEAD) / (1.4 * DIM_HEAD)
            power = (t - n // 2) / float(WINDOW // 2)
            scale = base[None, :] ** power[:, None]
            scale = jnp.concatenate([scale, scale], axis=-1)
            cos, sin = (jnp.cos(freqs), jnp.sin(freqs))
            q = q * cos * scale + rotate_half(q) * sin * scale
            k = k * cos / scale + rotate_half(k) * sin / scale
            return (q, k)

        def local_attention(q, k, v):
            b, h, n, d = q.shape
            w = n // WINDOW
            bq = q.reshape(b, h, w, WINDOW, d) * QK_SCALE
            bk = k.reshape(b, h, w, WINDOW, d)
            bv = v.reshape(b, h, w, WINDOW, d)

            def look_around(t):
                p = jnp.pad(t, ((0, 0), (0, 0), (1, 0), (0, 0), (0, 0)))
                return jnp.concatenate([p[:, :, :w], p[:, :, 1:]], axis=3)
            bk, bv = (look_around(bk), look_around(bv))
            bt = jnp.arange(n).reshape(w, WINDOW)
            btp = jnp.pad(bt, ((1, 0), (0, 0)), constant_values=-1)
            btk = jnp.concatenate([btp[:w], btp[1:]], axis=1)
            sim = jnp.einsum('bhwid,bhwjd->bhwij', bq, bk)
            i = bt[:, :, None]
            j = btk[:, None, :]
            mask = (i < j) | (i > j + WINDOW) | (j == -1)
            sim = jnp.where(mask, -jnp.finfo(sim.dtype).max, sim)
            attn = jax.nn.softmax(sim, axis=-1)
            out = jnp.einsum('bhwij,bhwjd->bhwid', attn, bv)
            return out.reshape(b, h, n, d)

        def _layer(x, wqkv, qs, ksc, wo, lg, lb, w1, b1, w2, b2):
            b, n, _ = x.shape
            h = shift_token(x)
            qkv = h @ wqkv
            q, k, v = jnp.split(qkv, 3, axis=-1)
            to_heads = lambda t: t.reshape(b, n, HEADS, DIM_HEAD).transpose(0, 2, 1, 3)
            q, k, v = (to_heads(q), to_heads(k), to_heads(v))
            q = l2norm(q) * qs
            k = l2norm(k) * ksc
            q, k = rotary_xpos(q, k)
            o = local_attention(q, k, v)
            o = o.transpose(0, 2, 1, 3).reshape(b, n, INNER)
            x = x + o @ wo
            h = shift_token(x)
            mu = h.mean(-1, keepdims=True)
            var = h.var(-1, keepdims=True)
            h = (h - mu) / jnp.sqrt(var + 1e-05) * lg + lb
            h = h @ w1 + b1
            a, g = jnp.split(h, 2, axis=-1)
            h = a * jax.nn.gelu(g, approximate=False)
            x = x + h @ w2 + b2
            return x
        key = jax.random.key(seed)
        ks = jax.random.split(key, 6)
        return {'x': jax.random.normal(ks[0], (B, N, DIM), jnp.float32), 'wqkv': jax.random.normal(ks[1], (DEPTH, DIM, 3 * INNER), jnp.float32) * 0.02, 'q_scale': jnp.ones((DEPTH, DIM_HEAD), jnp.float32), 'k_scale': jnp.ones((DEPTH, DIM_HEAD), jnp.float32), 'wo': jax.random.normal(ks[2], (DEPTH, INNER, DIM), jnp.float32) * 0.02, 'ln_g': jnp.ones((DEPTH, DIM), jnp.float32), 'ln_b': jnp.zeros((DEPTH, DIM), jnp.float32), 'w1': jax.random.normal(ks[3], (DEPTH, DIM, 2 * HID), jnp.float32) * 0.02, 'b1': jnp.zeros((DEPTH, 2 * HID), jnp.float32), 'w2': jax.random.normal(ks[4], (DEPTH, HID, DIM), jnp.float32) * 0.02, 'b2': jnp.zeros((DEPTH, DIM), jnp.float32)}
    _L0_ffn_in = _L0_ffn_setup()
    _d = {'L0_attn_x': _L0_attn_in['x'], 'L0_attn_Wqa': _L0_attn_in['Wqa'], 'L0_attn_Wqb': _L0_attn_in['Wqb'], 'L0_attn_Wkva': _L0_attn_in['Wkva'], 'L0_attn_Wkvb': _L0_attn_in['Wkvb'], 'L0_attn_Wout': _L0_attn_in['Wout'], 'L0_attn_bout': _L0_attn_in['bout'], 'L0_ffn_wqkv': _L0_ffn_in['wqkv'], 'L0_ffn_q_scale': _L0_ffn_in['q_scale'], 'L0_ffn_k_scale': _L0_ffn_in['k_scale'], 'L0_ffn_wo': _L0_ffn_in['wo'], 'L0_ffn_ln_g': _L0_ffn_in['ln_g'], 'L0_ffn_ln_b': _L0_ffn_in['ln_b'], 'L0_ffn_w1': _L0_ffn_in['w1'], 'L0_ffn_b1': _L0_ffn_in['b1'], 'L0_ffn_w2': _L0_ffn_in['w2'], 'L0_ffn_b2': _L0_ffn_in['b2']}
    _x0 = _d['L0_attn_x']
    _d['L0_attn_x'] = jax.random.normal(jax.random.fold_in(jax.random.key(seed), 1), (8, 256, 128), dtype=_x0.dtype)
    del _x0
    return _d

def reference(L0_attn_x, L0_attn_Wqa, L0_attn_Wqb, L0_attn_Wkva, L0_attn_Wkvb, L0_attn_Wout, L0_attn_bout, L0_ffn_wqkv, L0_ffn_q_scale, L0_ffn_k_scale, L0_ffn_wo, L0_ffn_ln_g, L0_ffn_ln_b, L0_ffn_w1, L0_ffn_b1, L0_ffn_w2, L0_ffn_b2):

    def _L0_attn_ref(x, Wqa, Wqb, Wkva, Wkvb, Wout, bout):
        import jax, jax.numpy as jnp
        import numpy as np
        B, S, E = (4, 256, 128)
        H, KVH = (16, 4)
        D = E // H
        QL, KVL = (64, 32)
        ROPE_BASE = 10000.0

        def _rope(x):
            d = x.shape[-1]
            inv_freq = 1.0 / ROPE_BASE ** (jnp.arange(0, d, 2, dtype=jnp.float32) / d)
            t = jnp.arange(x.shape[1], dtype=jnp.float32)
            freqs = jnp.outer(t, inv_freq)
            cos = jnp.cos(freqs)[None, :, None, :].astype(x.dtype)
            sin = jnp.sin(freqs)[None, :, None, :].astype(x.dtype)
            x1, x2 = (x[..., ::2], x[..., 1::2])
            r1 = x1 * cos - x2 * sin
            r2 = x1 * sin + x2 * cos
            return jnp.stack([r1, r2], axis=-1).reshape(x.shape)
        b, s, _ = x.shape
        scale = D ** (-0.5)
        q = (x @ Wqa @ Wqb).reshape(b, s, H, D)
        kv = (x @ Wkva @ Wkvb).reshape(b, s, KVH, D, 2)
        k, v = (kv[..., 0], kv[..., 1])
        q = _rope(q)
        k = _rope(k)
        g = H // KVH
        k = jnp.repeat(k, g, axis=2)
        v = jnp.repeat(v, g, axis=2)
        scores = jnp.einsum('bqhd,bkhd->bhqk', q, k) * scale
        causal = jnp.triu(jnp.ones((s, s), dtype=bool), k=1)
        scores = jnp.where(causal[None, None], -jnp.inf, scores)
        w = jax.nn.softmax(scores, axis=-1)
        out = jnp.einsum('bhqk,bkhd->bqhd', w, v).reshape(b, s, E)
        return out @ Wout + bout

    def _L0_ffn_ref(x, wqkv, q_scale, k_scale, wo, ln_g, ln_b, w1, b1, w2, b2):
        import jax, jax.numpy as jnp
        import numpy as np
        DIM = 128
        DEPTH = 2
        HEADS = 8
        DIM_HEAD = 64
        WINDOW = 64
        INNER = HEADS * DIM_HEAD
        HID = int(DIM * 4 * 2 / 3)
        B, N = (2, 1024)
        QK_SCALE = 8.0

        def shift_token(t):
            t1, t2 = jnp.split(t, 2, axis=-1)
            t2 = jnp.pad(t2, ((0, 0), (1, 0), (0, 0)))[:, :-1]
            return jnp.concatenate([t1, t2], axis=-1)

        def l2norm(t):
            return t / jnp.clip(jnp.linalg.norm(t, axis=-1, keepdims=True), 1e-12)

        def rotate_half(x):
            x1, x2 = jnp.split(x, 2, axis=-1)
            return jnp.concatenate([-x2, x1], axis=-1)

        def rotary_xpos(q, k):
            n = q.shape[-2]
            half_idx = jnp.arange(0, DIM_HEAD, 2, dtype=jnp.float32)
            inv_freq = 1.0 / 10000.0 ** (half_idx / DIM_HEAD)
            t = jnp.arange(n, dtype=jnp.float32)
            freqs = t[:, None] * inv_freq[None, :]
            freqs = jnp.concatenate([freqs, freqs], axis=-1)
            base = (half_idx + 0.4 * DIM_HEAD) / (1.4 * DIM_HEAD)
            power = (t - n // 2) / float(WINDOW // 2)
            scale = base[None, :] ** power[:, None]
            scale = jnp.concatenate([scale, scale], axis=-1)
            cos, sin = (jnp.cos(freqs), jnp.sin(freqs))
            q = q * cos * scale + rotate_half(q) * sin * scale
            k = k * cos / scale + rotate_half(k) * sin / scale
            return (q, k)

        def local_attention(q, k, v):
            b, h, n, d = q.shape
            w = n // WINDOW
            bq = q.reshape(b, h, w, WINDOW, d) * QK_SCALE
            bk = k.reshape(b, h, w, WINDOW, d)
            bv = v.reshape(b, h, w, WINDOW, d)

            def look_around(t):
                p = jnp.pad(t, ((0, 0), (0, 0), (1, 0), (0, 0), (0, 0)))
                return jnp.concatenate([p[:, :, :w], p[:, :, 1:]], axis=3)
            bk, bv = (look_around(bk), look_around(bv))
            bt = jnp.arange(n).reshape(w, WINDOW)
            btp = jnp.pad(bt, ((1, 0), (0, 0)), constant_values=-1)
            btk = jnp.concatenate([btp[:w], btp[1:]], axis=1)
            sim = jnp.einsum('bhwid,bhwjd->bhwij', bq, bk)
            i = bt[:, :, None]
            j = btk[:, None, :]
            mask = (i < j) | (i > j + WINDOW) | (j == -1)
            sim = jnp.where(mask, -jnp.finfo(sim.dtype).max, sim)
            attn = jax.nn.softmax(sim, axis=-1)
            out = jnp.einsum('bhwij,bhwjd->bhwid', attn, bv)
            return out.reshape(b, h, n, d)

        def _layer(x, wqkv, qs, ksc, wo, lg, lb, w1, b1, w2, b2):
            b, n, _ = x.shape
            h = shift_token(x)
            qkv = h @ wqkv
            q, k, v = jnp.split(qkv, 3, axis=-1)
            to_heads = lambda t: t.reshape(b, n, HEADS, DIM_HEAD).transpose(0, 2, 1, 3)
            q, k, v = (to_heads(q), to_heads(k), to_heads(v))
            q = l2norm(q) * qs
            k = l2norm(k) * ksc
            q, k = rotary_xpos(q, k)
            o = local_attention(q, k, v)
            o = o.transpose(0, 2, 1, 3).reshape(b, n, INNER)
            x = x + o @ wo
            h = shift_token(x)
            mu = h.mean(-1, keepdims=True)
            var = h.var(-1, keepdims=True)
            h = (h - mu) / jnp.sqrt(var + 1e-05) * lg + lb
            h = h @ w1 + b1
            a, g = jnp.split(h, 2, axis=-1)
            h = a * jax.nn.gelu(g, approximate=False)
            x = x + h @ w2 + b2
            return x
        for l in range(DEPTH):
            x = _layer(x, wqkv[l], q_scale[l], k_scale[l], wo[l], ln_g[l], ln_b[l], w1[l], b1[l], w2[l], b2[l])
        return x
    x = L0_attn_x
    x = x + _layernorm(_L0_attn_ref(_layernorm(x, axis=-1), L0_attn_Wqa, L0_attn_Wqb, L0_attn_Wkva, L0_attn_Wkvb, L0_attn_Wout, L0_attn_bout), axis=-1)
    x = x + _layernorm(_L0_ffn_ref(_layernorm(x, axis=-1), L0_ffn_wqkv, L0_ffn_q_scale, L0_ffn_k_scale, L0_ffn_wo, L0_ffn_ln_g, L0_ffn_ln_b, L0_ffn_w1, L0_ffn_b1, L0_ffn_w2, L0_ffn_b2), axis=-1)
    return x

_drawn_inputs = setup_inputs


def setup_inputs(seed=0):
    import zlib

    import numpy as np

    out = dict(_drawn_inputs(seed))
    spreads = {'L0_ffn_q_scale': (1.0, 0.6),
     'L0_ffn_k_scale': (1.0, 0.6),
     'L0_ffn_ln_g': (1.0, 0.6),
     'L0_ffn_ln_b': (0.0, 0.8),
     'L0_ffn_b1': (0.0, 0.8),
     'L0_ffn_b2': (0.0, 0.8)}
    factors = {'L0_attn_Wqa': 64.0, 'L0_attn_Wqb': 64.0, 'L0_ffn_w1': 7.796, 'L0_ffn_w2': 7.542}
    for name, (base, spread) in spreads.items():
        noise = np.random.default_rng([zlib.crc32(name.encode()), seed]).standard_normal(out[name].shape)
        drawn = base * np.exp(spread * noise) if base else spread * noise
        out[name] = jnp.asarray(drawn.astype(out[name].dtype))
    for name, factor in factors.items():
        out[name] = (out[name] * factor).astype(out[name].dtype)
    return out
```

```python
import numpy as np
import concourse.bass as bass
from concourse import mybir
from contextlib import ExitStack

FP32 = mybir.dt.float32
BF16 = mybir.dt.bfloat16
ALU = mybir.AluOpType
ACT = mybir.ActivationFunctionType
AX = mybir.AxisListType

PARTS = 128
BATCH, SEQ, DIM = 8, 256, 128
TILES = SEQ // PARTS

A_HEADS, A_KV = 16, 4
A_D = DIM // A_HEADS
A_GROUP = A_HEADS // A_KV
A_QL, A_KVL = 64, 32
A_QK = A_HEADS + A_KV
A_SCALE = A_D ** -0.5
SPLIT = 3
A_STACK = SPLIT * SPLIT * A_D

DEPTH, HEADS, HD = 2, 8, 64
WINDOW = 64
INNER = HEADS * HD
PAIRS = HEADS // 2
QK_SCALE = 8.0
HID = int(DIM * 4 * 2 / 3)
HCH = [(c, min(PARTS, HID - c)) for c in range(0, HID, PARTS)]
NCH = len(HCH)
GROUPS = BATCH // 2
GT = 2 * TILES
EPS = 1e-5
TINY = 1e-24
NEG = -1e30

C_ID = 0
C_MA = C_ID + PARTS
C_MB0 = C_MA + PARTS
C_MB1 = C_MB0 + PARTS
B1K = SEQ - WINDOW
C_RA = C_MB1 + B1K
C_RB = C_RA + 2 * TILES * A_D
C_END = C_RB + 2 * TILES * 2 * HD


def shape_constants():
    f = np.float32
    c = np.zeros((PARTS, C_END), f)
    q = np.arange(PARTS)[:, None]
    k = np.arange(PARTS)[None, :]
    c[:, C_ID:C_MA] = np.eye(PARTS)
    c[:, C_MA:C_MB0] = np.where(k > q, NEG, 0)
    c[:, C_MB0:C_MB1] = np.where((k > q) | (q > k + WINDOW), NEG, 0)
    q1, k1 = q + PARTS, np.arange(B1K)[None, :] + WINDOW
    c[:, C_MB1:C_RA] = np.where((k1 > q1) | (q1 > k1 + WINDOW), NEG, 0)
    t = np.arange(SEQ, dtype=f)

    inv = f(1.0) / f(10000.0) ** (np.arange(0, A_D, 2, dtype=f) / f(A_D))
    ang = np.outer(t, inv).astype(f)
    cos, sin = np.repeat(np.cos(ang), 2, 1), np.repeat(np.sin(ang), 2, 1)
    sin[:, 0::2] *= -1
    for n, tab in enumerate((cos, sin)):
        w = TILES * A_D
        c[:, C_RA + n * w:C_RA + (n + 1) * w] = tab.reshape(TILES, PARTS, A_D).transpose(1, 0, 2).reshape(PARTS, w)

    half = np.arange(0, HD, 2, dtype=f)
    inv = f(1.0) / f(10000.0) ** (half / f(HD))
    ang = t[:, None] * inv[None, :]
    cos, sin = np.cos(ang), np.sin(ang)
    base = (half + f(0.4 * HD)) / f(1.4 * HD)
    scale = base[None, :] ** ((t - f(SEQ // 2)) / f(WINDOW // 2))[:, None]
    for n, (lo, hi) in enumerate(((cos, cos), (-sin, sin))):
        tab = np.concatenate([lo, hi], 1)
        both = np.stack([tab * np.tile(scale, 2), tab / np.tile(scale, 2)], 1).astype(f)
        w = TILES * 2 * HD
        c[:, C_RB + n * w:C_RB + (n + 1) * w] = both.reshape(TILES, PARTS, 2, HD).transpose(1, 0, 2, 3).reshape(PARTS, w)
    return c


ONE = 1


class Own:

    def __init__(self, eng, sem, per):
        self.eng, self.sem, self.per, self.n, self.base = eng, sem, per, 0, 0

    def begin(self, index):
        self.base, self.n = index * self.per, 0

    def end(self):
        assert self.n == self.per, (self.sem.name, self.n, self.per)

    def step(self, ins):
        self.n += 1
        ins.then_inc(self.sem, 1)
        self.eng.wait_ge(self.sem, self.base + self.n)


def build_program(nc, a, out):
    ctx = ExitStack()
    with ctx:
        def sb(name, shape, dt=FP32):
            return ctx.enter_context(nc.sbuf_tensor(name, shape, dt))

        def pb(name, shape, dt=FP32):
            return ctx.enter_context(nc.psum_tensor(name, shape, dt))

        def sem(name):
            return ctx.enter_context(nc.semaphore(name))

        const = sb("const", [PARTS, C_END])
        ident = const[:, C_ID:C_MA]
        cos_a = const[:, C_RA:C_RA + TILES * A_D].rearrange("p (t d) -> p t d", t=TILES)
        sin_a = const[:, C_RA + TILES * A_D:C_RB].rearrange("p (t d) -> p t d", t=TILES)
        rot_raw = const[:, C_RB:C_END].rearrange("p (n t c d) -> p n t c d", n=2, t=TILES, c=2)
        ident_h = sb("ident_h", [PARTS, PARTS], BF16)
        mask_a0 = sb("mask_a0", [PARTS, 4, PARTS], BF16)
        mask_a1 = sb("mask_a1", [PARTS, 2, 2, PARTS], BF16)
        mask_b0 = sb("mask_b0", [PARTS, 4, PARTS], BF16)
        mask_b1 = sb("mask_b1", [PARTS, 2, B1K], BF16)
        minus_half = sb("minus_half", [PARTS, 16])

        x_all = sb("x_all", [PARTS, BATCH, TILES, DIM])
        xT = sb("xT", [PARTS, BATCH, SEQ])

        wqa = sb("wqa", [PARTS, A_QL])
        wkva = sb("wkva", [PARTS, A_KVL])
        wqb = sb("wqb", [A_QL, DIM])
        wkvb = sb("wkvb", [A_KVL, 2 * A_KV * A_D])
        wqaT = sb("wqaT", [A_QL, PARTS])
        wkvaT = sb("wkvaT", [A_KVL, PARTS])
        A_W = DIM + 2 * A_KV * A_D
        w_a = sb("w_a", [PARTS, A_W])
        wout = sb("wout", [PARTS, DIM])
        bout = sb("bout", [PARTS, DIM])

        st = sb("st", [PARTS, TILES, 6])
        mv = sb("mv", [PARTS, TILES, 2])
        ve = sb("ve", [PARTS, TILES])
        rs1 = sb("rs1", [PARTS, TILES])
        xn = sb("xn", [PARTS, TILES, DIM])
        xnT = sb("xnT", [PARTS, SEQ])
        rope_c = sb("rope_c", [PARTS, TILES, A_QK, A_D])
        rope_s = sb("rope_s", [PARTS, TILES, A_QK, A_D])
        v_new = sb("v_new", [PARTS, TILES, A_KV * A_D])
        v_a = sb("v_a", [PARTS, TILES, A_KV * A_D])
        rest = sb("rest", [PARTS, TILES, A_QK, A_D])
        stack = sb("stack", [PARTS, TILES, A_QK, SPLIT, SPLIT, A_D], BF16)
        qkT_a = sb("qkT_a", [A_STACK, A_QK, SEQ], BF16)
        p_a = sb("p_a", [PARTS, A_HEADS, PARTS + SEQ])
        mx_a = sb("mx_a", [PARTS, TILES, A_HEADS])
        nm_a = sb("nm_a", [PARTS, TILES, A_HEADS])
        sum_a = sb("sum_a", [PARTS, TILES, A_HEADS])
        inv_a = sb("inv_a", [PARTS, TILES, A_HEADS])
        pT_a = sb("pT_a", [PARTS, 4, PARTS + SEQ])
        o_a = sb("o_a", [PARTS, TILES, DIM])
        oT_a = sb("oT_a", [PARTS, SEQ])
        y_a = sb("y_a", [PARTS, TILES, DIM])
        z_a = sb("z_a", [PARTS, TILES, DIM])
        st2 = sb("st2", [PARTS, TILES, 6])
        mv2 = sb("mv2", [PARTS, TILES, 2])
        ve2 = sb("ve2", [PARTS, TILES])
        rs2 = sb("rs2", [PARTS, TILES])

        wqkv = sb("wqkv", [PARTS, 3 * INNER])
        wo = sb("wo", [PARTS, PAIRS, DIM])
        scales = sb("scales", [PARTS, 2, HD])
        tab_c = sb("tab_c", [PARTS, TILES, 2, HD])
        tab_s = sb("tab_s", [PARTS, TILES, 2, HD])
        hT = sb("hT", [PARTS, SEQ])
        sq = sb("sq", [PARTS, 2, INNER])
        ss = sb("ss", [PARTS, TILES, 2 * HEADS])
        r_qk = sb("r_qk", [PARTS, TILES, 2 * HEADS])
        r_q8 = sb("r_q8", [PARTS, TILES, HEADS])
        rc = sb("rc", [PARTS, TILES, 2, INNER])
        rs = sb("rs", [PARTS, TILES, 2, INNER])
        qkT = sb("qkT", [PARTS, 2, PAIRS, SEQ])
        v_b = sb("v_b", [PARTS, TILES, INNER])
        p_b0 = sb("p_b0", [PARTS, HEADS, PARTS])
        p_b1 = sb("p_b1", [PARTS, HEADS, SEQ])
        mx_b = sb("mx_b", [PARTS, TILES, HEADS])
        nm_b = sb("nm_b", [PARTS, TILES, HEADS])
        scq_b = sb("scq_b", [PARTS, TILES, HEADS])
        sum_b = sb("sum_b", [PARTS, TILES, HEADS])
        inv_b = sb("inv_b", [PARTS, TILES, HEADS])
        pT_b = sb("pT_b", [PARTS, 4, PARTS + SEQ])
        oT_b = sb("oT_b", [PARTS, PAIRS, SEQ])

        w1 = sb("w1", [PARTS, 2 * HID])
        w2 = sb("w2", [PARTS, NCH, DIM])
        b1 = sb("b1", [PARTS, 2, NCH])
        b2 = sb("b2", [PARTS, 1])
        ln_g = sb("ln_g", [PARTS, 1])
        ln_b = sb("ln_b", [PARTS, 1])
        hTf = sb("hTf", [PARTS, 2, SEQ])
        stf = sb("stf", [PARTS, GT, 6])
        mvf = sb("mvf", [PARTS, GT, 2])
        vef = sb("vef", [PARTS, GT])
        rsf = sb("rsf", [PARTS, GT])
        yf = sb("yf", [PARTS, GT, DIM])
        yfT = sb("yfT", [PARTS, GT * PARTS])
        gate = sb("gate", [PARTS, NCH, GT * PARTS])
        act = sb("act", [PARTS, NCH, GT * PARTS])
        stl = sb("stl", [PARTS, GROUPS, GT, 6])
        mvl = sb("mvl", [PARTS, GROUPS, GT, 2])
        vel = sb("vel", [PARTS, GROUPS * GT])
        rsl = sb("rsl", [PARTS, GROUPS * GT])
        xl = sb("xl", [PARTS, GROUPS, GT, DIM])

        bank = [pb(f"bank{i}", [PARTS, 1024]) for i in range(4)]

        ld_c, ld_x0, ld_x, ld_w = sem("ld_c"), sem("ld_x0"), sem("ld_x"), sem("ld_w")
        ld_att, ld_ffn = sem("ld_att"), sem("ld_ffn")
        st_out = sem("st_out")
        names = {}

        def S(name):
            if name not in names:
                names[name] = sem(name)
            return names[name]

        block = ctx.enter_context(nc.Block())

        def plain(eng):
            eng.sem_inc(S("plain"), 1)

        def full(i):
            return bank[i // 2][:, (i % 2) * 512:(i % 2) * 512 + 512]

        sc_a = [bank[0], bank[1]]
        USES_A = [(0, 0, 8), (1, 0, 4), (1, 4, 4), (0, 8, 8), (1, 8, 4), (1, 12, 4)]
        NUA = len(USES_A)
        pt_a = [full(4), full(5)]
        ov_a = full(6)
        misc_a = full(7)

        def keys_a(qt):
            return (qt + 1) * PARTS

        def p_slice_a(qt, h):
            return p_a[:, h, 0:PARTS] if qt == 0 else p_a[:, h, PARTS:PARTS + SEQ]

        USES_B = [(0, (0, 2, 4, 6)), (0, (1, 3, 5, 7)), (1, (0, 2)), (1, (1, 3)), (1, (4, 6)), (1, (5, 7))]
        NUB = len(USES_B)
        sc_b = [full(2), full(3), full(4)]
        pj = bank[0]
        pt_b = [full(5), full(6)]
        ov_b = full(7)

        def keys_b(qt):
            return PARTS if qt == 0 else B1K

        def p_slice_b(qt, h):
            return p_b0[:, h, :] if qt == 0 else p_b1[:, h, WINDOW:SEQ]

        lnf = [full(0), full(1)]
        up = [[full(2), full(3)], [full(4), full(5)]]
        down = full(6)

        @block.sync
        def _(e):
            e.dma_start(const[:, :], a["consts"]).then_inc(ld_c, 16)
            e.dma_start(x_all[:, 0, :, :], a["L0_attn_x"][0].rearrange("(t p) d -> p t d", p=PARTS)).then_inc(ld_x0, 16)
            e.dma_start(wqa[:, :], a["L0_attn_Wqa"]).then_inc(ld_w, 16)
            e.dma_start(wkva[:, :], a["L0_attn_Wkva"]).then_inc(ld_w, 16)
            e.dma_start(wqb[:, :], a["L0_attn_Wqb"]).then_inc(ld_w, 16)
            e.dma_start(wkvb[:, :], a["L0_attn_Wkvb"]).then_inc(ld_w, 16)
            e.dma_start(wout[:, :], a["L0_attn_Wout"]).then_inc(ld_w, 16)
            e.dma_start(bout[:, :], a["L0_attn_bout"].unsqueeze(0).broadcast_to([PARTS, DIM])).then_inc(ld_w, 16)
            e.dma_start(x_all[:, 1:BATCH, :, :],
                        a["L0_attn_x"][1:BATCH].rearrange("b (t p) d -> p b t d", p=PARTS)).then_inc(ld_x, 16)
            with e.Fori(0, DEPTH) as l:
                e.wait_ge(S("b_y"), ONE + l * BATCH)
                plain(e)
                one = bass.ds(l, 1)
                e.dma_start(wqkv[:, :], a["L0_ffn_wqkv"][one, :, :].rearrange("o p n -> p (o n)")).then_inc(ld_att, 16)
                e.dma_start(wo[:, :, :], a["L0_ffn_wo"][one, :, :].rearrange("o (c p) n -> p (o c) n", p=PARTS)).then_inc(ld_att, 16)
                e.dma_start(scales[:, 0, :], a["L0_ffn_q_scale"][one, :].broadcast_to([PARTS, HD])).then_inc(ld_att, 16)
                e.dma_start(scales[:, 1, :], a["L0_ffn_k_scale"][one, :].broadcast_to([PARTS, HD])).then_inc(ld_att, 16)
                e.wait_ge(S("f_x"), ONE + l * GROUPS)
                plain(e)
                e.dma_start(w1[:, :], a["L0_ffn_w1"][one, :, :].rearrange("o p n -> p (o n)")).then_inc(ld_ffn, 16)
                w2l = a["L0_ffn_w2"][one, :, :]
                b1l = a["L0_ffn_b1"][one, :]
                for c, (h0, n) in enumerate(HCH):
                    e.dma_start(w2[0:n, c, :], w2l[:, h0:h0 + n, :].rearrange("o p n -> (o p) n")).then_inc(ld_ffn, 16)
                    for half in range(2):
                        col = half * HID + h0
                        e.dma_start(b1[0:n, half, c:c + 1], b1l[:, col:col + n].rearrange("o p -> p o")).then_inc(ld_ffn, 16)
                e.dma_start(b2[:, :], a["L0_ffn_b2"][one, :].rearrange("o p -> p o")).then_inc(ld_ffn, 16)
                e.dma_start(ln_g[:, :], a["L0_ffn_ln_g"][one, :].rearrange("o p -> p o")).then_inc(ld_ffn, 16)
                e.dma_start(ln_b[:, :], a["L0_ffn_ln_b"][one, :].rearrange("o p -> p o")).then_inc(ld_ffn, 16)
            with e.Fori(0, GROUPS) as g:
                e.wait_ge(S("last_done"), g + 1)
                e.dma_start(out[bass.ds(g * 2, 2), :, :].rearrange("b (t p) d -> p (b t) d", p=PARTS),
                            xl[:, bass.ds(g, 1), :, :].rearrange("p o t d -> p (o t) d")).then_inc(st_out, 16)
            e.wait_ge(st_out, 16 * GROUPS)

        FFN_LOADS = 1 + 3 * NCH + 3

        @block.tensor
        def _(t):
            for name in ("a_xnT a_qkv a_st a_sc a_pT a_pv a_oT a_y a_h0T b_qk b_vp b_trT b_sc b_pT b_pv b_y f_h f_ty f_up "
                         "f_down").split():
                t.sem_inc(S(name), ONE)
            t.wait_ge(ld_c, 16)
            t.wait_ge(ld_w, 16 * 6)
            t.transpose(full(0)[0:A_QL, 0:PARTS], wqa[:, :], ident)
            t.transpose(full(0)[0:A_KVL, PARTS:2 * PARTS], wkva[:, :], ident).then_inc(S("w_t"), 1)
            t.wait_ge(S("w_copied"), 2)
            t.matmul(full(1)[:, 0:DIM], wqaT[:, :], wqb[:, :], start=True, stop=True)
            t.matmul(full(1)[:, DIM:A_W], wkvaT[:, :], wkvb[:, :], start=True, stop=True).then_inc(S("w_prod"), 1)
            t.wait_ge(S("consts_cast"), 1)

            def a_norm_t(b, first=False):
                t.wait_ge(S("a_xn"), ONE + b + 1)
                if not first:
                    t.wait_ge(S("a_h0T_out"), ONE + b - 1)
                for n in range(TILES):
                    m = t.transpose(misc_a[:, n * PARTS:(n + 1) * PARTS], xn[:, n, :], ident)
                m.then_inc(S("a_xnT"), 1)

            def a_proj(b):
                t.wait_ge(S("a_xnT_out"), ONE + b + 1)
                for n in range(TILES):
                    m = t.matmul(misc_a[:, n * A_W:(n + 1) * A_W], xnT[:, n * PARTS:(n + 1) * PARTS], w_a[:, :],
                                 start=True, stop=True)
                m.then_inc(S("a_qkv"), 1)

            def a_stack_t(b):
                t.wait_ge(S("a_stack"), ONE + b + 1)
                k = 0
                for n in range(TILES):
                    for h0 in range(0, A_QK, 8):
                        hs = min(8, A_QK - h0)
                        use = b * 6 + k
                        if k < 2:
                            t.wait_ge(S("a_pT_act" if k == 0 else "a_pT_dve"), ONE + b * (A_HEADS // 2))
                        else:
                            t.wait_ge(S("a_st_out"), ONE + use - 1)
                        dst = pt_a[k % 2].bitcast(BF16)
                        for h in range(h0, h0 + hs):
                            m = t.transpose(dst[0:A_STACK, (h - h0) * PARTS:(h - h0 + 1) * PARTS],
                                            stack[:, n, h, :, :, :].rearrange("p i j d -> p (i j d)"), ident_h[:, :])
                        m.then_inc(S("a_st"), 1)
                        k += 1

            def a_scores(b, u):
                qt, h0, nh = USES_A[u]
                use = b * NUA + u
                if u == 0:
                    t.wait_ge(S("a_st_out"), ONE + b * 6 + 6)
                t.wait_ge(S("a_exp"), ONE + (use - 1 if u else use))
                dst = sc_a[u % 2]
                per = 512 // keys_a(qt)
                mask = mask_a0 if qt == 0 else mask_a1
                for half in range(2):
                    m = t.matmul(dst[:, half * 512:half * 512 + 512], ident_h[:, :],
                                 mask[:, :, :].rearrange("p a b -> p (a b)") if qt == 0 else
                                 mask[:, :, :, :].rearrange("p a c b -> p (a c b)"), start=True, stop=False,
                                 skip_group_check=True)
                    for i in range(per):
                        h = h0 + half * per + i
                        c = half * 512 + i * keys_a(qt)
                        m = t.matmul(dst[:, c:c + keys_a(qt)], qkT_a[:, h, qt * PARTS:(qt + 1) * PARTS],
                                     qkT_a[:, A_HEADS + h // A_GROUP, 0:keys_a(qt)], start=False, stop=True,
                                     skip_group_check=True)
                m.then_inc(S("a_sc"), 1)

            def a_turn_p(b, h):
                use = b * A_HEADS + h
                u = [n for n, (qt, h0, nh) in enumerate(USES_A) if qt == 1 and h0 <= h < h0 + nh][0]
                t.wait_ge(S("a_exp"), ONE + b * NUA + u + 1)
                if h < 2:
                    t.wait_ge(S("a_st_out"), ONE + b * 6 + 5 + h)
                elif h % 2 == 0:
                    t.wait_ge(S("a_pT_act"), ONE + b * (A_HEADS // 2) + h // 2)
                else:
                    t.wait_ge(S("a_pT_dve"), ONE + b * (A_HEADS // 2) + h // 2)
                dst = pt_a[h % 2]
                for k in range(3):
                    m = t.transpose(dst[:, k * PARTS:(k + 1) * PARTS], p_a[:, h, k * PARTS:(k + 1) * PARTS], ident)
                m.then_inc(S("a_pT"), 1)

            def a_values(b, h):
                even = h % 2 == 0
                t.wait_ge(S("a_pT_act" if even else "a_pT_dve"), ONE + b * (A_HEADS // 2) + h // 2 + 1)
                if h == 0:
                    t.wait_ge(S("a_v"), ONE + b + 1)
                    t.wait_ge(S("a_o"), ONE + b)
                kv = h // A_GROUP
                for qt in range(TILES):
                    for kb in range(qt + 1):
                        blk = qt + kb
                        m = t.matmul(ov_a[:, qt * DIM + h * A_D:qt * DIM + (h + 1) * A_D],
                                     pT_a[:, h % 4, blk * PARTS:(blk + 1) * PARTS],
                                     v_a[:, kb, kv * A_D:(kv + 1) * A_D], start=(kb == 0), stop=(kb == qt))
                m.then_inc(S("a_pv"), 1)

            def a_out(b, more):
                t.wait_ge(S("a_o"), ONE + b + 1)
                if more:
                    t.wait_ge(S("a_rope"), ONE + b + 2)
                else:
                    t.wait_ge(S("a_h0T_out"), ONE + b)
                for n in range(TILES):
                    m = t.transpose(misc_a[:, n * PARTS:(n + 1) * PARTS], o_a[:, n, :], ident)
                m.then_inc(S("a_oT"), 1)
                t.wait_ge(S("a_oT_out"), ONE + b + 1)
                for n in range(TILES):
                    m = t.matmul(misc_a[:, n * DIM:(n + 1) * DIM], oT_a[:, n * PARTS:(n + 1) * PARTS], wout[:, :],
                                 start=True, stop=True)
                m.then_inc(S("a_y"), 1)

            def a_h0(b):
                t.wait_ge(S("a_h0"), ONE + b + 1)
                for n in range(TILES):
                    m = t.transpose(misc_a[:, n * PARTS:(n + 1) * PARTS], z_a[:, n, :], ident)
                m.then_inc(S("a_h0T"), 1)

            def a_body(b, more):
                a_scores(b, 0)
                a_scores(b, 1)
                if more:
                    a_norm_t(b + 1)
                a_scores(b, 2)
                a_scores(b, 3)
                if more:
                    a_proj(b + 1)
                for h in range(4):
                    a_turn_p(b, h)
                    if h >= 1:
                        a_values(b, h - 1)
                a_scores(b, 4)
                for h in range(4, 8):
                    a_turn_p(b, h)
                    a_values(b, h - 1)
                a_scores(b, 5)
                for h in range(8, A_HEADS):
                    a_turn_p(b, h)
                    a_values(b, h - 1)
                a_values(b, A_HEADS - 1)
                if more:
                    a_stack_t(b + 1)
                a_out(b, more)
                a_h0(b)

            t.wait_ge(S("w_ready"), 2)
            a_norm_t(0, first=True)
            a_proj(0)
            a_stack_t(0)
            with t.Fori(0, BATCH - 1) as b:
                a_body(b, True)
            a_body(BATCH - 1, False)

            def b_proj(i, n):
                if n == 0:
                    t.wait_ge(S("b_hT"), ONE + 2 * i + 2)
                    t.wait_ge(S("b_trT_out"), ONE + 4 * i)
                else:
                    t.wait_ge(S("b_rot"), ONE + 2 * i + 1)
                for c in range(2):
                    m = t.matmul(pj[:, c * INNER:(c + 1) * INNER], hT[:, n * PARTS:(n + 1) * PARTS],
                                 wqkv[:, c * INNER:(c + 1) * INNER], start=True, stop=True)
                m.then_inc(S("b_qk"), 1)

            def b_v(i):
                t.wait_ge(S("b_rot"), ONE + 2 * i + 2)
                for n in range(TILES):
                    m = t.matmul(pj[:, n * INNER:(n + 1) * INNER], hT[:, n * PARTS:(n + 1) * PARTS],
                                 wqkv[:, 2 * INNER:3 * INNER], start=True, stop=True)
                    m.then_inc(S("b_vp"), 1)

            def b_turn_qk(i):
                for n in range(TILES):
                    t.wait_ge(S("b_qkr"), ONE + 2 * i + n + 1)
                    for c in range(2):
                        if n == 0:
                            t.wait_ge(S("b_v"), ONE + 2 * i + c + 1)
                        else:
                            t.wait_ge(S("b_trT_out"), ONE + 4 * i + c + 1)
                        for p in range(PAIRS):
                            m = t.transpose(pj[:, c * 512 + p * PARTS:c * 512 + (p + 1) * PARTS],
                                            rc[:, n, c, p * PARTS:(p + 1) * PARTS], ident)
                        m.then_inc(S("b_trT"), 1)

            def b_scores(i, u):
                qt, heads = USES_B[u]
                nk = keys_b(qt)
                if u == 0:
                    t.wait_ge(S("b_trT_out"), ONE + 4 * i + 4)
                t.wait_ge(S("b_exp"), ONE + i * NUB + u - 2) if u >= 2 else t.wait_ge(S("b_exp"), ONE + i * NUB)
                dst = sc_b[u % 3]
                mask = mask_b0[:, :, :] if qt == 0 else mask_b1[:, :, :]
                t.matmul(dst[:, 0:len(heads) * nk], ident_h[:, :], mask.rearrange("p a b -> p (a b)"),
                         start=True, stop=False, skip_group_check=True)
                for n, h in enumerate(heads):
                    r = (h % 2) * HD
                    m = t.matmul(dst[:, n * nk:(n + 1) * nk], qkT[r:r + HD, 0, h // 2, qt * PARTS:(qt + 1) * PARTS],
                                 qkT[r:r + HD, 1, h // 2, SEQ * 0 + (0 if qt == 0 else WINDOW):(PARTS if qt == 0 else SEQ)],
                                 start=False, stop=True, skip_group_check=True)
                m.then_inc(S("b_sc"), 1)

            def b_turn_p(i, h):
                t.wait_ge(S("b_p"), ONE + i * HEADS + h + 1)
                name = "b_pT_act" if h % 2 == 0 else "b_pT_dve"
                t.wait_ge(S(name), ONE + i * (HEADS // 2) + h // 2)
                dst = pt_b[h % 2]
                t.transpose(dst[:, 0:PARTS], p_b0[:, h, :], ident)
                for kb in range(2):
                    m = t.transpose(dst[:, (kb + 1) * PARTS:(kb + 2) * PARTS], p_b1[:, h, kb * PARTS:(kb + 1) * PARTS], ident)
                m.then_inc(S("b_pT"), 1)

            def b_values(i, p):
                t.wait_ge(S("b_pT_act"), ONE + i * (HEADS // 2) + p + 1)
                t.wait_ge(S("b_pT_dve"), ONE + i * (HEADS // 2) + p + 1)
                if p == 0:
                    t.wait_ge(S("b_x"), ONE + i)
                if p == 2:
                    t.wait_ge(S("b_o"), ONE + 2 * i + 1)
                for kb in range(2):
                    q0 = kb * PARTS
                    for k in range(2):
                        h = 2 * p + k
                        src = pT_b[:, h % 4, 0:SEQ] if kb == 0 else pT_b[:, h % 4, SEQ:SEQ + PARTS]
                        m = t.matmul(ov_b[k * HD:(k + 1) * HD, (p % 2) * SEQ + q0:(p % 2) * SEQ + SEQ],
                                     v_b[:, kb, h * HD:(h + 1) * HD], src, start=(kb == 0), stop=(kb == 1),
                                     skip_group_check=True)
                m.then_inc(S("b_pv"), 1)

            def b_out(i):
                t.wait_ge(S("b_o"), ONE + 2 * i + 2)
                for p in range(PAIRS):
                    m = t.matmul(ov_b[:, 0:SEQ], wo[:, p, :], oT_b[:, p, :], start=(p == 0), stop=(p == PAIRS - 1))
                m.then_inc(S("b_y"), 1)

            def b_body(i, more):
                b_scores(i, 0)
                b_scores(i, 1)
                b_scores(i, 2)
                if more:
                    b_proj(i + 1, 0)
                b_scores(i, 3)
                b_scores(i, 4)
                if more:
                    b_proj(i + 1, 1)
                b_scores(i, 5)
                for h in range(HEADS):
                    b_turn_p(i, h)
                    if h % 2 == 0 and h:
                        b_values(i, h // 2 - 1)
                b_values(i, PAIRS - 1)
                if more:
                    b_v(i + 1)
                    b_turn_qk(i + 1)
                b_out(i)

            def f_norm_t(i):
                t.wait_ge(S("f_hT"), ONE + 4 * i + 4)
                t.wait_ge(S("f_y"), ONE + i)
                for n in range(GT):
                    m = t.transpose(lnf[0][:, n * PARTS:(n + 1) * PARTS], hTf[:, n // TILES, (n % TILES) * PARTS:(n % TILES + 1) * PARTS], ident)
                m.then_inc(S("f_h"), 1)

            def f_back_t(i):
                t.wait_ge(S("f_y"), ONE + i + 1)
                t.wait_ge(S("f_yT"), ONE + i)
                for n in range(GT):
                    m = t.transpose(lnf[1][:, n * PARTS:(n + 1) * PARTS], yf[:, n, :], ident)
                m.then_inc(S("f_ty"), 1)

            def f_up(i, c):
                if c == 0:
                    t.wait_ge(S("f_yT"), ONE + i + 1)
                h0, n = HCH[c]
                use = i * NCH + c
                if c < 2:
                    t.wait_ge(S("f_act"), ONE + i * NCH)
                else:
                    t.wait_ge(S("f_act"), ONE + i * NCH + c - 1)
                for half in range(2):
                    col = (1 - half) * HID + h0
                    m = t.matmul(up[half][c % 2][0:n, :], w1[:, col:col + n], yfT[:, :], start=True, stop=True)
                    m.then_inc(S("f_up"), 1)

            def f_down(i, c):
                h0, n = HCH[c]
                t.wait_ge(S("f_act"), ONE + i * NCH + c + 1)
                if c == 0:
                    t.wait_ge(S("f_x"), ONE + i)
                m = t.matmul(down[:, :], w2[0:n, c, :], act[0:n, c, :], start=(c == 0), stop=(c == NCH - 1))
                if c == NCH - 1:
                    m.then_inc(S("f_down"), 1)

            def f_body(i, more):
                f_up(i, 0)
                f_up(i, 1)
                if more:
                    f_norm_t(i + 1)
                f_up(i, 2)
                f_down(i, 0)
                f_down(i, 1)
                f_down(i, 2)
                if more:
                    f_back_t(i + 1)

            with t.Fori(0, DEPTH) as l:
                i0 = l * BATCH
                t.wait_ge(ld_att, l * 64 + 64)
                t.wait_ge(S("a_h0T_out"), ONE + BATCH)
                t.wait_ge(S("f_x"), ONE + l * GROUPS)
                b_proj(i0, 0)
                b_proj(i0, 1)
                b_v(i0)
                b_turn_qk(i0)
                with t.Fori(0, BATCH - 1) as b:
                    b_body(i0 + b, True)
                b_body(i0 + (BATCH - 1), False)
                g0 = l * GROUPS
                t.wait_ge(ld_ffn, (l + 1) * (16 * FFN_LOADS))
                t.wait_ge(S("b_x"), ONE + i0 + BATCH)
                f_norm_t(g0)
                f_back_t(g0)
                with t.Fori(0, GROUPS - 1) as g:
                    f_body(g0 + g, True)
                f_body(g0 + (GROUPS - 1), False)

            t.wait_ge(S("f_x"), ONE + DEPTH * GROUPS)
            for g in range(GROUPS):
                for n in range(GT):
                    m = t.transpose(full(g)[:, n * PARTS:(n + 1) * PARTS],
                                    xT[:, 2 * g + n // TILES, (n % TILES) * PARTS:(n % TILES + 1) * PARTS], ident)
                m.then_inc(S("last_t"), 1)

        @block.scalar
        def _(s):
            for name in ("a_xnT_out a_st_out a_exp a_pT_act a_oT_out a_h0T_out b_hT b_sq b_v b_trT_out b_exp b_pT_act b_o "
                         "f_hT f_yT f_gate").split():
                s.sem_inc(S(name), ONE)
            s.wait_ge(S("w_t"), 1)
            s.activation(wqaT[:, :], full(0)[0:A_QL, 0:PARTS], ACT.Copy).then_inc(S("w_copied"), 1)
            s.activation(wkvaT[:, :], full(0)[0:A_KVL, PARTS:2 * PARTS], ACT.Copy).then_inc(S("w_copied"), 1)
            s.wait_ge(S("w_prod"), 1)
            s.activation(w_a[:, 0:DIM], full(1)[:, 0:DIM], ACT.Copy).then_inc(S("w_ready"), 1)
            s.activation(w_a[:, DIM:A_W].rearrange("p (c x) -> p c x", c=2),
                         full(1)[:, DIM:A_W].rearrange("p (x c) -> p c x", c=2), ACT.Copy).then_inc(S("w_ready"), 1)

            def a_xnT(b):
                s.wait_ge(S("a_xnT"), ONE + b + 1)
                s.wait_ge(S("a_qkv"), ONE + b)
                s.activation(xnT[:, :], misc_a[:, 0:SEQ], ACT.Copy).then_inc(S("a_xnT_out"), 1)

            def a_stack_out(b):
                k = 0
                for n in range(TILES):
                    for h0 in range(0, A_QK, 8):
                        hs = min(8, A_QK - h0)
                        s.wait_ge(S("a_st"), ONE + b * 6 + k + 1)
                        if k == 0:
                            s.wait_ge(S("a_sc"), ONE + b * NUA)
                        src = pt_a[k % 2].bitcast(BF16)[0:A_STACK, 0:hs * PARTS].rearrange("p (h q) -> p h q", h=hs)
                        s.activation(qkT_a[:, h0:h0 + hs, n * PARTS:(n + 1) * PARTS], src, ACT.Copy)\
                            .then_inc(S("a_st_out"), 1)
                        k += 1

            def a_exp(b, u):
                qt, h0, nh = USES_A[u]
                s.wait_ge(S("a_sc"), ONE + b * NUA + u + 1)
                s.wait_ge(S("a_nm"), ONE + b * NUA + u + 1)
                if u == 0:
                    s.wait_ge(S("a_pT"), ONE + b * A_HEADS)
                nk = keys_a(qt)
                for i in range(nh):
                    m = s.activation(p_slice_a(qt, h0 + i), sc_a[u % 2][:, i * nk:(i + 1) * nk], ACT.Exp,
                                     bias=nm_a[:, qt, h0 + i:h0 + i + 1], scale=A_SCALE,
                                     accum_out=sum_a[:, qt, h0 + i:h0 + i + 1])
                m.then_inc(S("a_exp"), 1)

            def a_pT_out(b, h):
                s.wait_ge(S("a_pT"), ONE + b * A_HEADS + h + 1)
                if h >= 4:
                    s.wait_ge(S("a_pv"), ONE + b * A_HEADS + h - 3)
                s.activation(pT_a[:, h % 4, :], pt_a[h % 2][:, 0:PARTS + SEQ], ACT.Copy).then_inc(S("a_pT_act"), 1)

            def a_tail(b):
                s.wait_ge(S("a_oT"), ONE + b + 1)
                s.activation(oT_a[:, :], misc_a[:, 0:SEQ], ACT.Copy).then_inc(S("a_oT_out"), 1)
                s.wait_ge(S("a_h0T"), ONE + b + 1)
                s.activation(xT[:, bass.ds(b, 1), :].rearrange("p o s -> p (o s)"), misc_a[:, 0:SEQ], ACT.Copy)\
                    .then_inc(S("a_h0T_out"), 1)

            def a_body(b, more):
                a_exp(b, 0)
                a_exp(b, 1)
                if more:
                    a_xnT(b + 1)
                a_exp(b, 2)
                a_exp(b, 3)
                a_pT_out(b, 0)
                a_pT_out(b, 2)
                a_exp(b, 4)
                a_pT_out(b, 4)
                a_pT_out(b, 6)
                a_exp(b, 5)
                for h in range(8, A_HEADS, 2):
                    a_pT_out(b, h)
                if more:
                    a_stack_out(b + 1)
                a_tail(b)

            a_xnT(0)
            a_stack_out(0)
            with s.Fori(0, BATCH - 1) as b:
                a_body(b, True)
            a_body(BATCH - 1, False)

            def b_hT(i, b):
                s.wait_ge(S("b_vp"), ONE + 2 * i)
                src = xT[:, bass.ds(b, 1), :].rearrange("p o s -> p (o s)")
                s.activation(hT[0:64, :], src[0:64, :], ACT.Copy).then_inc(S("b_hT"), 1)
                s.activation(hT[64:128, 1:SEQ], src[64:128, 0:SEQ - 1], ACT.Copy).then_inc(S("b_hT"), 1)

            def b_sq(i, n):
                s.wait_ge(S("b_qk"), ONE + 2 * i + n + 1)
                s.wait_ge(S("b_ss"), ONE + 2 * i + n)
                s.activation(sq[:, :, :].rearrange("p c n -> p (c n)"), pj[:, :], ACT.Square).then_inc(S("b_sq"), 1)

            def b_v(i):
                for n in range(TILES):
                    s.wait_ge(S("b_vp"), ONE + 2 * i + n + 1)
                    s.wait_ge(S("b_pv"), ONE + i * PAIRS)
                    s.activation(v_b[:, n, :], pj[:, n * INNER:(n + 1) * INNER], ACT.Copy).then_inc(S("b_v"), 1)

            def b_qkT(i):
                for n in range(TILES):
                    for c in range(2):
                        s.wait_ge(S("b_trT"), ONE + 4 * i + 2 * n + c + 1)
                        s.wait_ge(S("b_sc"), ONE + i * NUB)
                        s.activation(qkT[:, c, :, n * PARTS:(n + 1) * PARTS],
                                     pj[:, c * 512:(c + 1) * 512].rearrange("p (a q) -> p a q", a=PAIRS),
                                     ACT.Copy).then_inc(S("b_trT_out"), 1)

            def b_exp(i, u):
                qt, heads = USES_B[u]
                s.wait_ge(S("b_sc"), ONE + i * NUB + u + 1)
                s.wait_ge(S("b_nm"), ONE + i * NUB + u + 1)
                if u == 0:
                    s.wait_ge(S("b_pT"), ONE + i * HEADS)
                nk = keys_b(qt)
                for n, h in enumerate(heads):
                    m = s.activation(p_slice_b(qt, h), sc_b[u % 3][:, n * nk:(n + 1) * nk], ACT.Exp,
                                     bias=nm_b[:, qt, h:h + 1], scale=scq_b[:, qt, h:h + 1],
                                     accum_out=sum_b[:, qt, h:h + 1])
                m.then_inc(S("b_exp"), 1)

            def b_pT_out(i, h):
                s.wait_ge(S("b_pT"), ONE + i * HEADS + h + 1)
                if h >= 4:
                    s.wait_ge(S("b_pv"), ONE + i * PAIRS + h // 2 - 1)
                s.activation(pT_b[:, h % 4, :], pt_b[h % 2][:, 0:PARTS + SEQ], ACT.Copy).then_inc(S("b_pT_act"), 1)

            def b_o(i, k):
                s.wait_ge(S("b_pv"), ONE + i * PAIRS + 2 * k + 2)
                s.wait_ge(S("b_y"), ONE + i)
                s.activation(oT_b[:, 2 * k:2 * k + 2, :], ov_b[:, :].rearrange("p (a q) -> p a q", a=2), ACT.Copy)\
                    .then_inc(S("b_o"), 1)

            def b_body(i, b, more):
                if more:
                    b_hT(i + 1, b + 1)
                b_exp(i, 0)
                b_exp(i, 1)
                b_exp(i, 2)
                if more:
                    b_sq(i + 1, 0)
                b_exp(i, 3)
                b_exp(i, 4)
                if more:
                    b_sq(i + 1, 1)
                b_exp(i, 5)
                b_pT_out(i, 0)
                b_pT_out(i, 2)
                b_pT_out(i, 4)
                b_o(i, 0)
                b_pT_out(i, 6)
                b_o(i, 1)
                if more:
                    b_v(i + 1)
                    b_qkT(i + 1)

            def f_hT(i, g):
                s.wait_ge(S("f_h"), ONE + i)
                src = xT[:, bass.ds(g * 2, 2), :]
                for n in range(2):
                    s.activation(hTf[0:64, n, :], src[0:64, n, :], ACT.Copy).then_inc(S("f_hT"), 1)
                    s.activation(hTf[64:128, n, 1:SEQ], src[64:128, n, 0:SEQ - 1], ACT.Copy).then_inc(S("f_hT"), 1)

            def f_yT(i):
                s.wait_ge(S("f_ty"), ONE + i + 1)
                s.wait_ge(S("f_up"), ONE + i * (2 * NCH))
                s.activation(yfT[:, :], lnf[1], ACT.Identity, bias=ln_b[:, 0:1], scale=ln_g[:, 0:1])\
                    .then_inc(S("f_yT"), 1)

            def f_gate(i, c):
                h0, n = HCH[c]
                s.wait_ge(S("f_up"), ONE + i * (2 * NCH) + 2 * c + 1)
                s.wait_ge(S("f_act"), ONE + i * NCH)
                s.activation(gate[0:n, c, :], up[0][c % 2][0:n, :], ACT.Gelu, bias=b1[0:n, 1, c:c + 1])\
                    .then_inc(S("f_gate"), 1)

            def f_body(i, g, more):
                if more:
                    f_hT(i + 1, g + 1)
                for c in range(NCH):
                    f_gate(i, c)
                if more:
                    f_yT(i + 1)

            with s.Fori(0, DEPTH) as l:
                i0 = l * BATCH
                s.wait_ge(S("b_zero"), 2)
                s.wait_ge(S("f_x"), ONE + l * GROUPS)
                s.wait_ge(S("a_h0T_out"), ONE + BATCH)
                b_hT(i0, 0)
                b_sq(i0, 0)
                b_sq(i0, 1)
                b_v(i0)
                b_qkT(i0)
                with s.Fori(0, BATCH - 1) as b:
                    b_body(i0 + b, b, True)
                b_body(i0 + (BATCH - 1), BATCH - 1, False)
                g0 = l * GROUPS
                s.wait_ge(ld_ffn, (l + 1) * (16 * FFN_LOADS))
                s.wait_ge(S("b_x"), ONE + i0 + BATCH)
                f_hT(g0, 0)
                f_yT(g0)
                with s.Fori(0, GROUPS - 1) as g:
                    f_body(g0 + g, g, True)
                f_body(g0 + (GROUPS - 1), GROUPS - 1, False)

        @block.vector
        def _(v):
            for name in ("a_ve a_xn a_rope a_nm a_pT_dve a_o a_ve2 a_h0 b_tab b_ss b_n2 b_rot b_r8 b_scq b_mx b_nm b_inv "
                         "b_p b_pT_dve b_x f_st f_mv f_ve f_y f_act f_x").split():
                v.sem_inc(S(name), ONE)
            v.memset(minus_half[:, :], -0.5).then_inc(S("half"), 1)
            v.memset(hT[64:128, 0:1], 0.0).then_inc(S("b_zero"), 1)
            v.memset(p_b1[:, :, 0:WINDOW], 0.0).then_inc(S("b_zero"), 1)
            v.memset(hTf[64:128, :, 0:1], 0.0).then_inc(S("f_zero"), 1)
            v.memset(mask_a1[:, :, 0, :], 0.0)
            v.wait_ge(ld_c, 16)
            v.tensor_copy(ident_h[:, :], ident)
            v.tensor_copy(mask_a0[:, :, :], const[:, C_MA:C_MB0].unsqueeze(1).broadcast_to([PARTS, 4, PARTS]))
            v.tensor_copy(mask_a1[:, :, 1, :], const[:, C_MA:C_MB0].unsqueeze(1).broadcast_to([PARTS, 2, PARTS]))
            v.tensor_copy(mask_b0[:, :, :], const[:, C_MB0:C_MB1].unsqueeze(1).broadcast_to([PARTS, 4, PARTS]))
            v.tensor_copy(mask_b1[:, :, :], const[:, C_MB1:C_RA].unsqueeze(1).broadcast_to([PARTS, 2, B1K]))\
                .then_inc(S("consts_cast"), 1)

            own_p = Own(v, S("dve_ap"), 2)
            own_s = Own(v, S("dve_as"), 7)
            own_t = Own(v, S("dve_at"), 8)

            def bcast_heads(x, n, h, d):
                return x.unsqueeze(2).broadcast_to([PARTS, n, h, d])

            def a_stats(b, x_loaded):
                own_p.begin(b)
                v.wait_ge(x_loaded, 16)
                v.wait_ge(S("a_rs"), ONE + b)
                src = x_all[:, bass.ds(b, 1), :, :].rearrange("p o t d -> p (o t) d")
                for n in range(TILES):
                    m = v.bn_stats(st[:, n, :], src[:, n, :])
                own_p.step(m)
                plain(v)
                for n in range(TILES):
                    m = v.bn_aggr(mv[:, n, :], st[:, n, :])
                own_p.step(m)
                v.tensor_scalar(ve[:, :], mv[:, :, 1], EPS, None, ALU.add).then_inc(S("a_ve"), 1)

            def a_norm(b):
                src = x_all[:, bass.ds(b, 1), :, :].rearrange("p o t d -> p (o t) d")
                v.wait_ge(S("a_rs"), ONE + b + 1)
                v.wait_ge(S("a_xnT"), ONE + b)
                for n in range(TILES):
                    m = v.tensor_scalar(xn[:, n, :], src[:, n, :], mv[:, n, 0:1], rs1[:, n:n + 1],
                                        ALU.subtract, ALU.mult)
                m.then_inc(S("a_xn"), 1)

            def a_rope(b):
                v.wait_ge(S("a_qkv"), ONE + b + 1)
                v.wait_ge(S("a_sum"), ONE + b)
                v.wait_ge(S("a_v"), ONE + b)
                qkv = misc_a[:, 0:TILES * A_W].rearrange("p (t w) -> p t w", t=TILES)
                w = A_QK * A_D
                qk = qkv[:, :, 0:w].rearrange("p t (h d) -> p t h d", d=A_D)
                v.tensor_tensor(rope_c[:, :, :, :], qk, bcast_heads(cos_a, TILES, A_QK, A_D), ALU.mult)
                for k in range(2):
                    v.tensor_tensor(rope_s[:, :, :, k::2], qk[:, :, :, 1 - k::2],
                                    bcast_heads(sin_a[:, :, k::2], TILES, A_QK, A_D // 2), ALU.mult)
                v.tensor_copy(v_new[:, :, :], qkv[:, :, w:A_W]).then_inc(S("a_rope"), 1)

            def a_max(b, u):
                qt, h0, nh = USES_A[u]
                v.wait_ge(S("a_sc"), ONE + b * NUA + u + 1)
                if u == 0:
                    v.wait_ge(S("a_exp"), ONE + b * NUA)
                nk = keys_a(qt)
                own_s.step(v.tensor_reduce(mx_a[:, qt, h0:h0 + nh], sc_a[u % 2][:, :].rearrange("p (h k) -> p h k", k=nk),
                                           AX.X, ALU.max))
                v.tensor_scalar(nm_a[:, qt, h0:h0 + nh], mx_a[:, qt, h0:h0 + nh], -A_SCALE, None, ALU.mult)\
                    .then_inc(S("a_nm"), 1)

            def a_pT_out(b, h):
                v.wait_ge(S("a_pT"), ONE + b * A_HEADS + h + 1)
                if h >= 4:
                    v.wait_ge(S("a_pv"), ONE + b * A_HEADS + h - 3)
                v.tensor_copy(pT_a[:, h % 4, :], pt_a[h % 2][:, 0:PARTS + SEQ]).then_inc(S("a_pT_dve"), 1)

            def a_o(b):
                v.wait_ge(S("a_exp"), ONE + b * NUA + NUA)
                own_s.step(v.reciprocal(inv_a[:, :, :], sum_a[:, :, :]))
                v.wait_ge(S("a_pv"), ONE + b * A_HEADS + A_HEADS)
                v.wait_ge(S("a_oT"), ONE + b)
                m = v.tensor_tensor(o_a[:, :, :].rearrange("p t (h d) -> p t h d", d=A_D),
                                    ov_a[:, 0:TILES * DIM].rearrange("p (t h d) -> p t h d", t=TILES, d=A_D),
                                    inv_a[:, :, :].unsqueeze(3).broadcast_to([PARTS, TILES, A_HEADS, A_D]), ALU.mult)
                m.then_inc(S("a_o"), 1)

            def a_tail(b):
                own_t.begin(b)
                v.wait_ge(S("a_y"), ONE + b + 1)
                own_t.step(v.tensor_tensor(y_a[:, :, :], misc_a[:, 0:TILES * DIM].rearrange("p (t d) -> p t d", t=TILES),
                                           bout[:, :].unsqueeze(1).broadcast_to([PARTS, TILES, DIM]), ALU.add))
                for k in range(2):
                    src = y_a if k == 0 else z_a
                    for n in range(TILES):
                        m = v.bn_stats(st2[:, n, :], src[:, n, :])
                    own_t.step(m)
                    plain(v)
                    for n in range(TILES):
                        m = v.bn_aggr(mv2[:, n, :], st2[:, n, :])
                    own_t.step(m)
                    v.tensor_scalar(ve2[:, :], mv2[:, :, 1], EPS, None, ALU.add).then_inc(S("a_ve2"), 1)
                    v.wait_ge(S("a_rs2"), ONE + 2 * b + k + 1)
                    if k == 0:
                        v.wait_ge(S("a_h0T"), ONE + b)
                        for n in range(TILES):
                            m = v.tensor_scalar(y_a[:, n, :], y_a[:, n, :], mv2[:, n, 0:1], rs2[:, n:n + 1],
                                                ALU.subtract, ALU.mult)
                        own_t.step(m)
                        x1 = x_all[:, bass.ds(b, 1), :, :].rearrange("p o t d -> p (o t) d")
                        own_t.step(v.tensor_tensor(z_a[:, :, :], y_a[:, :, :], x1, ALU.add))
                        own_t.step(v.tensor_tensor(x1, y_a[:, :, :], x1, ALU.add))
                    else:
                        for n in range(TILES):
                            m = v.tensor_scalar(z_a[:, n, :], z_a[:, n, :], mv2[:, n, 0:1], rs2[:, n:n + 1],
                                                ALU.subtract, ALU.mult)
                        m.then_inc(S("a_h0"), 1)
                own_t.end()

            def a_body(b, more):
                own_s.begin(b)
                a_max(b, 0)
                if more:
                    a_stats(b + 1, ld_x)
                a_max(b, 1)
                if more:
                    a_norm(b + 1)
                a_max(b, 2)
                a_max(b, 3)
                if more:
                    a_rope(b + 1)
                a_pT_out(b, 1)
                a_pT_out(b, 3)
                a_max(b, 4)
                a_pT_out(b, 5)
                a_pT_out(b, 7)
                a_max(b, 5)
                for h in range(9, A_HEADS, 2):
                    a_pT_out(b, h)
                a_o(b)
                a_tail(b)

            v.wait_ge(S("half"), 1)
            a_stats(0, ld_x0)
            a_norm(0)
            a_rope(0)
            with v.Fori(0, BATCH - 1) as b:
                a_body(b, True)
            a_body(BATCH - 1, False)

            def l_tables(l):
                v.wait_ge(ld_att, l * 64 + 64)
                v.wait_ge(S("b_rot"), ONE + l * (BATCH * TILES))
                for n in range(TILES):
                    v.tensor_tensor(tab_c[:, n, :, :], rot_raw[:, 0, n, :, :], scales[:, :, :], ALU.mult)
                    for k in range(2):
                        o = slice(k * (HD // 2), (k + 1) * (HD // 2))
                        p = slice((1 - k) * (HD // 2), (2 - k) * (HD // 2))
                        m = v.tensor_tensor(tab_s[:, n, :, o], rot_raw[:, 1, n, :, o], scales[:, :, p], ALU.mult)
                m.then_inc(S("b_tab"), 1)
                v.wait_ge(S("b_tab"), ONE + l + 1)

            def b_norms(i, n):
                v.wait_ge(S("b_sq"), ONE + 2 * i + n + 1)
                v.wait_ge(S("b_r"), ONE + 2 * i)
                v.tensor_reduce(ss[:, n, :], sq[:, :, :].rearrange("p c (h d) -> p (c h) d", d=HD), AX.X, ALU.add)\
                    .then_inc(S("b_ss"), 1)
                v.wait_ge(S("b_ss"), ONE + 2 * i + n + 1)
                v.tensor_scalar(ss[:, n, :], ss[:, n, :], TINY, None, ALU.max).then_inc(S("b_n2"), 1)

            def b_rot(i, n):
                v.wait_ge(S("b_trT"), ONE + 4 * i)
                v.wait_ge(S("b_qkr"), ONE + 2 * i)
                src = pj[:, :].rearrange("p (c h d) -> p c h d", c=2, d=HD)
                v.tensor_tensor(rc[:, n, :, :].rearrange("p c (h d) -> p c h d", d=HD), src,
                                tab_c[:, n, :, :].unsqueeze(2).broadcast_to([PARTS, 2, HEADS, HD]), ALU.mult)
                dst = rs[:, n, :, :].rearrange("p c (h d) -> p c h d", d=HD)
                for k in range(2):
                    o = slice(k * (HD // 2), (k + 1) * (HD // 2))
                    p = slice((1 - k) * (HD // 2), (2 - k) * (HD // 2))
                    m = v.tensor_tensor(dst[:, :, :, o], src[:, :, :, p],
                                        tab_s[:, n, :, o].unsqueeze(2).broadcast_to([PARTS, 2, HEADS, HD // 2]), ALU.mult)
                m.then_inc(S("b_rot"), 1)

            def b_r8(i):
                v.wait_ge(S("b_r"), ONE + 2 * i + 2)
                v.tensor_scalar(r_q8[:, :, :], r_qk[:, :, 0:HEADS], QK_SCALE, None, ALU.mult).then_inc(S("b_r8"), 1)

            def b_scq(i):
                v.wait_ge(S("b_r8"), ONE + i + 1)
                v.wait_ge(S("b_exp"), ONE + i * NUB)
                v.tensor_copy(scq_b[:, :, :], r_q8[:, :, :]).then_inc(S("b_scq"), 1)
                v.wait_ge(S("b_scq"), ONE + i + 1)

            def b_max(i, u):
                qt, heads = USES_B[u]
                nk = keys_b(qt)
                v.wait_ge(S("b_sc"), ONE + i * NUB + u + 1)
                hs = slice(heads[0], heads[-1] + 1, 2)
                v.tensor_reduce(mx_b[:, qt, hs], sc_b[u % 3][:, 0:len(heads) * nk].rearrange("p (h k) -> p h k", k=nk),
                                AX.X, ALU.max).then_inc(S("b_mx"), 1)
                v.wait_ge(S("b_mx"), ONE + i * NUB + u + 1)
                v.scalar_tensor_tensor(out=nm_b[:, qt, hs], in0=mx_b[:, qt, hs], scalar=-1.0, in1=scq_b[:, qt, hs],
                                       op0=ALU.mult, op1=ALU.mult).then_inc(S("b_nm"), 1)

            def b_probs(i, heads, k):
                v.wait_ge(S("b_exp"), ONE + i * NUB + (4 if k == 0 else 6))
                h0 = heads[0]
                v.reciprocal(inv_b[:, :, h0:h0 + 4], sum_b[:, :, h0:h0 + 4]).then_inc(S("b_inv"), 1)
                v.wait_ge(S("b_inv"), ONE + 2 * i + k + 1)
                for h in heads:
                    v.tensor_scalar(p_slice_b(0, h), p_slice_b(0, h), inv_b[:, 0, h:h + 1], None, ALU.mult)
                    v.tensor_scalar(p_slice_b(1, h), p_slice_b(1, h), inv_b[:, 1, h:h + 1], None, ALU.mult)\
                        .then_inc(S("b_p"), 1)

            def b_pT_out(i, h):
                v.wait_ge(S("b_pT"), ONE + i * HEADS + h + 1)
                if h >= 4:
                    v.wait_ge(S("b_pv"), ONE + i * PAIRS + h // 2 - 1)
                v.tensor_copy(pT_b[:, h % 4, :], pt_b[h % 2][:, 0:PARTS + SEQ]).then_inc(S("b_pT_dve"), 1)

            def b_x(i, b):
                v.wait_ge(S("b_y"), ONE + i + 1)
                x = xT[:, bass.ds(b, 1), :].rearrange("p o s -> p (o s)")
                v.tensor_tensor(x, ov_b[:, 0:SEQ], x, ALU.add).then_inc(S("b_x"), 1)

            def b_body(i, b, more):
                b_scq(i)
                b_max(i, 0)
                b_max(i, 1)
                b_max(i, 2)
                b_max(i, 3)
                if more:
                    b_norms(i + 1, 0)
                    b_rot(i + 1, 0)
                b_max(i, 4)
                b_max(i, 5)
                b_probs(i, (0, 1, 2, 3), 0)
                if more:
                    b_norms(i + 1, 1)
                    b_rot(i + 1, 1)
                b_pT_out(i, 1)
                b_probs(i, (4, 5, 6, 7), 1)
                b_pT_out(i, 3)
                b_pT_out(i, 5)
                b_pT_out(i, 7)
                if more:
                    b_r8(i + 1)
                b_x(i, b)

            def f_stats(i):
                v.wait_ge(S("f_h"), ONE + i + 1)
                for n in range(GT):
                    m = v.bn_stats(stf[:, n, :], lnf[0][:, n * PARTS:(n + 1) * PARTS])
                m.then_inc(S("f_st"), 1)
                v.wait_ge(S("f_st"), ONE + i + 1)
                plain(v)
                for n in range(GT):
                    m = v.bn_aggr(mvf[:, n, :], stf[:, n, :])
                m.then_inc(S("f_mv"), 1)
                v.wait_ge(S("f_mv"), ONE + i + 1)
                v.tensor_scalar(vef[:, :], mvf[:, :, 1], EPS, None, ALU.add).then_inc(S("f_ve"), 1)

            def f_norm(i):
                v.wait_ge(S("f_rs"), ONE + i + 1)
                v.wait_ge(S("f_ty"), ONE + i)
                for n in range(GT):
                    m = v.tensor_scalar(yf[:, n, :], lnf[0][:, n * PARTS:(n + 1) * PARTS], mvf[:, n, 0:1],
                                        rsf[:, n:n + 1], ALU.subtract, ALU.mult)
                m.then_inc(S("f_y"), 1)

            def f_act(i, c):
                h0, n = HCH[c]
                v.wait_ge(S("f_up"), ONE + i * (2 * NCH) + 2 * c + 2)
                v.wait_ge(S("f_gate"), ONE + i * NCH + c + 1)
                v.wait_ge(S("f_down"), ONE + i)
                v.scalar_tensor_tensor(out=act[0:n, c, :], in0=up[1][c % 2][0:n, :], scalar=b1[0:n, 0, c:c + 1],
                                       in1=gate[0:n, c, :], op0=ALU.add, op1=ALU.mult).then_inc(S("f_act"), 1)

            def f_x(i, g):
                v.wait_ge(S("f_down"), ONE + i + 1)
                x = xT[:, bass.ds(g * 2, 2), :].rearrange("p o s -> p (o s)")
                v.scalar_tensor_tensor(out=x, in0=down[:, :], scalar=b2[:, 0:1], in1=x, op0=ALU.add, op1=ALU.add)\
                    .then_inc(S("f_x"), 1)

            def f_body(i, g, more):
                f_act(i, 0)
                f_act(i, 1)
                if more:
                    f_stats(i + 1)
                f_act(i, 2)
                if more:
                    f_norm(i + 1)
                f_x(i, g)

            with v.Fori(0, DEPTH) as l:
                i0 = l * BATCH
                l_tables(l)
                for n in range(TILES):
                    b_norms(i0, n)
                    b_rot(i0, n)
                b_r8(i0)
                with v.Fori(0, BATCH - 1) as b:
                    b_body(i0 + b, b, True)
                b_body(i0 + (BATCH - 1), BATCH - 1, False)
                g0 = l * GROUPS
                v.wait_ge(ld_ffn, (l + 1) * (16 * FFN_LOADS))
                f_stats(g0)
                f_norm(g0)
                with v.Fori(0, GROUPS - 1) as g:
                    f_body(g0 + g, g, True)
                f_body(g0 + (GROUPS - 1), GROUPS - 1, False)

            for g in range(GROUPS):
                v.wait_ge(S("last_t"), g + 1)
                for n in range(GT):
                    m = v.bn_stats(stl[:, g, n, :], full(g)[:, n * PARTS:(n + 1) * PARTS])
            m.then_inc(S("last_st"), 1)
            v.wait_ge(S("last_st"), 1)
            for g in range(GROUPS):
                for n in range(GT):
                    m = v.bn_aggr(mvl[:, g, n, :], stl[:, g, n, :])
            m.then_inc(S("last_mv"), 1)
            v.wait_ge(S("last_mv"), 1)
            v.tensor_scalar(vel[:, :], mvl[:, :, :, 1].rearrange("p g t -> p (g t)"), EPS, None, ALU.add)\
                .then_inc(S("last_ve"), 1)
            v.wait_ge(S("last_rs"), 1)
            for g in range(GROUPS):
                for n in range(GT):
                    m = v.tensor_scalar(xl[:, g, n, :], full(g)[:, n * PARTS:(n + 1) * PARTS], mvl[:, g, n, 0:1],
                                        rsl[:, g * GT + n:g * GT + n + 1], ALU.subtract, ALU.mult)
                m.then_inc(S("last_n"), 1)
                v.wait_ge(S("last_n"), g + 1)
                v.tensor_tensor(xl[:, g, :, :], xl[:, g, :, :],
                                x_all[:, 2 * g:2 * g + 2, :, :].rearrange("p b t d -> p (b t) d"), ALU.add)\
                    .then_inc(S("last_done"), 1)

        @block.gpsimd
        def _(g):
            for name in ("a_rs a_sum a_stack a_v a_rs2 b_r b_add b_qkr f_rs").split():
                g.sem_inc(S(name), ONE)
            g.wait_ge(S("half"), 1)

            def a_rs(b):
                g.wait_ge(S("a_ve"), ONE + b + 1)
                g.tensor_tensor(rs1[:, :], ve[:, :], minus_half[:, 0:TILES], ALU.pow).then_inc(S("a_rs"), 1)

            def a_split(b):
                own.begin(b)
                g.wait_ge(S("a_rope"), ONE + b + 1)
                g.wait_ge(S("a_st"), ONE + b * 6)
                g.tensor_tensor(rest[:, :, :, :], rope_c[:, :, :, :], rope_s[:, :, :, :], ALU.add)\
                    .then_inc(S("a_sum"), 1)
                g.wait_ge(S("a_sum"), ONE + b + 1)
                plain(g)
                for i in range(SPLIT):
                    for n in range(TILES):
                        for h0, h1, dst in ((0, A_HEADS, stack[:, n, 0:A_HEADS, i, :, :]),
                                            (A_HEADS, A_QK, stack[:, n, A_HEADS:A_QK, :, i, :])):
                            m = g.tensor_copy(dst, rest[:, n, h0:h1, :].unsqueeze(2)
                                              .broadcast_to([PARTS, h1 - h0, SPLIT, A_D]))
                    if i == SPLIT - 1:
                        m.then_inc(S("a_stack"), 1)
                        break
                    own.step(m)
                    g.tensor_tensor(rest[:, :, 0:A_HEADS, :], rest[:, :, 0:A_HEADS, :],
                                    stack[:, :, 0:A_HEADS, i, 0, :], ALU.subtract)
                    own.step(g.tensor_tensor(rest[:, :, A_HEADS:A_QK, :], rest[:, :, A_HEADS:A_QK, :],
                                             stack[:, :, A_HEADS:A_QK, 0, i, :], ALU.subtract))
                    plain(g)
                own.end()

            def a_v(b):
                g.wait_ge(S("a_rope"), ONE + b + 1)
                g.wait_ge(S("a_pv"), ONE + b * A_HEADS)
                plain(g)
                g.tensor_copy(v_a[:, :, :], v_new[:, :, :]).then_inc(S("a_v"), 1)

            def a_rs2(b):
                for k in range(2):
                    g.wait_ge(S("a_ve2"), ONE + 2 * b + k + 1)
                    g.tensor_tensor(rs2[:, :], ve2[:, :], minus_half[:, 0:TILES], ALU.pow).then_inc(S("a_rs2"), 1)

            own = Own(g, S("pool_a"), 2 * (SPLIT - 1))
            a_rs(0)
            a_split(0)
            a_v(0)
            with g.Fori(0, BATCH - 1) as b:
                a_rs(b + 1)
                a_split(b + 1)
                a_v(b + 1)
                a_rs2(b)
            a_rs2(BATCH - 1)

            def b_norm(i, n):
                g.wait_ge(S("b_n2"), ONE + 2 * i + n + 1)
                g.wait_ge(S("b_r8"), ONE + i)
                g.tensor_tensor(r_qk[:, n, :], ss[:, n, :], minus_half[:, :], ALU.pow).then_inc(S("b_r"), 1)
                g.wait_ge(S("b_rot"), ONE + 2 * i + n + 1)
                g.tensor_tensor(rc[:, n, :, :], rc[:, n, :, :], rs[:, n, :, :], ALU.add).then_inc(S("b_add"), 1)
                g.wait_ge(S("b_add"), ONE + 2 * i + n + 1)
                k = rc[:, n, 1, :].rearrange("p (h d) -> p h d", d=HD)
                g.tensor_tensor(k, k, r_qk[:, n, HEADS:2 * HEADS].unsqueeze(2).broadcast_to([PARTS, HEADS, HD]),
                                ALU.mult).then_inc(S("b_qkr"), 1)

            with g.Fori(0, DEPTH) as l:
                with g.Fori(0, BATCH) as b:
                    for n in range(TILES):
                        b_norm(l * BATCH + b, n)
                with g.Fori(0, GROUPS) as q:
                    i = l * GROUPS + q
                    g.wait_ge(S("f_ve"), ONE + i + 1)
                    g.tensor_tensor(rsf[:, :], vef[:, :], minus_half[:, 0:GT], ALU.pow).then_inc(S("f_rs"), 1)

            g.wait_ge(S("last_ve"), 1)
            g.tensor_tensor(rsl[:, :], vel[:, :], minus_half[:, :], ALU.pow).then_inc(S("last_rs"), 1)


_INS = ["L0_attn_x", "L0_attn_Wqa", "L0_attn_Wqb", "L0_attn_Wkva", "L0_attn_Wkvb", "L0_attn_Wout", "L0_attn_bout",
        "L0_ffn_wqkv", "L0_ffn_q_scale", "L0_ffn_k_scale", "L0_ffn_wo", "L0_ffn_ln_g", "L0_ffn_ln_b", "L0_ffn_w1",
        "L0_ffn_b1", "L0_ffn_w2", "L0_ffn_b2"]


def kernel(**inputs):
    import numpy as _np
    import concourse.bacc as _bacc
    from concourse import mybir as _mybir
    from concourse.bass_utils import run_bass_kernel_spmd as _run

    nc = _bacc.Bacc("TRN2", target_bir_lowering=False, num_devices=1)
    arrays, args = {}, {}
    for name in _INS:
        x = _np.ascontiguousarray(inputs[name])
        arrays[f"in_{name}_dram"] = x
        args[name] = nc.dram_tensor(f"in_{name}_dram", x.shape, _mybir.dt.from_np(x.dtype), kind="ExternalInput").ap()
    arrays["consts_dram"] = shape_constants()
    args["consts"] = nc.dram_tensor("consts_dram", arrays["consts_dram"].shape, _mybir.dt.float32,
                                    kind="ExternalInput").ap()
    out = nc.dram_tensor("out_dram", (BATCH, SEQ, DIM), _mybir.dt.float32, kind="ExternalOutput").ap()
    build_program(nc, args, out)
    r = _run(nc, [arrays], core_ids=[0])
    return r.results[0]["out_dram"]
```

```python
import numpy as np
import concourse.bass as bass
from concourse import mybir
from contextlib import ExitStack

FP32 = mybir.dt.float32
BF16 = mybir.dt.bfloat16
ALU = mybir.AluOpType
ACT = mybir.ActivationFunctionType
AX = mybir.AxisListType

PARTS = 128
BATCH, SEQ, DIM = 8, 256, 128
TILES = SEQ // PARTS

A_HEADS, A_KV = 16, 4
A_D = DIM // A_HEADS
A_GROUP = A_HEADS // A_KV
A_QL, A_KVL = 64, 32
A_QK = A_HEADS + A_KV
A_SCALE = A_D ** -0.5
SPLIT = 3
A_STACK = SPLIT * SPLIT * A_D
A_COLS = PARTS // A_GROUP

DEPTH, HEADS, HD = 2, 8, 64
WINDOW = 64
INNER = HEADS * HD
PAIRS = HEADS // 2
QK_SCALE = 8.0
HID = int(DIM * 4 * 2 / 3)
HCH = [(c, min(PARTS, HID - c)) for c in range(0, HID, PARTS)]
NCH = len(HCH)
GROUPS = BATCH // 2
GT = 2 * TILES
EPS = 1e-5
TINY = 1e-24
NEG = -1e30

C_ID = 0
C_MA = C_ID + PARTS
C_MB0 = C_MA + PARTS
C_MB1 = C_MB0 + PARTS
B1K = SEQ - WINDOW
C_RA = C_MB1 + B1K
C_RB = C_RA + 2 * TILES * A_D
C_END = C_RB + 2 * TILES * 2 * HD


def shape_constants():
    f = np.float32
    c = np.zeros((PARTS, C_END), f)
    q = np.arange(PARTS)[:, None]
    k = np.arange(PARTS)[None, :]
    c[:, C_ID:C_MA] = np.eye(PARTS)
    c[:, C_MA:C_MB0] = np.where(k > q, NEG, 0)
    c[:, C_MB0:C_MB1] = np.where((k > q) | (q > k + WINDOW), NEG, 0)
    q1, k1 = q + PARTS, np.arange(B1K)[None, :] + WINDOW
    c[:, C_MB1:C_RA] = np.where((k1 > q1) | (q1 > k1 + WINDOW), NEG, 0)
    t = np.arange(SEQ, dtype=f)

    inv = f(1.0) / f(10000.0) ** (np.arange(0, A_D, 2, dtype=f) / f(A_D))
    ang = np.outer(t, inv).astype(f)
    cos, sin = np.repeat(np.cos(ang), 2, 1), np.repeat(np.sin(ang), 2, 1)
    sin[:, 0::2] *= -1
    for n, tab in enumerate((cos, sin)):
        w = TILES * A_D
        c[:, C_RA + n * w:C_RA + (n + 1) * w] = tab.reshape(TILES, PARTS, A_D).transpose(1, 0, 2).reshape(PARTS, w)

    half = np.arange(0, HD, 2, dtype=f)
    inv = f(1.0) / f(10000.0) ** (half / f(HD))
    ang = t[:, None] * inv[None, :]
    cos, sin = np.cos(ang), np.sin(ang)
    base = (half + f(0.4 * HD)) / f(1.4 * HD)
    scale = base[None, :] ** ((t - f(SEQ // 2)) / f(WINDOW // 2))[:, None]
    for n, (lo, hi) in enumerate(((cos, cos), (-sin, sin))):
        tab = np.concatenate([lo, hi], 1)
        both = np.stack([tab * np.tile(scale, 2), tab / np.tile(scale, 2)], 1).astype(f)
        w = TILES * 2 * HD
        c[:, C_RB + n * w:C_RB + (n + 1) * w] = both.reshape(TILES, PARTS, 2, HD).transpose(1, 0, 2, 3).reshape(PARTS, w)
    return c


ONE = 1


class Own:

    def __init__(self, eng, sem, per):
        self.eng, self.sem, self.per, self.n, self.base = eng, sem, per, 0, 0

    def begin(self, index):
        self.base, self.n = index * self.per, 0

    def end(self):
        assert self.n == self.per, (self.sem.name, self.n, self.per)

    def step(self, ins):
        self.n += 1
        ins.then_inc(self.sem, 1)
        self.eng.wait_ge(self.sem, self.base + self.n)


def build_program(nc, a, out):
    ctx = ExitStack()
    with ctx:
        def sb(name, shape, dt=FP32):
            return ctx.enter_context(nc.sbuf_tensor(name, shape, dt))

        def pb(name, shape, dt=FP32):
            return ctx.enter_context(nc.psum_tensor(name, shape, dt))

        def sem(name):
            return ctx.enter_context(nc.semaphore(name))

        const = sb("const", [PARTS, C_END])
        ident = const[:, C_ID:C_MA]
        cos_a = const[:, C_RA:C_RA + TILES * A_D].rearrange("p (t d) -> p t d", t=TILES)
        sin_a = const[:, C_RA + TILES * A_D:C_RB].rearrange("p (t d) -> p t d", t=TILES)
        rot_raw = const[:, C_RB:C_END].rearrange("p (n t c d) -> p n t c d", n=2, t=TILES, c=2)
        ident_h = sb("ident_h", [PARTS, PARTS], BF16)
        ident_4 = sb("ident_4", [PARTS, 4, PARTS], BF16)
        mask_a = sb("mask_a", [PARTS, 4, PARTS], BF16)
        mask_b0 = sb("mask_b0", [PARTS, 4, PARTS], BF16)
        mask_b1 = sb("mask_b1", [PARTS, 2, B1K], BF16)
        minus_half = sb("minus_half", [PARTS, 16])

        x_all = sb("x_all", [PARTS, BATCH, TILES, DIM])
        xT = sb("xT", [PARTS, BATCH, SEQ])

        wqa = sb("wqa", [PARTS, A_QL])
        wkva = sb("wkva", [PARTS, A_KVL])
        wqb = sb("wqb", [A_QL, DIM])
        wkvb = sb("wkvb", [A_KVL, 2 * A_KV * A_D])
        wqaT = sb("wqaT", [A_QL, PARTS])
        wkvaT = sb("wkvaT", [A_KVL, PARTS])
        A_W = DIM + 2 * A_KV * A_D
        w_a = sb("w_a", [PARTS, A_W])
        wout = sb("wout", [PARTS, DIM])
        bout = sb("bout", [PARTS, DIM])

        st = sb("st", [PARTS, BATCH, TILES, 6])
        mv = sb("mv", [PARTS, BATCH, TILES, 2])
        ve = sb("ve", [PARTS, BATCH, TILES])
        rs1 = sb("rs1", [PARTS, BATCH, TILES])
        xn = sb("xn", [PARTS, TILES, DIM])
        xnT = sb("xnT", [PARTS, SEQ])
        rope_c = sb("rope_c", [PARTS, TILES, A_QK, A_D])
        rope_s = sb("rope_s", [PARTS, TILES, A_QK, A_D])
        v_new = sb("v_new", [PARTS, TILES, A_KV * A_D])
        v_a = [sb(f"v_a{i}", [PARTS, TILES, A_KV, A_COLS]) for i in range(2)]
        rest = sb("rest", [PARTS, TILES, A_QK, A_D])
        stack = sb("stack", [PARTS, TILES, A_QK, SPLIT, SPLIT, A_D], BF16)
        qkT_a = [sb(f"qkT_a{i}", [A_STACK + SPLIT, A_QK, SEQ], BF16) for i in range(2)]
        mx_a = sb("mx_a", [PARTS, TILES, A_HEADS])
        m_left = sb("m_left", [PARTS, TILES, A_HEADS])
        m_part = sb("m_part", [PARTS, TILES, SPLIT, A_HEADS], BF16)
        mT = sb("mT", [SPLIT * A_HEADS, SEQ], BF16)
        pT_k0 = sb("pT_k0", [PARTS, A_HEADS, SEQ])
        pT_k1 = sb("pT_k1", [PARTS, A_HEADS, PARTS])
        ovT = sb("ovT", [PARTS, A_KV, SEQ])
        inv_a = sb("inv_a", [PARTS, TILES, A_HEADS])
        o_a = sb("o_a", [PARTS, TILES, DIM])
        oT_a = sb("oT_a", [PARTS, SEQ])
        y_a = sb("y_a", [PARTS, TILES, DIM])
        z_a = sb("z_a", [PARTS, TILES, DIM])
        st2 = sb("st2", [PARTS, TILES, 6])
        mv2 = sb("mv2", [PARTS, TILES, 2])
        ve2 = sb("ve2", [PARTS, TILES])
        rs2 = sb("rs2", [PARTS, TILES])

        wqkv = sb("wqkv", [PARTS, 3 * INNER])
        wo = sb("wo", [PARTS, PAIRS, DIM])
        scales = sb("scales", [PARTS, 2, HD])
        tab_c = sb("tab_c", [PARTS, TILES, 2, HD])
        tab_s = sb("tab_s", [PARTS, TILES, 2, HD])
        hT = sb("hT", [PARTS, SEQ])
        sq = sb("sq", [PARTS, 2, INNER])
        ss = sb("ss", [PARTS, TILES, 2 * HEADS])
        r_qk = sb("r_qk", [PARTS, TILES, 2 * HEADS])
        r_q8 = [sb(f"r_q8{i}", [PARTS, TILES, HEADS]) for i in range(2)]
        rc = sb("rc", [PARTS, TILES, 2, INNER])
        rs = sb("rs", [PARTS, TILES, 2, INNER])
        qkT = [sb(f"qkT{i}", [PARTS, 2, PAIRS, SEQ]) for i in range(2)]
        v_b = [sb(f"v_b{i}", [PARTS, TILES, INNER]) for i in range(2)]
        p_b0 = [sb(f"p_b0{i}", [PARTS, HEADS, PARTS]) for i in range(2)]
        p_b1 = [sb(f"p_b1{i}", [PARTS, HEADS, SEQ]) for i in range(2)]
        mx_b = [sb(f"mx_b{i}", [PARTS, TILES, HEADS]) for i in range(2)]
        nm_b = [sb(f"nm_b{i}", [PARTS, TILES, HEADS]) for i in range(2)]
        sum_b = [sb(f"sum_b{i}", [PARTS, TILES, HEADS]) for i in range(2)]
        inv_b = [sb(f"inv_b{i}", [PARTS, TILES, HEADS]) for i in range(2)]
        pT_b = sb("pT_b", [PARTS, 4, PARTS + SEQ])
        oT_b = sb("oT_b", [PARTS, PAIRS, SEQ])

        w1 = sb("w1", [PARTS, 2 * HID])
        w2 = sb("w2", [PARTS, NCH, DIM])
        b1 = sb("b1", [PARTS, 2, NCH])
        b2 = sb("b2", [PARTS, 1])
        ln_g = sb("ln_g", [PARTS, 1])
        ln_b = sb("ln_b", [PARTS, 1])
        hTf = sb("hTf", [PARTS, 2, SEQ])
        stf = sb("stf", [PARTS, GT, 6])
        mvf = sb("mvf", [PARTS, GT, 2])
        vef = sb("vef", [PARTS, GT])
        rsf = sb("rsf", [PARTS, GT])
        yf = sb("yf", [PARTS, GT, DIM])
        yfT = sb("yfT", [PARTS, GT * PARTS])
        n_heads = NCH * GT * PARTS // SEQ
        gate, act = (pT_k0[:, k * n_heads:(k + 1) * n_heads, :].rearrange("p h q -> p (h q)")
                     .rearrange("p (c n) -> p c n", c=NCH) for k in range(2))
        stl = sb("stl", [PARTS, GROUPS, GT, 6])
        mvl = sb("mvl", [PARTS, GROUPS, GT, 2])
        vel = sb("vel", [PARTS, GROUPS * GT])
        rsl = sb("rsl", [PARTS, GROUPS * GT])
        xl = p_b1[0][:, :, :].rearrange("p h s -> p (h s)").rearrange("p (g t d) -> p g t d", g=GROUPS, t=GT)

        bank = [pb(f"bank{i}", [PARTS, 1024]) for i in range(4)]

        ld_c, ld_x0, ld_x, ld_w = sem("ld_c"), sem("ld_x0"), sem("ld_x"), sem("ld_w")
        ld_att, ld_ffn, ld_m = sem("ld_att"), sem("ld_ffn"), sem("ld_m")
        st_out = sem("st_out")
        names = {}

        def S(name):
            if name not in names:
                names[name] = sem(name)
            return names[name]

        block = ctx.enter_context(nc.Block())

        def plain(eng):
            eng.sem_inc(S("plain"), 1)

        def full(i):
            return bank[i // 2][:, (i % 2) * 512:(i % 2) * 512 + 512]

        USES_Q = [(0, h, 4) for h in range(0, A_HEADS, 4)] + [(1, h, 2) for h in range(0, A_HEADS, 2)]
        NQ = len(USES_Q)
        USES_K = [u for h in range(0, A_HEADS, A_GROUP) for u in ((0, h, 2), (0, h + 2, 2), (1, h, 4))]
        NK = len(USES_K)
        STACKS = [(n, h0, min(8, A_QK - h0)) for n in range(TILES) for h0 in range(0, A_QK, 8)]
        NS = len(STACKS)
        M_LOADS = 16 * SPLIT

        USES_B = [(0, (0, 2, 4, 6)), (0, (1, 3, 5, 7)), (1, (0, 2)), (1, (1, 3)), (1, (4, 6)), (1, (5, 7))]
        NUB = len(USES_B)
        sc_b = [full(2), full(3), full(4)]
        pj = bank[0]
        pt_b = [full(5), full(6)]
        ov_b = full(7)

        def keys_b(qt):
            return PARTS if qt == 0 else B1K

        def p_slice_b(par, qt, h):
            return p_b0[par][:, h, :] if qt == 0 else p_b1[par][:, h, WINDOW:SEQ]

        def done(x, per, first):
            return per * x if first else per * (x - 1)

        lnf = [full(0), full(1)]
        up = [[full(2), full(3)], [full(4), full(5)]]
        down = full(6)

        @block.sync
        def _(e):
            e.dma_start(const[:, :], a["consts"]).then_inc(ld_c, 16)
            e.dma_start(x_all[:, 0, :, :], a["L0_attn_x"][0].rearrange("(t p) d -> p t d", p=PARTS)).then_inc(ld_x0, 16)
            e.dma_start(wqa[:, :], a["L0_attn_Wqa"]).then_inc(ld_w, 16)
            e.dma_start(wkva[:, :], a["L0_attn_Wkva"]).then_inc(ld_w, 16)
            e.dma_start(wqb[:, :], a["L0_attn_Wqb"]).then_inc(ld_w, 16)
            e.dma_start(wkvb[:, :], a["L0_attn_Wkvb"]).then_inc(ld_w, 16)
            e.dma_start(wout[:, :], a["L0_attn_Wout"]).then_inc(ld_w, 16)
            e.dma_start(bout[:, :], a["L0_attn_bout"].unsqueeze(0).broadcast_to([PARTS, DIM])).then_inc(ld_w, 16)
            e.dma_start(x_all[:, 1:BATCH, :, :],
                        a["L0_attn_x"][1:BATCH].rearrange("b (t p) d -> p b t d", p=PARTS)).then_inc(ld_x, 16)
            def load_layer(l, first=False):
                one = bass.ds(l, 1)
                if not first:
                    e.wait_ge(S("b_y"), ONE + l * BATCH)
                    plain(e)
                e.dma_start(wqkv[:, :], a["L0_ffn_wqkv"][one, :, :].rearrange("o p n -> p (o n)")).then_inc(ld_att, 16)
                e.dma_start(wo[:, :, :], a["L0_ffn_wo"][one, :, :].rearrange("o (c p) n -> p (o c) n", p=PARTS)).then_inc(ld_att, 16)
                e.dma_start(scales[:, 0, :], a["L0_ffn_q_scale"][one, :].broadcast_to([PARTS, HD])).then_inc(ld_att, 16)
                e.dma_start(scales[:, 1, :], a["L0_ffn_k_scale"][one, :].broadcast_to([PARTS, HD])).then_inc(ld_att, 16)
                if not first:
                    e.wait_ge(S("f_x"), ONE + l * GROUPS)
                    plain(e)
                e.dma_start(w1[:, :], a["L0_ffn_w1"][one, :, :].rearrange("o p n -> p (o n)")).then_inc(ld_ffn, 16)
                w2l = a["L0_ffn_w2"][one, :, :]
                b1l = a["L0_ffn_b1"][one, :]
                for c, (h0, n) in enumerate(HCH):
                    e.dma_start(w2[0:n, c, :], w2l[:, h0:h0 + n, :].rearrange("o p n -> (o p) n")).then_inc(ld_ffn, 16)
                    for half in range(2):
                        col = half * HID + h0
                        e.dma_start(b1[0:n, half, c:c + 1], b1l[:, col:col + n].rearrange("o p -> p o")).then_inc(ld_ffn, 16)
                e.dma_start(b2[:, :], a["L0_ffn_b2"][one, :].rearrange("o p -> p o")).then_inc(ld_ffn, 16)
                e.dma_start(ln_g[:, :], a["L0_ffn_ln_g"][one, :].rearrange("o p -> p o")).then_inc(ld_ffn, 16)
                e.dma_start(ln_b[:, :], a["L0_ffn_ln_b"][one, :].rearrange("o p -> p o")).then_inc(ld_ffn, 16)

            load_layer(0, first=True)
            with e.Fori(0, BATCH // 2) as j:
                for par in range(2):
                    e.wait_ge(S("a_mT_out"), ONE + 2 * j + par + 1)
                    plain(e)
                    for i in range(SPLIT):
                        e.dma_start(qkT_a[par][A_STACK + i:A_STACK + i + 1, 0:A_HEADS, :],
                                    mT[i * A_HEADS:(i + 1) * A_HEADS, :]).then_inc(ld_m, 16)
            with e.Fori(1, DEPTH) as l:
                load_layer(l)
            with e.Fori(0, GROUPS) as g:
                e.wait_ge(S("last_done"), g + 1)
                e.dma_start(out[bass.ds(g * 2, 2), :, :].rearrange("b (t p) d -> p (b t) d", p=PARTS),
                            xl[:, bass.ds(g, 1), :, :].rearrange("p o t d -> p (o t) d")).then_inc(st_out, 16)
            e.wait_ge(st_out, 16 * GROUPS)

        FFN_LOADS = 1 + 3 * NCH + 3

        @block.tensor
        def _(t):
            for name in ("a_xnT a_qkv a_st a_sc a_mT a_p2 a_pv a_back a_oT a_y a_h0T b_qk b_vp b_trT b_sc b_pT b_pv b_y f_h f_ty f_up "
                         "f_down").split():
                t.sem_inc(S(name), ONE)
            t.wait_ge(ld_c, 16)
            t.wait_ge(ld_w, 16 * 6)
            t.transpose(full(0)[0:A_QL, 0:PARTS], wqa[:, :], ident)
            t.transpose(full(0)[0:A_KVL, PARTS:2 * PARTS], wkva[:, :], ident).then_inc(S("w_t"), 1)
            t.wait_ge(S("w_copied"), 2)
            t.matmul(full(1)[:, 0:DIM], wqaT[:, :], wqb[:, :], start=True, stop=True)
            t.matmul(full(1)[:, DIM:A_W], wkvaT[:, :], wkvb[:, :], start=True, stop=True).then_inc(S("w_prod"), 1)
            t.wait_ge(S("consts_cast"), 1)

            def a_norm_t(b):
                t.wait_ge(S("a_xn"), ONE + b + 1)
                t.wait_ge(S("a_st_out"), ONE + b * NS)
                for n in range(TILES):
                    m = t.transpose(full(7)[:, n * PARTS:(n + 1) * PARTS], xn[:, n, :], ident)
                m.then_inc(S("a_xnT"), 1)

            def a_proj(b):
                t.wait_ge(S("a_xnT_out"), ONE + b + 1)
                for n in range(TILES):
                    m = t.matmul(full(7)[:, n * A_W:(n + 1) * A_W], xnT[:, n * PARTS:(n + 1) * PARTS], w_a[:, :],
                                 start=True, stop=True)
                m.then_inc(S("a_qkv"), 1)

            def a_stack_t(b):
                for k, (n, h0, hs) in enumerate(STACKS):
                    t.wait_ge(S("a_stack"), ONE + b * TILES + n + 1)
                    if k == 0:
                        t.wait_ge(S("a_mT_out"), ONE + b)
                    elif k > 1:
                        t.wait_ge(S("a_st_out"), ONE + b * NS + k - 1)
                    dst = full(6 + k % 2).bitcast(BF16)
                    for h in range(h0, h0 + hs):
                        m = t.transpose(dst[0:A_STACK, (h - h0) * PARTS:(h - h0 + 1) * PARTS],
                                        stack[:, n, h, :, :, :].rearrange("p i j d -> p (i j d)"), ident_h[:, :])
                    m.then_inc(S("a_st"), 1)

            def a_scores_q(b, par, u):
                qt, h0, nh = USES_Q[u]
                nk = (qt + 1) * PARTS
                if u == 0:
                    t.wait_ge(S("a_st_out"), ONE + b * NS + NS)
                if u >= 2:
                    t.wait_ge(S("a_mx"), ONE + b * NQ + u - 1)
                else:
                    t.wait_ge(S("a_mx"), ONE + b * NQ)
                dst = full(u % 2)
                for i in range(nh):
                    h = h0 + i
                    t.matmul(dst[:, i * nk:(i + 1) * nk], qkT_a[par][0:A_STACK, h, qt * PARTS:(qt + 1) * PARTS],
                             qkT_a[par][0:A_STACK, A_HEADS + h // A_GROUP, 0:nk], start=True, stop=False,
                             skip_group_check=True)
                t.matmul(dst.rearrange("p (h k) -> p h k", h=nh)[:, :, nk - PARTS:nk], ident_h[:, :],
                         mask_a[:, 0:nh, :], start=False, stop=True, skip_group_check=True).then_inc(S("a_sc"), 1)

            def a_turn_m(b, first=False):
                t.wait_ge(S("a_mp"), ONE + b + 1)
                if not first:
                    t.wait_ge(S("a_h0T_out"), ONE + b - 1)
                plain(t)
                dst = full(6).bitcast(BF16)
                for n in range(TILES):
                    m = t.transpose(dst[0:SPLIT * A_HEADS, n * PARTS:(n + 1) * PARTS],
                                    m_part[:, n, :, :].rearrange("p i h -> p (i h)"), ident_h[:, :])
                m.then_inc(S("a_mT"), 1)

            def a_scores_k(b, par, u):
                kt, h0, nh = USES_K[u]
                q0 = kt * PARTS
                if u == 0:
                    t.wait_ge(ld_m, b * M_LOADS + M_LOADS)
                if u >= 2:
                    t.wait_ge(S("a_exp"), ONE + b * NK + u - 1)
                else:
                    t.wait_ge(S("a_exp"), ONE + b * NK)
                dst = full(2 + u % 2)
                t.matmul(dst, qkT_a[par][:, A_HEADS + h0 // A_GROUP, kt * PARTS:(kt + 1) * PARTS],
                         qkT_a[par][:, h0:h0 + nh, q0:SEQ], start=True, stop=False, skip_group_check=True)
                t.matmul(dst.rearrange("p (h q) -> p h q", h=nh)[:, :, 0:PARTS], mask_a[:, 0, :],
                         ident_4[:, 0:nh, :], start=False, stop=True, skip_group_check=True).then_inc(S("a_p2"), 1)

            def a_values(b, par, g):
                t.wait_ge(S("a_exp"), ONE + b * NK + 3 * g + 3)
                if g == 0:
                    t.wait_ge(S("a_v"), ONE + b + 1)
                    t.wait_ge(S("a_yin"), ONE + b)
                dst = full(4 + g // 2)[:, (g % 2) * SEQ:(g % 2 + 1) * SEQ]
                for kt in range(TILES):
                    for i in range(A_GROUP):
                        h = g * A_GROUP + i
                        src = pT_k0[:, h, :] if kt == 0 else pT_k1[:, h, :]
                        m = t.matmul(dst[i * A_COLS:(i + 1) * A_COLS, kt * PARTS:SEQ], v_a[par][:, kt, g, :], src,
                                     start=(kt == 0), stop=(kt == 1), tile_position=(0, i * A_COLS),
                                     skip_group_check=True)
                m.then_inc(S("a_pv"), 1)

            def a_turn_back(b):
                t.wait_ge(S("a_ov"), ONE + b * 2 + 2)
                for n in range(TILES):
                    for g in range(A_KV):
                        m = t.transpose(full(4 + n)[:, g * PARTS:(g + 1) * PARTS],
                                        ovT[:, g, n * PARTS:(n + 1) * PARTS], ident)
                m.then_inc(S("a_back"), 1)

            def a_out(b):
                t.wait_ge(S("a_o"), ONE + b + 1)
                for n in range(TILES):
                    m = t.transpose(full(4)[:, n * PARTS:(n + 1) * PARTS], o_a[:, n, :], ident)
                m.then_inc(S("a_oT"), 1)
                t.wait_ge(S("a_oT_out"), ONE + b + 1)
                for n in range(TILES):
                    m = t.matmul(full(4)[:, n * DIM:(n + 1) * DIM], oT_a[:, n * PARTS:(n + 1) * PARTS], wout[:, :],
                                 start=True, stop=True)
                m.then_inc(S("a_y"), 1)

            def a_h0(b, one, two):
                t.wait_ge(S("a_h0"), ONE + b + 1)
                if two:
                    t.wait_ge(S("a_st_out"), ONE + (b + 2) * NS + NS)
                elif one:
                    t.wait_ge(S("a_mT_out"), ONE + b + 2)
                for n in range(TILES):
                    m = t.transpose(full(6)[:, n * PARTS:(n + 1) * PARTS], z_a[:, n, :], ident)
                m.then_inc(S("a_h0T"), 1)

            def a_step(b, par, one, two):
                nxt = 1 - par
                if two:
                    a_norm_t(b + 2)
                for g in range(A_KV):
                    for u in range(3 * g, 3 * g + 3):
                        a_scores_k(b, par, u)
                        if one:
                            a_scores_q(b + 1, nxt, u)
                        if two and u == 0:
                            a_proj(b + 2)
                    if g:
                        a_values(b, par, g - 1)
                a_values(b, par, A_KV - 1)
                a_turn_back(b)
                if one:
                    a_turn_m(b + 1)
                a_out(b)
                if two:
                    a_stack_t(b + 2)
                a_h0(b, one, two)

            t.wait_ge(S("w_ready"), 2)
            a_norm_t(0)
            a_proj(0)
            a_stack_t(0)
            a_norm_t(1)
            a_proj(1)
            for u in range(NQ):
                a_scores_q(0, 0, u)
            a_turn_m(0, first=True)
            a_stack_t(1)
            with t.Fori(0, (BATCH - 2) // 2) as j:
                a_step(2 * j, 0, True, True)
                a_step(2 * j + 1, 1, True, True)
            a_step(BATCH - 2, 0, True, False)
            a_step(BATCH - 1, 1, False, False)

            def b_proj(i, n):
                if n == 0:
                    t.wait_ge(S("b_hT"), ONE + 2 * i + 2)
                    t.wait_ge(S("b_trT_out"), ONE + 4 * i)
                else:
                    t.wait_ge(S("b_rot"), ONE + 2 * i + 1)
                for c in range(2):
                    m = t.matmul(pj[:, c * INNER:(c + 1) * INNER], hT[:, n * PARTS:(n + 1) * PARTS],
                                 wqkv[:, c * INNER:(c + 1) * INNER], start=True, stop=True)
                m.then_inc(S("b_qk"), 1)

            def b_v(i):
                t.wait_ge(S("b_rot"), ONE + 2 * i + 2)
                for n in range(TILES):
                    m = t.matmul(pj[:, n * INNER:(n + 1) * INNER], hT[:, n * PARTS:(n + 1) * PARTS],
                                 wqkv[:, 2 * INNER:3 * INNER], start=True, stop=True)
                    m.then_inc(S("b_vp"), 1)

            def b_turn_qk(i, n):
                t.wait_ge(S("b_qkr"), ONE + 2 * i + n + 1)
                for c in range(2):
                    if n == 0:
                        t.wait_ge(S("b_v"), ONE + 2 * i + c + 1)
                    else:
                        t.wait_ge(S("b_trT_out"), ONE + 4 * i + c + 1)
                    for p in range(PAIRS):
                        m = t.transpose(pj[:, c * 512 + p * PARTS:c * 512 + (p + 1) * PARTS],
                                        rc[:, n, c, p * PARTS:(p + 1) * PARTS], ident)
                    m.then_inc(S("b_trT"), 1)

            def b_scores(x, par, u):
                qt, heads = USES_B[u]
                nk = keys_b(qt)
                if u == 0:
                    t.wait_ge(S("b_trT_out"), ONE + 4 * x + 4)
                t.wait_ge(S("b_exp"), ONE + x * NUB + (u - 2 if u >= 2 else 0))
                dst = sc_b[u % 3]
                mask = mask_b0[:, :, :] if qt == 0 else mask_b1[:, :, :]
                k0, k1 = (0, PARTS) if qt == 0 else (WINDOW, SEQ)
                t.matmul(dst[:, 0:len(heads) * nk], ident_h[:, :], mask.rearrange("p a b -> p (a b)"),
                         start=True, stop=False, skip_group_check=True)
                for n, h in enumerate(heads):
                    r = (h % 2) * HD
                    m = t.matmul(dst[:, n * nk:(n + 1) * nk],
                                 qkT[par][r:r + HD, 0, h // 2, qt * PARTS:(qt + 1) * PARTS],
                                 qkT[par][r:r + HD, 1, h // 2, k0:k1], start=False, stop=True,
                                 skip_group_check=True)
                m.then_inc(S("b_sc"), 1)

            def b_turn_p(i, par, h):
                t.wait_ge(S("b_p"), ONE + i * HEADS + h + 1)
                t.wait_ge(S("b_pT_act" if h % 2 == 0 else "b_pT_dve"), ONE + i * (HEADS // 2) + h // 2)
                dst = pt_b[h % 2]
                t.transpose(dst[:, 0:PARTS], p_b0[par][:, h, :], ident)
                for kb in range(2):
                    m = t.transpose(dst[:, (kb + 1) * PARTS:(kb + 2) * PARTS],
                                    p_b1[par][:, h, kb * PARTS:(kb + 1) * PARTS], ident)
                m.then_inc(S("b_pT"), 1)

            def b_values(i, par, p):
                t.wait_ge(S("b_pT_act"), ONE + i * (HEADS // 2) + p + 1)
                t.wait_ge(S("b_pT_dve"), ONE + i * (HEADS // 2) + p + 1)
                if p == 0:
                    t.wait_ge(S("b_x"), ONE + i)
                if p == 2:
                    t.wait_ge(S("b_o"), ONE + 2 * i + 1)
                for kb in range(2):
                    q0 = kb * PARTS
                    for k in range(2):
                        h = 2 * p + k
                        src = pT_b[:, h % 4, 0:SEQ] if kb == 0 else pT_b[:, h % 4, SEQ:SEQ + PARTS]
                        m = t.matmul(ov_b[k * HD:(k + 1) * HD, (p % 2) * SEQ + q0:(p % 2) * SEQ + SEQ],
                                     v_b[par][:, kb, h * HD:(h + 1) * HD], src, start=(kb == 0), stop=(kb == 1),
                                     skip_group_check=True)
                m.then_inc(S("b_pv"), 1)

            def b_out(i):
                t.wait_ge(S("b_o"), ONE + 2 * i + 2)
                for p in range(PAIRS):
                    m = t.matmul(ov_b[:, 0:SEQ], wo[:, p, :], oT_b[:, p, :], start=(p == 0), stop=(p == PAIRS - 1))
                m.then_inc(S("b_y"), 1)

            def b_step(i, par, one, two):
                nxt = 1 - par
                if one:
                    b_v(i + 1)
                b_turn_p(i, par, 0)
                b_turn_p(i, par, 1)
                b_values(i, par, 0)
                b_turn_p(i, par, 2)
                b_turn_p(i, par, 3)
                if one:
                    b_turn_qk(i + 1, 0)
                b_values(i, par, 1)
                b_turn_p(i, par, 4)
                b_turn_p(i, par, 5)
                if one:
                    b_turn_qk(i + 1, 1)
                b_values(i, par, 2)
                b_turn_p(i, par, 6)
                b_turn_p(i, par, 7)
                if one:
                    b_scores(i + 1, nxt, 0)
                if two:
                    b_proj(i + 2, 0)
                b_values(i, par, 3)
                if one:
                    b_scores(i + 1, nxt, 1)
                if one:
                    b_scores(i + 1, nxt, 2)
                b_out(i)
                if one:
                    b_scores(i + 1, nxt, 3)
                if two:
                    b_proj(i + 2, 1)
                if one:
                    b_scores(i + 1, nxt, 4)
                    b_scores(i + 1, nxt, 5)

            def f_norm_t(i):
                t.wait_ge(S("f_hT"), ONE + 4 * i + 4)
                t.wait_ge(S("f_y"), ONE + i)
                for n in range(GT):
                    m = t.transpose(lnf[0][:, n * PARTS:(n + 1) * PARTS], hTf[:, n // TILES, (n % TILES) * PARTS:(n % TILES + 1) * PARTS], ident)
                m.then_inc(S("f_h"), 1)

            def f_back_t(i):
                t.wait_ge(S("f_y"), ONE + i + 1)
                t.wait_ge(S("f_yT"), ONE + i)
                for n in range(GT):
                    m = t.transpose(lnf[1][:, n * PARTS:(n + 1) * PARTS], yf[:, n, :], ident)
                m.then_inc(S("f_ty"), 1)

            def f_up(i, c):
                if c == 0:
                    t.wait_ge(S("f_yT"), ONE + i + 1)
                h0, n = HCH[c]
                use = i * NCH + c
                if c < 2:
                    t.wait_ge(S("f_act"), ONE + i * NCH)
                else:
                    t.wait_ge(S("f_act"), ONE + i * NCH + c - 1)
                for half in range(2):
                    col = (1 - half) * HID + h0
                    m = t.matmul(up[half][c % 2][0:n, :], w1[:, col:col + n], yfT[:, :], start=True, stop=True)
                    m.then_inc(S("f_up"), 1)

            def f_down(i, c):
                h0, n = HCH[c]
                t.wait_ge(S("f_act"), ONE + i * NCH + c + 1)
                if c == 0:
                    t.wait_ge(S("f_x"), ONE + i)
                m = t.matmul(down[:, :], w2[0:n, c, :], act[0:n, c, :], start=(c == 0), stop=(c == NCH - 1))
                if c == NCH - 1:
                    m.then_inc(S("f_down"), 1)

            def f_body(i, more):
                f_up(i, 0)
                f_up(i, 1)
                if more:
                    f_norm_t(i + 1)
                f_up(i, 2)
                f_down(i, 0)
                f_down(i, 1)
                f_down(i, 2)
                if more:
                    f_back_t(i + 1)

            with t.Fori(0, DEPTH) as l:
                i0 = l * BATCH
                t.wait_ge(ld_att, l * 64 + 64)
                t.wait_ge(S("a_h0T_out"), ONE + BATCH)
                t.wait_ge(S("f_x"), ONE + l * GROUPS)
                b_proj(i0, 0)
                b_proj(i0, 1)
                b_v(i0)
                b_turn_qk(i0, 0)
                b_turn_qk(i0, 1)
                b_proj(i0 + 1, 0)
                b_proj(i0 + 1, 1)
                for u in range(NUB):
                    b_scores(i0, 0, u)
                with t.Fori(0, (BATCH - 2) // 2) as j:
                    b_step(i0 + 2 * j, 0, True, True)
                    b_step(i0 + 2 * j + 1, 1, True, True)
                b_step(i0 + (BATCH - 2), 0, True, False)
                b_step(i0 + (BATCH - 1), 1, False, False)
                g0 = l * GROUPS
                t.wait_ge(ld_ffn, (l + 1) * (16 * FFN_LOADS))
                t.wait_ge(S("b_x"), ONE + i0 + BATCH)
                f_norm_t(g0)
                f_back_t(g0)
                with t.Fori(0, GROUPS - 1) as g:
                    f_body(g0 + g, True)
                f_body(g0 + (GROUPS - 1), False)

            t.wait_ge(S("f_x"), ONE + DEPTH * GROUPS)
            for g in range(GROUPS):
                for n in range(GT):
                    m = t.transpose(full(g)[:, n * PARTS:(n + 1) * PARTS],
                                    xT[:, 2 * g + n // TILES, (n % TILES) * PARTS:(n % TILES + 1) * PARTS], ident)
                m.then_inc(S("last_t"), 1)

        @block.scalar
        def _(s):
            for name in ("a_xnT_out a_st_out a_mT_out a_exp a_ov a_oT_out a_h0T_out b_hT b_sq b_v b_trT_out b_exp b_pT_act b_o "
                         "f_hT f_yT f_gate").split():
                s.sem_inc(S(name), ONE)
            s.wait_ge(S("w_t"), 1)
            s.activation(wqaT[:, :], full(0)[0:A_QL, 0:PARTS], ACT.Copy).then_inc(S("w_copied"), 1)
            s.activation(wkvaT[:, :], full(0)[0:A_KVL, PARTS:2 * PARTS], ACT.Copy).then_inc(S("w_copied"), 1)
            s.wait_ge(S("w_prod"), 1)
            s.activation(w_a[:, 0:DIM], full(1)[:, 0:DIM], ACT.Copy).then_inc(S("w_ready"), 1)
            s.activation(w_a[:, DIM:A_W].rearrange("p (c x) -> p c x", c=2),
                         full(1)[:, DIM:A_W].rearrange("p (x c) -> p c x", c=2), ACT.Copy).then_inc(S("w_ready"), 1)

            def a_xnT(b):
                s.wait_ge(S("a_xnT"), ONE + b + 1)
                s.wait_ge(S("a_qkv"), ONE + b)
                s.activation(xnT[:, :], full(7)[:, 0:SEQ], ACT.Copy).then_inc(S("a_xnT_out"), 1)

            def a_stack_out(b, par, first=False):
                for k, (n, h0, hs) in enumerate(STACKS):
                    s.wait_ge(S("a_st"), ONE + b * NS + k + 1)
                    if k == 0 and not first:
                        s.wait_ge(S("a_p2"), ONE + (b - 1) * NK)
                    src = full(6 + k % 2).bitcast(BF16)[0:A_STACK, 0:hs * PARTS].rearrange("p (h q) -> p h q", h=hs)
                    s.activation(qkT_a[par][0:A_STACK, h0:h0 + hs, n * PARTS:(n + 1) * PARTS], src, ACT.Copy)\
                        .then_inc(S("a_st_out"), 1)

            def a_mT_out(b, first=False):
                s.wait_ge(S("a_mT"), ONE + b + 1)
                if not first:
                    s.wait_ge(ld_m, b * M_LOADS)
                s.activation(mT[:, :], full(6).bitcast(BF16)[0:SPLIT * A_HEADS, 0:SEQ], ACT.Copy)\
                    .then_inc(S("a_mT_out"), 1)

            def a_exp(b, u):
                kt, h0, nh = USES_K[u]
                s.wait_ge(S("a_p2"), ONE + b * NK + u + 1)
                if u == 0:
                    s.wait_ge(S("a_pv"), ONE + b * A_KV)
                dst = pT_k0[:, h0:h0 + nh, :] if kt == 0 else pT_k1[:, h0:h0 + nh, :]
                s.activation(dst.rearrange("p h q -> p (h q)"), full(2 + u % 2), ACT.Exp, scale=A_SCALE)\
                    .then_inc(S("a_exp"), 1)

            def a_ov(b, k):
                s.wait_ge(S("a_pv"), ONE + b * A_KV + 2 * k + 2)
                s.wait_ge(S("a_back"), ONE + b)
                s.activation(ovT[:, 2 * k:2 * k + 2, :].rearrange("p g q -> p (g q)"), full(4 + k), ACT.Copy)\
                    .then_inc(S("a_ov"), 1)

            def a_oT(b):
                s.wait_ge(S("a_oT"), ONE + b + 1)
                s.wait_ge(S("a_y"), ONE + b)
                s.activation(oT_a[:, :], full(4)[:, 0:SEQ], ACT.Copy).then_inc(S("a_oT_out"), 1)

            def a_h0T(b):
                s.wait_ge(S("a_h0T"), ONE + b + 1)
                s.activation(xT[:, bass.ds(b, 1), :].rearrange("p o s -> p (o s)"), full(6)[:, 0:SEQ], ACT.Copy)\
                    .then_inc(S("a_h0T_out"), 1)

            def a_step(b, par, one, two):
                if two:
                    a_xnT(b + 2)
                for u in range(NK):
                    a_exp(b, u)
                    if u == 10:
                        a_ov(b, 0)
                a_ov(b, 1)
                if one:
                    a_mT_out(b + 1)
                a_oT(b)
                if two:
                    a_stack_out(b + 2, par)
                a_h0T(b)

            s.wait_ge(S("a_rows"), 1)
            a_xnT(0)
            a_stack_out(0, 0, first=True)
            a_xnT(1)
            a_mT_out(0, first=True)
            a_stack_out(1, 1, first=True)
            with s.Fori(0, (BATCH - 2) // 2) as j:
                a_step(2 * j, 0, True, True)
                a_step(2 * j + 1, 1, True, True)
            a_step(BATCH - 2, 0, True, False)
            a_step(BATCH - 1, 1, False, False)

            def b_hT(i, b):
                s.wait_ge(S("b_vp"), ONE + 2 * i)
                src = xT[:, bass.ds(b, 1), :].rearrange("p o s -> p (o s)")
                s.activation(hT[0:64, :], src[0:64, :], ACT.Copy).then_inc(S("b_hT"), 1)
                s.activation(hT[64:128, 1:SEQ], src[64:128, 0:SEQ - 1], ACT.Copy).then_inc(S("b_hT"), 1)

            def b_sq(i, n):
                s.wait_ge(S("b_qk"), ONE + 2 * i + n + 1)
                s.wait_ge(S("b_ss"), ONE + 2 * i + n)
                s.activation(sq[:, :, :].rearrange("p c n -> p (c n)"), pj[:, :], ACT.Square).then_inc(S("b_sq"), 1)

            def b_v(x, par, first=False):
                for n in range(TILES):
                    s.wait_ge(S("b_vp"), ONE + 2 * x + n + 1)
                    if n == 0:
                        s.wait_ge(S("b_pv"), ONE + done(x, PAIRS, first))
                    s.activation(v_b[par][:, n, :], pj[:, n * INNER:(n + 1) * INNER], ACT.Copy).then_inc(S("b_v"), 1)

            def b_qkT(x, par, n, first=False):
                for c in range(2):
                    s.wait_ge(S("b_trT"), ONE + 4 * x + 2 * n + c + 1)
                    if n == 0 and c == 0:
                        s.wait_ge(S("b_sc"), ONE + done(x, NUB, first))
                    s.activation(qkT[par][:, c, :, n * PARTS:(n + 1) * PARTS],
                                 pj[:, c * 512:(c + 1) * 512].rearrange("p (a q) -> p a q", a=PAIRS),
                                 ACT.Copy).then_inc(S("b_trT_out"), 1)

            def b_exp(x, par, u, first=False):
                qt, heads = USES_B[u]
                s.wait_ge(S("b_sc"), ONE + x * NUB + u + 1)
                s.wait_ge(S("b_nm"), ONE + x * NUB + u + 1)
                if u == 0:
                    s.wait_ge(S("b_pT"), ONE + done(x, HEADS, first))
                nk = keys_b(qt)
                for n, h in enumerate(heads):
                    m = s.activation(p_slice_b(par, qt, h), sc_b[u % 3][:, n * nk:(n + 1) * nk], ACT.Exp,
                                     bias=nm_b[par][:, qt, h:h + 1], scale=r_q8[par][:, qt, h:h + 1],
                                     accum_out=sum_b[par][:, qt, h:h + 1])
                m.then_inc(S("b_exp"), 1)

            def b_pT_out(i, h):
                s.wait_ge(S("b_pT"), ONE + i * HEADS + h + 1)
                if h >= 4:
                    s.wait_ge(S("b_pv"), ONE + i * PAIRS + h // 2 - 1)
                s.activation(pT_b[:, h % 4, :], pt_b[h % 2][:, 0:PARTS + SEQ], ACT.Copy).then_inc(S("b_pT_act"), 1)

            def b_o(i, k):
                s.wait_ge(S("b_pv"), ONE + i * PAIRS + 2 * k + 2)
                s.wait_ge(S("b_y"), ONE + i)
                s.activation(oT_b[:, 2 * k:2 * k + 2, :], ov_b[:, :].rearrange("p (a q) -> p a q", a=2), ACT.Copy)\
                    .then_inc(S("b_o"), 1)

            def b_step(i, b, par, one, two):
                nxt = 1 - par
                b_pT_out(i, 0)
                if one:
                    b_v(i + 1, nxt)
                b_pT_out(i, 2)
                if one:
                    b_qkT(i + 1, nxt, 0)
                b_pT_out(i, 4)
                b_o(i, 0)
                if one:
                    b_qkT(i + 1, nxt, 1)
                b_pT_out(i, 6)
                if two:
                    b_hT(i + 2, b + 2)
                    b_sq(i + 2, 0)
                if one:
                    b_exp(i + 1, nxt, 0)
                b_o(i, 1)
                if one:
                    b_exp(i + 1, nxt, 1)
                    b_exp(i + 1, nxt, 2)
                if two:
                    b_sq(i + 2, 1)
                if one:
                    b_exp(i + 1, nxt, 3)
                    b_exp(i + 1, nxt, 4)
                    b_exp(i + 1, nxt, 5)

            def f_hT(i, g):
                s.wait_ge(S("f_h"), ONE + i)
                src = xT[:, bass.ds(g * 2, 2), :]
                for n in range(2):
                    s.activation(hTf[0:64, n, :], src[0:64, n, :], ACT.Copy).then_inc(S("f_hT"), 1)
                    s.activation(hTf[64:128, n, 1:SEQ], src[64:128, n, 0:SEQ - 1], ACT.Copy).then_inc(S("f_hT"), 1)

            def f_yT(i):
                s.wait_ge(S("f_ty"), ONE + i + 1)
                s.wait_ge(S("f_up"), ONE + i * (2 * NCH))
                s.activation(yfT[:, :], lnf[1], ACT.Identity, bias=ln_b[:, 0:1], scale=ln_g[:, 0:1])\
                    .then_inc(S("f_yT"), 1)

            def f_gate(i, c):
                h0, n = HCH[c]
                s.wait_ge(S("f_up"), ONE + i * (2 * NCH) + 2 * c + 1)
                s.wait_ge(S("f_act"), ONE + i * NCH)
                s.activation(gate[0:n, c, :], up[0][c % 2][0:n, :], ACT.Gelu, bias=b1[0:n, 1, c:c + 1])\
                    .then_inc(S("f_gate"), 1)

            def f_body(i, g, more):
                if more:
                    f_hT(i + 1, g + 1)
                for c in range(NCH):
                    f_gate(i, c)
                if more:
                    f_yT(i + 1)

            with s.Fori(0, DEPTH) as l:
                i0 = l * BATCH
                s.wait_ge(S("b_zero"), 2)
                s.wait_ge(S("f_x"), ONE + l * GROUPS)
                s.wait_ge(S("a_h0T_out"), ONE + BATCH)
                b_hT(i0, 0)
                b_sq(i0, 0)
                b_sq(i0, 1)
                b_v(i0, 0, first=True)
                b_qkT(i0, 0, 0, first=True)
                b_qkT(i0, 0, 1, first=True)
                b_hT(i0 + 1, 1)
                b_sq(i0 + 1, 0)
                b_sq(i0 + 1, 1)
                for u in range(NUB):
                    b_exp(i0, 0, u, first=True)
                with s.Fori(0, (BATCH - 2) // 2) as j:
                    b_step(i0 + 2 * j, 2 * j, 0, True, True)
                    b_step(i0 + 2 * j + 1, 2 * j + 1, 1, True, True)
                b_step(i0 + (BATCH - 2), BATCH - 2, 0, True, False)
                b_step(i0 + (BATCH - 1), BATCH - 1, 1, False, False)
                g0 = l * GROUPS
                s.wait_ge(ld_ffn, (l + 1) * (16 * FFN_LOADS))
                s.wait_ge(S("b_x"), ONE + i0 + BATCH)
                f_hT(g0, 0)
                f_yT(g0)
                with s.Fori(0, GROUPS - 1) as g:
                    f_body(g0 + g, g, True)
                f_body(g0 + (GROUPS - 1), GROUPS - 1, False)

        @block.vector
        def _(v):
            for name in ("a_xn a_rope a_mx a_mp a_inv a_o a_yin a_ve2 a_h0 b_tab b_ss b_n2 b_rot b_r8 b_scq b_mx b_nm b_inv "
                         "b_p b_pT_dve b_x f_st f_mv f_ve f_y f_act f_x").split():
                v.sem_inc(S(name), ONE)
            v.memset(minus_half[:, :], -0.5).then_inc(S("half"), 1)
            v.memset(hT[64:128, 0:1], 0.0).then_inc(S("b_zero"), 1)
            for par in range(2):
                m = v.memset(p_b1[par][:, :, 0:WINDOW], 0.0)
            m.then_inc(S("b_zero"), 1)
            v.memset(hTf[64:128, :, 0:1], 0.0).then_inc(S("f_zero"), 1)
            for par in range(2):
                v.memset(qkT_a[par][64:A_STACK + SPLIT, A_HEADS:A_QK, :], 1.0)
                v.memset(v_a[par][:, :, :, A_D:A_D + 1], 1.0)
                m = v.memset(v_a[par][:, :, :, A_D + 1:A_COLS], 0.0)
            m.then_inc(S("a_rows"), 1)
            v.wait_ge(ld_c, 16)
            v.tensor_copy(ident_h[:, :], ident)
            v.tensor_copy(ident_4[:, :, :], ident.unsqueeze(1).broadcast_to([PARTS, 4, PARTS]))
            v.tensor_copy(mask_a[:, :, :], const[:, C_MA:C_MB0].unsqueeze(1).broadcast_to([PARTS, 4, PARTS]))
            v.tensor_copy(mask_b0[:, :, :], const[:, C_MB0:C_MB1].unsqueeze(1).broadcast_to([PARTS, 4, PARTS]))
            v.tensor_copy(mask_b1[:, :, :], const[:, C_MB1:C_RA].unsqueeze(1).broadcast_to([PARTS, 2, B1K]))\
                .then_inc(S("consts_cast"), 1)

            own_m = Own(v, S("dve_am"), 3)
            own_t = Own(v, S("dve_at"), 7)

            def bcast_heads(x, n, h, d):
                return x.unsqueeze(2).broadcast_to([PARTS, n, h, d])

            def a_stats(k, b0, b1):
                v.wait_ge(ld_x if k else ld_x0, 16)
                for b in range(b0, b1):
                    for n in range(TILES):
                        m = v.bn_stats(st[:, b, n, :], x_all[:, b, n, :])
                m.then_inc(S("a_stat"), 1)
                v.wait_ge(S("a_stat"), 2 * k + 1)
                for b in range(b0, b1):
                    for n in range(TILES):
                        m = v.bn_aggr(mv[:, b, n, :], st[:, b, n, :])
                m.then_inc(S("a_stat"), 1)
                v.wait_ge(S("a_stat"), 2 * k + 2)
                v.tensor_scalar(ve[:, b0:b1, :], mv[:, b0:b1, :, 1], EPS, None, ALU.add).then_inc(S("a_ve"), 1)

            def a_norm(b):
                one = bass.ds(b, 1)
                v.wait_ge(S("a_xnT"), ONE + b)
                for n in range(TILES):
                    m = v.tensor_scalar(xn[:, n, :], x_all[:, one, n, :].rearrange("p o d -> p (o d)"),
                                        mv[:, one, n, 0], rs1[:, one, n], ALU.subtract, ALU.mult)
                m.then_inc(S("a_xn"), 1)

            def a_rope(b):
                v.wait_ge(S("a_qkv"), ONE + b + 1)
                v.wait_ge(S("a_sum"), ONE + b * TILES)
                v.wait_ge(S("a_v"), ONE + b)
                qkv = full(7)[:, 0:TILES * A_W].rearrange("p (t w) -> p t w", t=TILES)
                w = A_QK * A_D
                qk = qkv[:, :, 0:w].rearrange("p t (h d) -> p t h d", d=A_D)
                v.tensor_tensor(rope_c[:, :, :, :], qk, bcast_heads(cos_a, TILES, A_QK, A_D), ALU.mult)
                for k in range(2):
                    v.tensor_tensor(rope_s[:, :, :, k::2], qk[:, :, :, 1 - k::2],
                                    bcast_heads(sin_a[:, :, k::2], TILES, A_QK, A_D // 2), ALU.mult)
                v.tensor_copy(v_new[:, :, :], qkv[:, :, w:A_W]).then_inc(S("a_rope"), 1)

            def a_max(b, u):
                qt, h0, nh = USES_Q[u]
                v.wait_ge(S("a_sc"), ONE + b * NQ + u + 1)
                if u == 0:
                    v.wait_ge(S("a_mp"), ONE + b)
                v.tensor_reduce(mx_a[:, qt, h0:h0 + nh], full(u % 2).rearrange("p (h k) -> p h k", h=nh),
                                AX.X, ALU.max).then_inc(S("a_mx"), 1)

            def a_split_m(b):
                own_m.begin(b)
                v.wait_ge(S("a_mx"), ONE + b * NQ + NQ)
                v.wait_ge(S("a_mT"), ONE + b)
                own_m.step(v.tensor_scalar(m_part[:, :, 0, :], mx_a[:, :, :], -1.0, None, ALU.mult))
                own_m.step(v.scalar_tensor_tensor(out=m_left[:, :, :], in0=mx_a[:, :, :], scalar=-1.0,
                                                  in1=m_part[:, :, 0, :], op0=ALU.mult, op1=ALU.subtract))
                own_m.step(v.tensor_copy(m_part[:, :, 1, :], m_left[:, :, :]))
                v.tensor_tensor(m_part[:, :, 2, :], m_left[:, :, :], m_part[:, :, 1, :], ALU.subtract)\
                    .then_inc(S("a_mp"), 1)

            def a_o(b):
                v.wait_ge(S("a_back"), ONE + b + 1)
                both = bank[2][:, :].rearrange("p (t h c) -> p t h c", t=TILES, c=A_COLS)
                v.reciprocal(inv_a[:, :, :], both[:, :, :, A_D]).then_inc(S("a_inv"), 1)
                v.wait_ge(S("a_inv"), ONE + b + 1)
                v.wait_ge(S("a_oT"), ONE + b)
                v.tensor_tensor(o_a[:, :, :].rearrange("p t (h d) -> p t h d", d=A_D), both[:, :, :, 0:A_D],
                                inv_a[:, :, :].unsqueeze(3).broadcast_to([PARTS, TILES, A_HEADS, A_D]), ALU.mult)\
                    .then_inc(S("a_o"), 1)

            def a_tail(b):
                own_t.begin(b)
                v.wait_ge(S("a_y"), ONE + b + 1)
                v.tensor_tensor(y_a[:, :, :], full(4)[:, 0:TILES * DIM].rearrange("p (t d) -> p t d", t=TILES),
                                bout[:, :].unsqueeze(1).broadcast_to([PARTS, TILES, DIM]), ALU.add)\
                    .then_inc(S("a_yin"), 1)
                v.wait_ge(S("a_yin"), ONE + b + 1)
                for k in range(2):
                    src = y_a if k == 0 else z_a
                    for n in range(TILES):
                        m = v.bn_stats(st2[:, n, :], src[:, n, :])
                    own_t.step(m)
                    plain(v)
                    for n in range(TILES):
                        m = v.bn_aggr(mv2[:, n, :], st2[:, n, :])
                    own_t.step(m)
                    v.tensor_scalar(ve2[:, :], mv2[:, :, 1], EPS, None, ALU.add).then_inc(S("a_ve2"), 1)
                    v.wait_ge(S("a_rs2"), ONE + 2 * b + k + 1)
                    if k == 0:
                        v.wait_ge(S("a_h0T"), ONE + b)
                        for n in range(TILES):
                            m = v.tensor_scalar(y_a[:, n, :], y_a[:, n, :], mv2[:, n, 0:1], rs2[:, n:n + 1],
                                                ALU.subtract, ALU.mult)
                        own_t.step(m)
                        x1 = x_all[:, bass.ds(b, 1), :, :].rearrange("p o t d -> p (o t) d")
                        own_t.step(v.tensor_tensor(z_a[:, :, :], y_a[:, :, :], x1, ALU.add))
                        own_t.step(v.tensor_tensor(x1, y_a[:, :, :], x1, ALU.add))
                    else:
                        for n in range(TILES):
                            m = v.tensor_scalar(z_a[:, n, :], z_a[:, n, :], mv2[:, n, 0:1], rs2[:, n:n + 1],
                                                ALU.subtract, ALU.mult)
                        m.then_inc(S("a_h0"), 1)
                own_t.end()

            def a_step(b, one, two):
                if two:
                    a_norm(b + 2)
                if one:
                    a_max(b + 1, 0)
                    a_max(b + 1, 1)
                if two:
                    a_rope(b + 2)
                if one:
                    for u in range(2, NQ):
                        a_max(b + 1, u)
                    a_split_m(b + 1)
                a_o(b)
                a_tail(b)

            v.wait_ge(S("half"), 1)
            a_stats(0, 0, 1)
            v.wait_ge(S("a_rs"), 1)
            a_norm(0)
            a_stats(1, 1, BATCH)
            a_rope(0)
            v.wait_ge(S("a_rs"), 2)
            a_norm(1)
            a_rope(1)
            for u in range(NQ):
                a_max(0, u)
            a_split_m(0)
            with v.Fori(0, BATCH - 2) as b:
                a_step(b, True, True)
            a_step(BATCH - 2, True, False)
            a_step(BATCH - 1, False, False)

            def l_tables(l):
                v.wait_ge(ld_att, l * 64 + 64)
                v.wait_ge(S("b_rot"), ONE + l * (BATCH * TILES))
                for n in range(TILES):
                    v.tensor_tensor(tab_c[:, n, :, :], rot_raw[:, 0, n, :, :], scales[:, :, :], ALU.mult)
                    for k in range(2):
                        o = slice(k * (HD // 2), (k + 1) * (HD // 2))
                        p = slice((1 - k) * (HD // 2), (2 - k) * (HD // 2))
                        m = v.tensor_tensor(tab_s[:, n, :, o], rot_raw[:, 1, n, :, o], scales[:, :, p], ALU.mult)
                m.then_inc(S("b_tab"), 1)
                v.wait_ge(S("b_tab"), ONE + l + 1)

            def b_norms(i, n):
                v.wait_ge(S("b_sq"), ONE + 2 * i + n + 1)
                v.wait_ge(S("b_r"), ONE + 2 * i)
                v.tensor_reduce(ss[:, n, :], sq[:, :, :].rearrange("p c (h d) -> p (c h) d", d=HD), AX.X, ALU.add)\
                    .then_inc(S("b_ss"), 1)
                v.wait_ge(S("b_ss"), ONE + 2 * i + n + 1)
                v.tensor_scalar(ss[:, n, :], ss[:, n, :], TINY, None, ALU.max).then_inc(S("b_n2"), 1)

            def b_rot(i, n):
                v.wait_ge(S("b_trT"), ONE + 4 * i)
                v.wait_ge(S("b_qkr"), ONE + 2 * i)
                v.wait_ge(S("b_sq"), ONE + 2 * i + n + 1)
                src = pj[:, :].rearrange("p (c h d) -> p c h d", c=2, d=HD)
                v.tensor_tensor(rc[:, n, :, :].rearrange("p c (h d) -> p c h d", d=HD), src,
                                tab_c[:, n, :, :].unsqueeze(2).broadcast_to([PARTS, 2, HEADS, HD]), ALU.mult)
                dst = rs[:, n, :, :].rearrange("p c (h d) -> p c h d", d=HD)
                for k in range(2):
                    o = slice(k * (HD // 2), (k + 1) * (HD // 2))
                    p = slice((1 - k) * (HD // 2), (2 - k) * (HD // 2))
                    m = v.tensor_tensor(dst[:, :, :, o], src[:, :, :, p],
                                        tab_s[:, n, :, o].unsqueeze(2).broadcast_to([PARTS, 2, HEADS, HD // 2]), ALU.mult)
                m.then_inc(S("b_rot"), 1)

            def b_r8(x, par, first=False):
                v.wait_ge(S("b_r"), ONE + 2 * x + 2)
                v.wait_ge(S("b_exp"), ONE + done(x, NUB, first))
                v.tensor_scalar(r_q8[par][:, :, :], r_qk[:, :, 0:HEADS], QK_SCALE, None, ALU.mult)\
                    .then_inc(S("b_r8"), 1)

            def b_max(x, par, u):
                qt, heads = USES_B[u]
                nk = keys_b(qt)
                v.wait_ge(S("b_sc"), ONE + x * NUB + u + 1)
                hs = slice(heads[0], heads[-1] + 1, 2)
                v.tensor_reduce(mx_b[par][:, qt, hs],
                                sc_b[u % 3][:, 0:len(heads) * nk].rearrange("p (h k) -> p h k", k=nk),
                                AX.X, ALU.max).then_inc(S("b_mx"), 1)
                v.wait_ge(S("b_mx"), ONE + x * NUB + u + 1)
                v.scalar_tensor_tensor(out=nm_b[par][:, qt, hs], in0=mx_b[par][:, qt, hs], scalar=-1.0,
                                       in1=r_q8[par][:, qt, hs], op0=ALU.mult, op1=ALU.mult).then_inc(S("b_nm"), 1)

            def b_probs(i, par, k):
                v.wait_ge(S("b_exp"), ONE + i * NUB + (4 if k == 0 else 6))
                h0 = 4 * k
                v.reciprocal(inv_b[par][:, :, h0:h0 + 4], sum_b[par][:, :, h0:h0 + 4]).then_inc(S("b_inv"), 1)
                v.wait_ge(S("b_inv"), ONE + 2 * i + k + 1)
                for h in range(h0, h0 + 4):
                    for qt in range(2):
                        m = v.tensor_scalar(p_slice_b(par, qt, h), p_slice_b(par, qt, h),
                                            inv_b[par][:, qt, h:h + 1], None, ALU.mult)
                    m.then_inc(S("b_p"), 1)

            def b_pT_out(i, h):
                v.wait_ge(S("b_pT"), ONE + i * HEADS + h + 1)
                if h >= 4:
                    v.wait_ge(S("b_pv"), ONE + i * PAIRS + h // 2 - 1)
                v.tensor_copy(pT_b[:, h % 4, :], pt_b[h % 2][:, 0:PARTS + SEQ]).then_inc(S("b_pT_dve"), 1)

            def b_x(i, b):
                v.wait_ge(S("b_y"), ONE + i + 1)
                x = xT[:, bass.ds(b, 1), :].rearrange("p o s -> p (o s)")
                v.tensor_tensor(x, ov_b[:, 0:SEQ], x, ALU.add).then_inc(S("b_x"), 1)

            def b_step(i, b, par, one, two):
                nxt = 1 - par
                b_probs(i, par, 0)
                if one:
                    b_norms(i + 1, 1)
                b_pT_out(i, 1)
                b_probs(i, par, 1)
                for h in (3, 5):
                    b_pT_out(i, h)
                if one:
                    b_r8(i + 1, nxt)
                b_pT_out(i, 7)
                if one:
                    b_max(i + 1, nxt, 0)
                if two:
                    b_rot(i + 2, 0)
                if one:
                    b_max(i + 1, nxt, 1)
                if one:
                    b_max(i + 1, nxt, 2)
                b_x(i, b)
                if two:
                    b_norms(i + 2, 0)
                if one:
                    b_max(i + 1, nxt, 3)
                if two:
                    b_rot(i + 2, 1)
                if one:
                    b_max(i + 1, nxt, 4)
                    b_max(i + 1, nxt, 5)

            def f_stats(i):
                v.wait_ge(S("f_h"), ONE + i + 1)
                for n in range(GT):
                    m = v.bn_stats(stf[:, n, :], lnf[0][:, n * PARTS:(n + 1) * PARTS])
                m.then_inc(S("f_st"), 1)
                v.wait_ge(S("f_st"), ONE + i + 1)
                plain(v)
                for n in range(GT):
                    m = v.bn_aggr(mvf[:, n, :], stf[:, n, :])
                m.then_inc(S("f_mv"), 1)
                v.wait_ge(S("f_mv"), ONE + i + 1)
                v.tensor_scalar(vef[:, :], mvf[:, :, 1], EPS, None, ALU.add).then_inc(S("f_ve"), 1)

            def f_norm(i):
                v.wait_ge(S("f_rs"), ONE + i + 1)
                v.wait_ge(S("f_ty"), ONE + i)
                for n in range(GT):
                    m = v.tensor_scalar(yf[:, n, :], lnf[0][:, n * PARTS:(n + 1) * PARTS], mvf[:, n, 0:1],
                                        rsf[:, n:n + 1], ALU.subtract, ALU.mult)
                m.then_inc(S("f_y"), 1)

            def f_act(i, c):
                h0, n = HCH[c]
                v.wait_ge(S("f_up"), ONE + i * (2 * NCH) + 2 * c + 2)
                v.wait_ge(S("f_gate"), ONE + i * NCH + c + 1)
                v.wait_ge(S("f_down"), ONE + i)
                v.scalar_tensor_tensor(out=act[0:n, c, :], in0=up[1][c % 2][0:n, :], scalar=b1[0:n, 0, c:c + 1],
                                       in1=gate[0:n, c, :], op0=ALU.add, op1=ALU.mult).then_inc(S("f_act"), 1)

            def f_x(i, g):
                v.wait_ge(S("f_down"), ONE + i + 1)
                x = xT[:, bass.ds(g * 2, 2), :].rearrange("p o s -> p (o s)")
                v.scalar_tensor_tensor(out=x, in0=down[:, :], scalar=b2[:, 0:1], in1=x, op0=ALU.add, op1=ALU.add)\
                    .then_inc(S("f_x"), 1)

            def f_body(i, g, more):
                f_act(i, 0)
                f_act(i, 1)
                if more:
                    f_stats(i + 1)
                f_act(i, 2)
                if more:
                    f_norm(i + 1)
                f_x(i, g)

            with v.Fori(0, DEPTH) as l:
                i0 = l * BATCH
                l_tables(l)
                for n in range(TILES):
                    b_rot(i0, n)
                    b_norms(i0, n)
                b_r8(i0, 0, first=True)
                b_rot(i0 + 1, 0)
                b_norms(i0 + 1, 0)
                b_rot(i0 + 1, 1)
                for u in range(NUB):
                    b_max(i0, 0, u)
                with v.Fori(0, (BATCH - 2) // 2) as j:
                    b_step(i0 + 2 * j, 2 * j, 0, True, True)
                    b_step(i0 + 2 * j + 1, 2 * j + 1, 1, True, True)
                b_step(i0 + (BATCH - 2), BATCH - 2, 0, True, False)
                b_step(i0 + (BATCH - 1), BATCH - 1, 1, False, False)
                g0 = l * GROUPS
                v.wait_ge(ld_ffn, (l + 1) * (16 * FFN_LOADS))
                f_stats(g0)
                f_norm(g0)
                with v.Fori(0, GROUPS - 1) as g:
                    f_body(g0 + g, g, True)
                f_body(g0 + (GROUPS - 1), GROUPS - 1, False)

            for g in range(GROUPS):
                v.wait_ge(S("last_t"), g + 1)
                for n in range(GT):
                    m = v.bn_stats(stl[:, g, n, :], full(g)[:, n * PARTS:(n + 1) * PARTS])
            m.then_inc(S("last_st"), 1)
            v.wait_ge(S("last_st"), 1)
            for g in range(GROUPS):
                for n in range(GT):
                    m = v.bn_aggr(mvl[:, g, n, :], stl[:, g, n, :])
            m.then_inc(S("last_mv"), 1)
            v.wait_ge(S("last_mv"), 1)
            v.tensor_scalar(vel[:, :], mvl[:, :, :, 1].rearrange("p g t -> p (g t)"), EPS, None, ALU.add)\
                .then_inc(S("last_ve"), 1)
            v.wait_ge(S("last_rs"), 1)
            for g in range(GROUPS):
                for n in range(GT):
                    m = v.tensor_scalar(xl[:, g, n, :], full(g)[:, n * PARTS:(n + 1) * PARTS], mvl[:, g, n, 0:1],
                                        rsl[:, g * GT + n:g * GT + n + 1], ALU.subtract, ALU.mult)
                m.then_inc(S("last_n"), 1)
                v.wait_ge(S("last_n"), g + 1)
                v.tensor_tensor(xl[:, g, :, :], xl[:, g, :, :],
                                x_all[:, 2 * g:2 * g + 2, :, :].rearrange("p b t d -> p (b t) d"), ALU.add)\
                    .then_inc(S("last_done"), 1)

        @block.gpsimd
        def _(g):
            for name in ("a_sum a_stack a_v a_rs2 b_r b_add b_qkr f_rs").split():
                g.sem_inc(S(name), ONE)
            g.wait_ge(S("half"), 1)

            def a_rs(k, b0, b1):
                g.wait_ge(S("a_ve"), k + 1)
                w = (b1 - b0) * TILES
                g.tensor_tensor(rs1[:, b0:b1, :].rearrange("p b t -> p (b t)"),
                                ve[:, b0:b1, :].rearrange("p b t -> p (b t)"), minus_half[:, 0:w], ALU.pow)\
                    .then_inc(S("a_rs"), 1)

            def a_split(b):
                own.begin(b)
                g.wait_ge(S("a_rope"), ONE + b + 1)
                g.wait_ge(S("a_st"), ONE + b * NS)
                for n in range(TILES):
                    g.tensor_tensor(rest[:, n, :, :], rope_c[:, n, :, :], rope_s[:, n, :, :], ALU.add)\
                        .then_inc(S("a_sum"), 1)
                    g.wait_ge(S("a_sum"), ONE + b * TILES + n + 1)
                    plain(g)
                    for i in range(SPLIT):
                        for h0, h1, dst in ((0, A_HEADS, stack[:, n, 0:A_HEADS, i, :, :]),
                                            (A_HEADS, A_QK, stack[:, n, A_HEADS:A_QK, :, i, :])):
                            m = g.tensor_copy(dst, rest[:, n, h0:h1, :].unsqueeze(2)
                                              .broadcast_to([PARTS, h1 - h0, SPLIT, A_D]))
                        if i == SPLIT - 1:
                            m.then_inc(S("a_stack"), 1)
                            break
                        own.step(m)
                        g.tensor_tensor(rest[:, n, 0:A_HEADS, :], rest[:, n, 0:A_HEADS, :],
                                        stack[:, n, 0:A_HEADS, i, 0, :], ALU.subtract)
                        own.step(g.tensor_tensor(rest[:, n, A_HEADS:A_QK, :], rest[:, n, A_HEADS:A_QK, :],
                                                 stack[:, n, A_HEADS:A_QK, 0, i, :], ALU.subtract))
                        plain(g)
                own.end()

            def a_v(b, par, first=False):
                g.wait_ge(S("a_rope"), ONE + b + 1)
                if not first:
                    g.wait_ge(S("a_pv"), ONE + (b - 1) * A_KV)
                plain(g)
                g.tensor_copy(v_a[par][:, :, :, 0:A_D], v_new[:, :, :].rearrange("p t (h d) -> p t h d", d=A_D))\
                    .then_inc(S("a_v"), 1)

            def a_rs2(b):
                for k in range(2):
                    g.wait_ge(S("a_ve2"), ONE + 2 * b + k + 1)
                    g.tensor_tensor(rs2[:, :], ve2[:, :], minus_half[:, 0:TILES], ALU.pow).then_inc(S("a_rs2"), 1)

            def a_step(b, par, one, two):
                if one:
                    a_v(b + 1, 1 - par)
                if two:
                    a_split(b + 2)
                a_rs2(b)

            own = Own(g, S("pool_a"), TILES * 2 * (SPLIT - 1))
            g.wait_ge(S("a_rows"), 1)
            a_rs(0, 0, 1)
            a_rs(1, 1, BATCH)
            a_v(0, 0, first=True)
            a_split(0)
            a_split(1)
            with g.Fori(0, (BATCH - 2) // 2) as j:
                a_step(2 * j, 0, True, True)
                a_step(2 * j + 1, 1, True, True)
            a_step(BATCH - 2, 0, True, False)
            a_step(BATCH - 1, 1, False, False)

            def b_norm(i, n):
                g.wait_ge(S("b_n2"), ONE + 2 * i + n + 1)
                g.wait_ge(S("b_r8"), ONE + i)
                g.tensor_tensor(r_qk[:, n, :], ss[:, n, :], minus_half[:, :], ALU.pow).then_inc(S("b_r"), 1)
                g.wait_ge(S("b_rot"), ONE + 2 * i + n + 1)
                g.tensor_tensor(rc[:, n, :, :], rc[:, n, :, :], rs[:, n, :, :], ALU.add).then_inc(S("b_add"), 1)
                g.wait_ge(S("b_add"), ONE + 2 * i + n + 1)
                k = rc[:, n, 1, :].rearrange("p (h d) -> p h d", d=HD)
                g.tensor_tensor(k, k, r_qk[:, n, HEADS:2 * HEADS].unsqueeze(2).broadcast_to([PARTS, HEADS, HD]),
                                ALU.mult).then_inc(S("b_qkr"), 1)

            with g.Fori(0, DEPTH) as l:
                with g.Fori(0, BATCH) as b:
                    for n in range(TILES):
                        b_norm(l * BATCH + b, n)
                with g.Fori(0, GROUPS) as q:
                    i = l * GROUPS + q
                    g.wait_ge(S("f_ve"), ONE + i + 1)
                    g.tensor_tensor(rsf[:, :], vef[:, :], minus_half[:, 0:GT], ALU.pow).then_inc(S("f_rs"), 1)

            g.wait_ge(S("last_ve"), 1)
            g.tensor_tensor(rsl[:, :], vel[:, :], minus_half[:, :], ALU.pow).then_inc(S("last_rs"), 1)


_INS = ["L0_attn_x", "L0_attn_Wqa", "L0_attn_Wqb", "L0_attn_Wkva", "L0_attn_Wkvb", "L0_attn_Wout", "L0_attn_bout",
        "L0_ffn_wqkv", "L0_ffn_q_scale", "L0_ffn_k_scale", "L0_ffn_wo", "L0_ffn_ln_g", "L0_ffn_ln_b", "L0_ffn_w1",
        "L0_ffn_b1", "L0_ffn_w2", "L0_ffn_b2"]


def kernel(**inputs):
    import numpy as _np
    import concourse.bacc as _bacc
    from concourse import mybir as _mybir
    from concourse.bass_utils import run_bass_kernel_spmd as _run

    nc = _bacc.Bacc("TRN2", target_bir_lowering=False, num_devices=1)
    arrays, args = {}, {}
    for name in _INS:
        x = _np.ascontiguousarray(inputs[name])
        arrays[f"in_{name}_dram"] = x
        args[name] = nc.dram_tensor(f"in_{name}_dram", x.shape, _mybir.dt.from_np(x.dtype), kind="ExternalInput").ap()
    arrays["consts_dram"] = shape_constants()
    args["consts"] = nc.dram_tensor("consts_dram", arrays["consts_dram"].shape, _mybir.dt.float32,
                                    kind="ExternalInput").ap()
    out = nc.dram_tensor("out_dram", (BATCH, SEQ, DIM), _mybir.dt.float32, kind="ExternalOutput").ap()
    build_program(nc, args, out)
    r = _run(nc, [arrays], core_ids=[0])
    return r.results[0]["out_dram"]
```

```python
import numpy as np
import concourse.bass as bass
from concourse import mybir
from contextlib import ExitStack

FP32 = mybir.dt.float32
BF16 = mybir.dt.bfloat16
ALU = mybir.AluOpType
ACT = mybir.ActivationFunctionType
AX = mybir.AxisListType

PARTS = 128
BATCH, SEQ, DIM = 8, 256, 128
TILES = SEQ // PARTS

A_HEADS, A_KV = 16, 4
A_D = DIM // A_HEADS
A_GROUP = A_HEADS // A_KV
A_QL, A_KVL = 64, 32
A_QK = A_HEADS + A_KV
A_SCALE = A_D ** -0.5
SPLIT = 3
A_STACK = SPLIT * SPLIT * A_D
A_COLS = PARTS // A_GROUP

DEPTH, HEADS, HD = 2, 8, 64
WINDOW = 64
INNER = HEADS * HD
PAIRS = HEADS // 2
QK_SCALE = 8.0
HID = int(DIM * 4 * 2 / 3)
HCH = [(c, min(PARTS, HID - c)) for c in range(0, HID, PARTS)]
NCH = len(HCH)
GROUPS = BATCH // 2
GT = 2 * TILES
EPS = 1e-5
TINY = 1e-24
NEG = -1e30

C_ID = 0
C_MA = C_ID + PARTS
C_MB0 = C_MA + PARTS
C_MB1 = C_MB0 + PARTS
B1K = SEQ - WINDOW
C_RA = C_MB1 + B1K
C_RB = C_RA + 2 * TILES * A_D
C_END = C_RB + 2 * TILES * 2 * HD


def shape_constants():
    f = np.float32
    c = np.zeros((PARTS, C_END), f)
    q = np.arange(PARTS)[:, None]
    k = np.arange(PARTS)[None, :]
    c[:, C_ID:C_MA] = np.eye(PARTS)
    c[:, C_MA:C_MB0] = np.where(k > q, NEG, 0)
    c[:, C_MB0:C_MB1] = np.where((k > q) | (q > k + WINDOW), NEG, 0)
    q1, k1 = q + PARTS, np.arange(B1K)[None, :] + WINDOW
    c[:, C_MB1:C_RA] = np.where((k1 > q1) | (q1 > k1 + WINDOW), NEG, 0)
    t = np.arange(SEQ, dtype=f)

    inv = f(1.0) / f(10000.0) ** (np.arange(0, A_D, 2, dtype=f) / f(A_D))
    ang = np.outer(t, inv).astype(f)
    cos, sin = np.repeat(np.cos(ang), 2, 1), np.repeat(np.sin(ang), 2, 1)
    sin[:, 0::2] *= -1
    for n, tab in enumerate((cos, sin)):
        w = TILES * A_D
        c[:, C_RA + n * w:C_RA + (n + 1) * w] = tab.reshape(TILES, PARTS, A_D).transpose(1, 0, 2).reshape(PARTS, w)

    half = np.arange(0, HD, 2, dtype=f)
    inv = f(1.0) / f(10000.0) ** (half / f(HD))
    ang = t[:, None] * inv[None, :]
    cos, sin = np.cos(ang), np.sin(ang)
    base = (half + f(0.4 * HD)) / f(1.4 * HD)
    scale = base[None, :] ** ((t - f(SEQ // 2)) / f(WINDOW // 2))[:, None]
    for n, (lo, hi) in enumerate(((cos, cos), (-sin, sin))):
        tab = np.concatenate([lo, hi], 1)
        both = np.stack([tab * np.tile(scale, 2), tab / np.tile(scale, 2)], 1).astype(f)
        w = TILES * 2 * HD
        c[:, C_RB + n * w:C_RB + (n + 1) * w] = both.reshape(TILES, PARTS, 2, HD).transpose(1, 0, 2, 3).reshape(PARTS, w)
    return c


ONE = 1


class Own:

    def __init__(self, eng, sem, per):
        self.eng, self.sem, self.per, self.n, self.base = eng, sem, per, 0, 0

    def begin(self, index):
        self.base, self.n = index * self.per, 0

    def end(self):
        assert self.n == self.per, (self.sem.name, self.n, self.per)

    def step(self, ins):
        self.n += 1
        ins.then_inc(self.sem, 1)
        self.eng.wait_ge(self.sem, self.base + self.n)


def build_program(nc, a, out):
    ctx = ExitStack()
    with ctx:
        def sb(name, shape, dt=FP32):
            return ctx.enter_context(nc.sbuf_tensor(name, shape, dt))

        def pb(name, shape, dt=FP32):
            return ctx.enter_context(nc.psum_tensor(name, shape, dt))

        def sem(name):
            return ctx.enter_context(nc.semaphore(name))

        const = sb("const", [PARTS, C_END])
        ident = const[:, C_ID:C_MA]
        cos_a = const[:, C_RA:C_RA + TILES * A_D].rearrange("p (t d) -> p t d", t=TILES)
        sin_a = const[:, C_RA + TILES * A_D:C_RB].rearrange("p (t d) -> p t d", t=TILES)
        rot_raw = const[:, C_RB:C_END].rearrange("p (n t c d) -> p n t c d", n=2, t=TILES, c=2)
        ident_h = sb("ident_h", [PARTS, PARTS], BF16)
        ident_4 = sb("ident_4", [PARTS, 4, PARTS], BF16)
        mask_a = sb("mask_a", [PARTS, 4, PARTS], BF16)
        mask_b0 = sb("mask_b0", [PARTS, 4, PARTS], BF16)
        mask_b1 = sb("mask_b1", [PARTS, 2, B1K], BF16)
        minus_half = sb("minus_half", [PARTS, 16])

        x_all = sb("x_all", [PARTS, BATCH, TILES, DIM])
        xT = sb("xT", [PARTS, BATCH, SEQ])

        wqa = sb("wqa", [PARTS, A_QL])
        wkva = sb("wkva", [PARTS, A_KVL])
        wqb = sb("wqb", [A_QL, DIM])
        wkvb = sb("wkvb", [A_KVL, 2 * A_KV * A_D])
        wqaT = sb("wqaT", [A_QL, PARTS])
        wkvaT = sb("wkvaT", [A_KVL, PARTS])
        A_W = DIM + 2 * A_KV * A_D
        w_a = sb("w_a", [PARTS, A_W])
        wout = sb("wout", [PARTS, DIM])
        bout = sb("bout", [PARTS, DIM])

        st = sb("st", [PARTS, BATCH, TILES, 6])
        mv = sb("mv", [PARTS, BATCH, TILES, 2])
        ve = sb("ve", [PARTS, BATCH, TILES])
        rs1 = sb("rs1", [PARTS, BATCH, TILES])
        xn = sb("xn", [PARTS, TILES, DIM])
        xnT = sb("xnT", [PARTS, SEQ])
        rope_c = sb("rope_c", [PARTS, TILES, A_QK, A_D])
        rope_s = sb("rope_s", [PARTS, TILES, A_QK, A_D])
        v_new = sb("v_new", [PARTS, TILES, A_KV * A_D])
        v_a = [sb(f"v_a{i}", [PARTS, TILES, A_KV, A_COLS]) for i in range(2)]
        rest = sb("rest", [PARTS, TILES, A_QK, A_D])
        parts = sb("parts", [PARTS, TILES, A_QK, SPLIT, A_D], BF16)
        stack = sb("stack", [PARTS, TILES, A_QK, SPLIT, SPLIT, A_D], BF16)
        qkT_a = [sb(f"qkT_a{i}", [A_STACK + SPLIT, A_QK, SEQ], BF16) for i in range(2)]
        mx_a = sb("mx_a", [PARTS, TILES, A_HEADS])
        m_left = sb("m_left", [PARTS, TILES, A_HEADS])
        m_part = sb("m_part", [PARTS, TILES, SPLIT, A_HEADS], BF16)
        mT = sb("mT", [SPLIT * A_HEADS, SEQ], BF16)
        pT_k0 = sb("pT_k0", [PARTS, A_HEADS, SEQ])
        pT_k1 = sb("pT_k1", [PARTS, A_HEADS, PARTS])
        ovT = sb("ovT", [PARTS, A_KV, SEQ])
        inv_a = sb("inv_a", [PARTS, TILES, A_HEADS])
        o_a = sb("o_a", [PARTS, TILES, DIM])
        oT_a = sb("oT_a", [PARTS, SEQ])
        y_a = sb("y_a", [PARTS, TILES, DIM])
        z_a = sb("z_a", [PARTS, TILES, DIM])
        st2 = sb("st2", [PARTS, TILES, 6])
        mv2 = sb("mv2", [PARTS, TILES, 2])
        ve2 = sb("ve2", [PARTS, TILES])
        rs2 = sb("rs2", [PARTS, TILES])

        wqkv = sb("wqkv", [PARTS, 3 * INNER])
        wo = sb("wo", [PARTS, PAIRS, DIM])
        scales = sb("scales", [PARTS, 2, HD])
        tab_c = sb("tab_c", [PARTS, TILES, 2, HD])
        tab_s = sb("tab_s", [PARTS, TILES, 2, HD])
        hT = sb("hT", [PARTS, SEQ])
        sq = sb("sq", [PARTS, TILES, 2, INNER])
        ss = sb("ss", [PARTS, TILES, 2 * HEADS])
        r_qk = sb("r_qk", [PARTS, TILES, 2 * HEADS])
        r_q8 = [sb(f"r_q8{i}", [PARTS, TILES, HEADS]) for i in range(2)]
        rc = sb("rc", [PARTS, TILES, 2, INNER])
        rs = sb("rs", [PARTS, TILES, 2, INNER])
        qkT = [sb(f"qkT{i}", [PARTS, 2, PAIRS, SEQ]) for i in range(2)]
        v_b = [sb(f"v_b{i}", [PARTS, TILES, INNER]) for i in range(2)]
        p_b0 = [sb(f"p_b0{i}", [PARTS, HEADS, PARTS]) for i in range(2)]
        p_b1 = [sb(f"p_b1{i}", [PARTS, HEADS, SEQ]) for i in range(2)]
        mx_b = [sb(f"mx_b{i}", [PARTS, TILES, HEADS]) for i in range(2)]
        nm_b = [sb(f"nm_b{i}", [PARTS, TILES, HEADS]) for i in range(2)]
        sum_b = [sb(f"sum_b{i}", [PARTS, TILES, HEADS]) for i in range(2)]
        inv_b = [sb(f"inv_b{i}", [PARTS, TILES, HEADS]) for i in range(2)]
        pT_b = sb("pT_b", [PARTS, 4, PARTS + SEQ])
        oT_b = sb("oT_b", [PARTS, PAIRS, SEQ])

        w1 = sb("w1", [PARTS, 2 * HID])
        w2 = sb("w2", [PARTS, NCH, DIM])
        b1 = sb("b1", [PARTS, 2, NCH])
        b2 = sb("b2", [PARTS, 1])
        ln_g = sb("ln_g", [PARTS, 1])
        ln_b = sb("ln_b", [PARTS, 1])
        hTf = sb("hTf", [PARTS, 2, SEQ])
        stf = sb("stf", [PARTS, GT, 6])
        mvf = sb("mvf", [PARTS, GT, 2])
        vef = sb("vef", [PARTS, GT])
        rsf = sb("rsf", [PARTS, GT])
        yf = sb("yf", [PARTS, GT, DIM])
        yfT = sb("yfT", [PARTS, GT * PARTS])
        n_heads = NCH * GT * PARTS // SEQ
        gate, act = (pT_k0[:, k * n_heads:(k + 1) * n_heads, :].rearrange("p h q -> p (h q)")
                     .rearrange("p (c n) -> p c n", c=NCH) for k in range(2))
        stl = sb("stl", [PARTS, GROUPS, GT, 6])
        mvl = sb("mvl", [PARTS, GROUPS, GT, 2])
        vel = sb("vel", [PARTS, GROUPS, GT])
        rsl = sb("rsl", [PARTS, GROUPS, GT])
        shl = sb("shl", [PARTS, GROUPS, GT])
        xl = p_b1[0][:, :, :].rearrange("p h s -> p (h s)").rearrange("p (g t d) -> p g t d", g=GROUPS, t=GT)

        bank = [pb(f"bank{i}", [PARTS, 1024]) for i in range(4)]

        ld_ident, ld_c, ld_x0, ld_x = sem("ld_ident"), sem("ld_c"), sem("ld_x0"), sem("ld_x")
        ld_proj, ld_out = sem("ld_proj"), sem("ld_out")
        ld_att, ld_ffn, ld_m = sem("ld_att"), sem("ld_ffn"), sem("ld_m")
        st_out = sem("st_out")
        names = {}

        def S(name):
            if name not in names:
                names[name] = sem(name)
            return names[name]

        block = ctx.enter_context(nc.Block())

        def plain(eng):
            eng.sem_inc(S("plain"), 1)

        def full(i):
            return bank[i // 2][:, (i % 2) * 512:(i % 2) * 512 + 512]

        USES_Q = [(0, h, 4) for h in range(0, A_HEADS, 4)] + [(1, h, 2) for h in range(0, A_HEADS, 2)]
        NQ = len(USES_Q)
        USES_K = [u for h in range(0, A_HEADS, A_GROUP) for u in ((0, h, 2), (0, h + 2, 2), (1, h, 4))]
        NK = len(USES_K)
        STACKS = [(n, h0, min(8, A_QK - h0)) for h0 in range(0, A_QK, 8) for n in range(TILES)]
        NS = len(STACKS)
        M_LOADS = 16 * SPLIT

        USES_B = [(0, (0, 2, 4, 6)), (0, (1, 3, 5, 7)), (1, (0, 2)), (1, (1, 3)), (1, (4, 6)), (1, (5, 7))]
        NUB = len(USES_B)
        sc_b = [full(2), full(3), full(4)]
        pj = bank[0]
        pt_b = [full(5), full(6)]
        ov_b = full(7)

        def keys_b(qt):
            return PARTS if qt == 0 else B1K

        def p_slice_b(par, qt, h):
            return p_b0[par][:, h, :] if qt == 0 else p_b1[par][:, h, WINDOW:SEQ]

        def done(x, per, first):
            return per * x if first else per * (x - 1)

        lnf = [full(0), full(1)]
        up = [[full(2), full(3)], [full(4), full(5)]]
        down = full(6)

        @block.sync
        def _(e):
            e.dma_start(ident, a["consts"][:, C_ID:C_MA]).then_inc(ld_ident, 16)
            e.dma_start(x_all[:, 0:2, :, :], a["L0_attn_x"][0:2].rearrange("b (t p) d -> p b t d", p=PARTS))\
                .then_inc(ld_x0, 16)
            e.dma_start(wqa[:, :], a["L0_attn_Wqa"]).then_inc(ld_proj, 16)
            e.dma_start(wkva[:, :], a["L0_attn_Wkva"]).then_inc(ld_proj, 16)
            e.dma_start(wqb[:, :], a["L0_attn_Wqb"]).then_inc(ld_proj, 16)
            e.dma_start(wkvb[:, :], a["L0_attn_Wkvb"]).then_inc(ld_proj, 16)
            e.dma_start(const[:, C_MA:C_END], a["consts"][:, C_MA:C_END]).then_inc(ld_c, 16)
            e.dma_start(x_all[:, 2:BATCH, :, :],
                        a["L0_attn_x"][2:BATCH].rearrange("b (t p) d -> p b t d", p=PARTS)).then_inc(ld_x, 16)
            e.dma_start(wout[:, :], a["L0_attn_Wout"]).then_inc(ld_out, 16)
            e.dma_start(bout[:, :], a["L0_attn_bout"].unsqueeze(0).broadcast_to([PARTS, DIM])).then_inc(ld_out, 16)

            def load_layer(l, first=False):
                one = bass.ds(l, 1)
                if not first:
                    e.wait_ge(S("b_y"), ONE + l * BATCH)
                    plain(e)
                e.dma_start(wqkv[:, :], a["L0_ffn_wqkv"][one, :, :].rearrange("o p n -> p (o n)")).then_inc(ld_att, 16)
                e.dma_start(wo[:, :, :], a["L0_ffn_wo"][one, :, :].rearrange("o (c p) n -> p (o c) n", p=PARTS)).then_inc(ld_att, 16)
                e.dma_start(scales[:, 0, :], a["L0_ffn_q_scale"][one, :].broadcast_to([PARTS, HD])).then_inc(ld_att, 16)
                e.dma_start(scales[:, 1, :], a["L0_ffn_k_scale"][one, :].broadcast_to([PARTS, HD])).then_inc(ld_att, 16)
                if not first:
                    e.wait_ge(S("f_x"), ONE + l * GROUPS)
                    plain(e)
                e.dma_start(w1[:, :], a["L0_ffn_w1"][one, :, :].rearrange("o p n -> p (o n)")).then_inc(ld_ffn, 16)
                w2l = a["L0_ffn_w2"][one, :, :]
                b1l = a["L0_ffn_b1"][one, :]
                for c, (h0, n) in enumerate(HCH):
                    e.dma_start(w2[0:n, c, :], w2l[:, h0:h0 + n, :].rearrange("o p n -> (o p) n")).then_inc(ld_ffn, 16)
                    for half in range(2):
                        col = half * HID + h0
                        e.dma_start(b1[0:n, half, c:c + 1], b1l[:, col:col + n].rearrange("o p -> p o")).then_inc(ld_ffn, 16)
                e.dma_start(b2[:, :], a["L0_ffn_b2"][one, :].rearrange("o p -> p o")).then_inc(ld_ffn, 16)
                e.dma_start(ln_g[:, :], a["L0_ffn_ln_g"][one, :].rearrange("o p -> p o")).then_inc(ld_ffn, 16)
                e.dma_start(ln_b[:, :], a["L0_ffn_ln_b"][one, :].rearrange("o p -> p o")).then_inc(ld_ffn, 16)

            load_layer(0, first=True)
            with e.Fori(0, BATCH // 2) as j:
                for par in range(2):
                    e.wait_ge(S("a_mT_out"), ONE + 2 * j + par + 1)
                    plain(e)
                    for i in range(SPLIT):
                        e.dma_start(qkT_a[par][A_STACK + i:A_STACK + i + 1, 0:A_HEADS, :],
                                    mT[i * A_HEADS:(i + 1) * A_HEADS, :]).then_inc(ld_m, 16)
            with e.Fori(1, DEPTH) as l:
                load_layer(l)
            with e.Fori(0, GROUPS) as g:
                e.wait_ge(S("last_done"), g + 1)
                e.dma_start(out[bass.ds(g * 2, 2), :, :].rearrange("b (t p) d -> p (b t) d", p=PARTS),
                            xl[:, bass.ds(g, 1), :, :].rearrange("p o t d -> p (o t) d")).then_inc(st_out, 16)
            e.wait_ge(st_out, 16 * GROUPS)

        FFN_LOADS = 1 + 3 * NCH + 3

        @block.tensor
        def _(t):
            for name in ("a_xnT a_qkv a_st a_sc a_mT a_p2 a_pv a_back a_oT a_y a_h0T b_qk b_vp b_trT b_sc b_pT "
                         "b_pv b_y f_h f_ty f_up f_down").split():
                t.sem_inc(S(name), ONE)
            t.wait_ge(ld_ident, 16)
            t.wait_ge(ld_proj, 16 * 4)
            t.transpose(full(0)[0:A_QL, 0:PARTS], wqa[:, :], ident)
            t.transpose(full(0)[0:A_KVL, PARTS:2 * PARTS], wkva[:, :], ident).then_inc(S("w_t"), 1)
            t.wait_ge(S("w_copied"), 2)
            t.matmul(full(1)[:, 0:DIM], wqaT[:, :], wqb[:, :], start=True, stop=True)
            t.matmul(full(1)[:, DIM:A_W], wkvaT[:, :], wkvb[:, :], start=True, stop=True).then_inc(S("w_prod"), 1)

            def a_norm_t(b, dst=full(7), fresh=False):
                t.wait_ge(S("a_xn"), ONE + b + 1)
                if not fresh:
                    t.wait_ge(S("a_st_out"), ONE + b * NS)
                for n in range(TILES):
                    m = t.transpose(dst[:, n * PARTS:(n + 1) * PARTS], xn[:, n, :], ident)
                m.then_inc(S("a_xnT"), 1)

            def a_proj(b, dst=full(7)):
                t.wait_ge(S("a_xnT_out"), ONE + b + 1)
                for n in range(TILES):
                    m = t.matmul(dst[:, n * A_W:(n + 1) * A_W], xnT[:, n * PARTS:(n + 1) * PARTS], w_a[:, :],
                                 start=True, stop=True)
                m.then_inc(S("a_qkv"), 1)

            def a_stack_t(b, k):
                n, h0, hs = STACKS[k]
                t.wait_ge(S("a_stack"), ONE + b * TILES + n + 1)
                if k > 1:
                    t.wait_ge(S("a_st_out"), ONE + b * NS + k - 1)
                elif k == 0:
                    t.wait_ge(S("a_st_out"), ONE + b * NS)
                dst = full(6 + k % 2).bitcast(BF16)
                for h in range(h0, h0 + hs):
                    m = t.transpose(dst[0:A_STACK, (h - h0) * PARTS:(h - h0 + 1) * PARTS],
                                    stack[:, n, h, :, :, :].rearrange("p i j d -> p (i j d)"), ident_h[:, :])
                m.then_inc(S("a_st"), 1)

            def a_scores_q(b, par, u, prev=False):
                qt, h0, nh = USES_Q[u]
                nk = (qt + 1) * PARTS
                if u == 0:
                    t.wait_ge(S("a_st_out"), ONE + b * NS + NS)
                    t.wait_ge(S("a_mT_out"), ONE + b)
                elif u == 1 and prev:
                    t.wait_ge(S("a_h0T_out"), ONE + b - 2)
                if u >= 2:
                    t.wait_ge(S("a_mx"), ONE + b * NQ + u - 1)
                else:
                    t.wait_ge(S("a_mx"), ONE + b * NQ)
                dst = full(u % 2)
                for i in range(nh):
                    h = h0 + i
                    t.matmul(dst[:, i * nk:(i + 1) * nk], qkT_a[par][0:A_STACK, h, qt * PARTS:(qt + 1) * PARTS],
                             qkT_a[par][0:A_STACK, A_HEADS + h // A_GROUP, 0:nk], start=True, stop=False,
                             skip_group_check=True)
                t.matmul(dst.rearrange("p (h k) -> p h k", h=nh)[:, :, nk - PARTS:nk], ident_h[:, :],
                         mask_a[:, 0:nh, :], start=False, stop=True, skip_group_check=True).then_inc(S("a_sc"), 1)

            def a_turn_m(b):
                t.wait_ge(S("a_mp"), ONE + b + 1)
                plain(t)
                dst = full(0).bitcast(BF16)
                for n in range(TILES):
                    m = t.transpose(dst[0:SPLIT * A_HEADS, n * PARTS:(n + 1) * PARTS],
                                    m_part[:, n, :, :].rearrange("p i h -> p (i h)"), ident_h[:, :])
                m.then_inc(S("a_mT"), 1)

            def a_scores_k(b, par, u):
                kt, h0, nh = USES_K[u]
                q0 = kt * PARTS
                if u == 0:
                    t.wait_ge(ld_m, b * M_LOADS + M_LOADS)
                if u >= 2:
                    t.wait_ge(S("a_exp"), ONE + b * NK + u - 1)
                else:
                    t.wait_ge(S("a_exp"), ONE + b * NK)
                dst = full(2 + u % 2)
                t.matmul(dst, qkT_a[par][:, A_HEADS + h0 // A_GROUP, kt * PARTS:(kt + 1) * PARTS],
                         qkT_a[par][:, h0:h0 + nh, q0:SEQ], start=True, stop=False, skip_group_check=True)
                t.matmul(dst.rearrange("p (h q) -> p h q", h=nh)[:, :, 0:PARTS], mask_a[:, 0, :],
                         ident_4[:, 0:nh, :], start=False, stop=True, skip_group_check=True).then_inc(S("a_p2"), 1)

            def a_values(b, par, g):
                t.wait_ge(S("a_exp"), ONE + b * NK + 3 * g + 3)
                if g == 0:
                    t.wait_ge(S("a_v"), ONE + b + 1)
                    t.wait_ge(S("a_yin"), ONE + b)
                dst = full(4 + g // 2)[:, (g % 2) * SEQ:(g % 2 + 1) * SEQ]
                for kt in range(TILES):
                    for i in range(A_GROUP):
                        h = g * A_GROUP + i
                        src = pT_k0[:, h, :] if kt == 0 else pT_k1[:, h, :]
                        m = t.matmul(dst[i * A_COLS:(i + 1) * A_COLS, kt * PARTS:SEQ], v_a[par][:, kt, g, :], src,
                                     start=(kt == 0), stop=(kt == 1), tile_position=(0, i * A_COLS),
                                     skip_group_check=True)
                m.then_inc(S("a_pv"), 1)

            def a_turn_back(b):
                t.wait_ge(S("a_ov"), ONE + b * 2 + 2)
                for n in range(TILES):
                    for g in range(A_KV):
                        m = t.transpose(full(4 + n)[:, g * PARTS:(g + 1) * PARTS],
                                        ovT[:, g, n * PARTS:(n + 1) * PARTS], ident)
                m.then_inc(S("a_back"), 1)

            def a_turn_o(b):
                t.wait_ge(S("a_o"), ONE + b + 1)
                for n in range(TILES):
                    m = t.transpose(full(4)[:, n * PARTS:(n + 1) * PARTS], o_a[:, n, :], ident)
                m.then_inc(S("a_oT"), 1)

            def a_out(b):
                t.wait_ge(S("a_oT_out"), ONE + b + 1)
                for n in range(TILES):
                    m = t.matmul(full(4)[:, n * DIM:(n + 1) * DIM], oT_a[:, n * PARTS:(n + 1) * PARTS], wout[:, :],
                                 start=True, stop=True)
                m.then_inc(S("a_y"), 1)

            def a_h0(b):
                t.wait_ge(S("a_h0"), ONE + b + 1)
                for n in range(TILES):
                    m = t.transpose(full(1)[:, n * PARTS:(n + 1) * PARTS], z_a[:, n, :], ident)
                m.then_inc(S("a_h0T"), 1)

            def a_step(b, par, prev, one, two):
                nxt = 1 - par
                if two:
                    a_norm_t(b + 2)
                for u in range(NK):
                    if one:
                        a_scores_q(b + 1, nxt, u, prev)
                    if two and u == 0:
                        a_proj(b + 2)
                    a_scores_k(b, par, u)
                    if u % 3 == 2 and u > 2:
                        a_values(b, par, u // 3 - 1)
                    if two and u in (9, 10):
                        a_stack_t(b + 2, u - 9)
                if two:
                    a_stack_t(b + 2, 2)
                a_values(b, par, A_KV - 1)
                if one:
                    a_turn_m(b + 1)
                if two:
                    a_stack_t(b + 2, 3)
                if prev:
                    a_h0(b - 1)
                if two:
                    a_stack_t(b + 2, 4)
                a_turn_back(b)
                if two:
                    a_stack_t(b + 2, 5)
                a_turn_o(b)
                a_out(b)

            t.wait_ge(S("w_ready"), 2)
            a_norm_t(0, fresh=True)
            a_proj(0)
            a_norm_t(1, full(5), fresh=True)
            a_proj(1, full(5))
            t.wait_ge(S("ident_cast"), 1)
            for k in range(NS):
                a_stack_t(0, k)
            t.wait_ge(S("mask_cast"), 1)
            for u in range(NQ):
                a_scores_q(0, 0, u)
                if u % 2:
                    a_stack_t(1, u // 2)
            a_turn_m(0)
            t.wait_ge(S("a_ones"), 1)
            t.wait_ge(ld_out, 16 * 2)
            a_step(0, 0, False, True, True)
            with t.Fori(0, (BATCH - 4) // 2) as j:
                a_step(2 * j + 1, 1, True, True, True)
                a_step(2 * j + 2, 0, True, True, True)
            a_step(BATCH - 3, 1, True, True, True)
            a_step(BATCH - 2, 0, True, True, False)
            a_step(BATCH - 1, 1, True, False, False)
            a_h0(BATCH - 1)

            def b_proj(i, n, dst=pj, fresh=False):
                if n == 0:
                    t.wait_ge(S("b_hT"), ONE + 2 * i + 2)
                if n == 0 and not fresh:
                    t.wait_ge(S("b_trT_out"), ONE + 4 * i)
                elif n == 1 and not fresh:
                    t.wait_ge(S("b_rot"), ONE + 2 * i + 1)
                for c in range(2):
                    m = t.matmul(dst[:, c * INNER:(c + 1) * INNER], hT[:, n * PARTS:(n + 1) * PARTS],
                                 wqkv[:, c * INNER:(c + 1) * INNER], start=True, stop=True)
                m.then_inc(S("b_qk"), 1)

            def b_v(i, dst=pj, fresh=False):
                if not fresh:
                    t.wait_ge(S("b_rot"), ONE + 2 * i + 2)
                for n in range(TILES):
                    m = t.matmul(dst[:, n * INNER:(n + 1) * INNER], hT[:, n * PARTS:(n + 1) * PARTS],
                                 wqkv[:, 2 * INNER:3 * INNER], start=True, stop=True)
                    m.then_inc(S("b_vp"), 1)

            def b_turn_qk(i, n):
                t.wait_ge(S("b_qkr"), ONE + 2 * i + n + 1)
                for c in range(2):
                    if n == 0:
                        t.wait_ge(S("b_v"), ONE + 2 * i + c + 1)
                    else:
                        t.wait_ge(S("b_trT_out"), ONE + 4 * i + c + 1)
                    for p in range(PAIRS):
                        m = t.transpose(pj[:, c * 512 + p * PARTS:c * 512 + (p + 1) * PARTS],
                                        rc[:, n, c, p * PARTS:(p + 1) * PARTS], ident)
                    m.then_inc(S("b_trT"), 1)

            def b_scores(x, par, u):
                qt, heads = USES_B[u]
                nk = keys_b(qt)
                if u == 0:
                    t.wait_ge(S("b_trT_out"), ONE + 4 * x + 4)
                t.wait_ge(S("b_exp"), ONE + x * NUB + (u - 2 if u >= 2 else 0))
                dst = sc_b[u % 3]
                mask = mask_b0[:, :, :] if qt == 0 else mask_b1[:, :, :]
                k0, k1 = (0, PARTS) if qt == 0 else (WINDOW, SEQ)
                t.matmul(dst[:, 0:len(heads) * nk], ident_h[:, :], mask.rearrange("p a b -> p (a b)"),
                         start=True, stop=False, skip_group_check=True)
                for n, h in enumerate(heads):
                    r = (h % 2) * HD
                    m = t.matmul(dst[:, n * nk:(n + 1) * nk],
                                 qkT[par][r:r + HD, 0, h // 2, qt * PARTS:(qt + 1) * PARTS],
                                 qkT[par][r:r + HD, 1, h // 2, k0:k1], start=False, stop=True,
                                 skip_group_check=True)
                m.then_inc(S("b_sc"), 1)

            def b_turn_p(i, par, h):
                t.wait_ge(S("b_p"), ONE + i * HEADS + h + 1)
                t.wait_ge(S("b_pT_act" if h % 2 == 0 else "b_pT_dve"), ONE + i * (HEADS // 2) + h // 2)
                dst = pt_b[h % 2]
                t.transpose(dst[:, 0:PARTS], p_b0[par][:, h, :], ident)
                for kb in range(2):
                    m = t.transpose(dst[:, (kb + 1) * PARTS:(kb + 2) * PARTS],
                                    p_b1[par][:, h, kb * PARTS:(kb + 1) * PARTS], ident)
                m.then_inc(S("b_pT"), 1)

            def b_values(i, par, p):
                t.wait_ge(S("b_pT_act"), ONE + i * (HEADS // 2) + p + 1)
                t.wait_ge(S("b_pT_dve"), ONE + i * (HEADS // 2) + p + 1)
                if p == 0:
                    t.wait_ge(S("b_x"), ONE + i)
                if p == 2:
                    t.wait_ge(S("b_o"), ONE + 2 * i + 1)
                for kb in range(2):
                    q0 = kb * PARTS
                    for k in range(2):
                        h = 2 * p + k
                        src = pT_b[:, h % 4, 0:SEQ] if kb == 0 else pT_b[:, h % 4, SEQ:SEQ + PARTS]
                        m = t.matmul(ov_b[k * HD:(k + 1) * HD, (p % 2) * SEQ + q0:(p % 2) * SEQ + SEQ],
                                     v_b[par][:, kb, h * HD:(h + 1) * HD], src, start=(kb == 0), stop=(kb == 1),
                                     skip_group_check=True)
                m.then_inc(S("b_pv"), 1)

            def b_out(i):
                t.wait_ge(S("b_o"), ONE + 2 * i + 2)
                for p in range(PAIRS):
                    m = t.matmul(ov_b[:, 0:SEQ], wo[:, p, :], oT_b[:, p, :], start=(p == 0), stop=(p == PAIRS - 1))
                m.then_inc(S("b_y"), 1)

            def b_step(i, par, one, two, group=None):
                nxt = 1 - par
                last = group is not None
                if one:
                    b_v(i + 1)
                b_turn_p(i, par, 0)
                b_turn_p(i, par, 1)
                if one:
                    b_turn_qk(i + 1, 0)
                if last:
                    f_norm_t(group)
                b_turn_p(i, par, 2)
                b_turn_p(i, par, 3)
                b_values(i, par, 0)
                b_turn_p(i, par, 4)
                b_turn_p(i, par, 5)
                b_values(i, par, 1)
                if one:
                    b_turn_qk(i + 1, 1)
                if last:
                    f_back_t(group)
                b_turn_p(i, par, 6)
                b_turn_p(i, par, 7)
                if one:
                    b_scores(i + 1, nxt, 0)
                    b_scores(i + 1, nxt, 1)
                if two:
                    b_proj(i + 2, 0)
                b_values(i, par, 2)
                if one:
                    b_scores(i + 1, nxt, 2)
                b_values(i, par, 3)
                if last:
                    f_up(group, 0)
                if one:
                    b_scores(i + 1, nxt, 3)
                if two:
                    b_proj(i + 2, 1)
                b_out(i)
                if one:
                    b_scores(i + 1, nxt, 4)
                    b_scores(i + 1, nxt, 5)

            def f_norm_t(i):
                t.wait_ge(S("f_hT"), ONE + i + 1)
                t.wait_ge(S("f_y"), ONE + i)
                for n in range(GT):
                    q0 = (n % TILES) * PARTS
                    m = t.transpose(lnf[0][:, n * PARTS:(n + 1) * PARTS], hTf[:, n // TILES, q0:q0 + PARTS], ident)
                m.then_inc(S("f_h"), 1)

            def f_back_t(i):
                t.wait_ge(S("f_y"), ONE + i + 1)
                t.wait_ge(S("f_yT"), ONE + i)
                for n in range(GT):
                    m = t.transpose(lnf[1][:, n * PARTS:(n + 1) * PARTS], yf[:, n, :], ident)
                m.then_inc(S("f_ty"), 1)

            def f_up(i, c):
                if c == 0:
                    t.wait_ge(S("f_yT"), ONE + i + 1)
                h0, n = HCH[c]
                if c < 2:
                    t.wait_ge(S("f_act"), ONE + i * NCH)
                else:
                    t.wait_ge(S("f_act"), ONE + i * NCH + c - 1)
                for half in range(2):
                    col = (1 - half) * HID + h0
                    m = t.matmul(up[half][c % 2][0:n, :], w1[:, col:col + n], yfT[:, :], start=True, stop=True)
                    m.then_inc(S("f_up"), 1)

            def f_down(i, c):
                h0, n = HCH[c]
                t.wait_ge(S("f_act"), ONE + i * NCH + c + 1)
                if c == 0:
                    t.wait_ge(S("f_x"), ONE + i)
                m = t.matmul(down[:, :], w2[0:n, c, :], act[0:n, c, :], start=(c == 0), stop=(c == NCH - 1))
                if c == NCH - 1:
                    m.then_inc(S("f_down"), 1)

            def f_body(i, more):
                if more:
                    f_norm_t(i + 1)
                f_up(i, 1)
                f_up(i, 2)
                f_down(i, 0)
                if more:
                    f_back_t(i + 1)
                f_down(i, 1)
                f_down(i, 2)
                if more:
                    f_up(i + 1, 0)

            with t.Fori(0, DEPTH) as l:
                i0 = l * BATCH
                g0 = l * GROUPS
                t.wait_ge(ld_att, l * 64 + 64)
                t.wait_ge(S("b_masks"), 1)
                t.wait_ge(S("a_h0T_out"), ONE + BATCH)
                t.wait_ge(S("f_x"), ONE + g0)
                b_proj(i0, 0, bank[0], fresh=True)
                b_proj(i0, 1, bank[1], fresh=True)
                b_v(i0, bank[2], fresh=True)
                b_proj(i0 + 1, 0, bank[3], fresh=True)
                b_turn_qk(i0, 0)
                b_turn_qk(i0, 1)
                for u in range(3):
                    b_scores(i0, 0, u)
                b_proj(i0 + 1, 1)
                for u in range(3, NUB):
                    b_scores(i0, 0, u)
                with t.Fori(0, (BATCH - 2) // 2) as j:
                    b_step(i0 + 2 * j, 0, True, True)
                    b_step(i0 + 2 * j + 1, 1, True, True)
                b_step(i0 + (BATCH - 2), 0, True, False)
                t.wait_ge(ld_ffn, (l + 1) * (16 * FFN_LOADS))
                b_step(i0 + (BATCH - 1), 1, False, False, g0)
                t.wait_ge(S("b_x"), ONE + i0 + BATCH)
                plain(t)
                with t.Fori(0, GROUPS - 1) as g:
                    f_body(g0 + g, True)
                f_body(g0 + (GROUPS - 1), False)

            t.wait_ge(S("f_x"), ONE + DEPTH * GROUPS)
            for g in range(GROUPS):
                for n in range(GT):
                    m = t.transpose(full(g)[:, n * PARTS:(n + 1) * PARTS],
                                    xT[:, 2 * g + n // TILES, (n % TILES) * PARTS:(n % TILES + 1) * PARTS], ident)
                m.then_inc(S("last_t"), 1)

        @block.scalar
        def _(s):
            for name in ("a_xnT_out a_stack a_st_out a_mT_out a_exp a_ov a_oT_out a_h0T_out b_hT b_sq b_v "
                         "b_trT_out b_exp b_pT_act b_o f_gate").split():
                s.sem_inc(S(name), ONE)
            s.wait_ge(S("w_t"), 1)
            s.activation(wqaT[:, :], full(0)[0:A_QL, 0:PARTS], ACT.Copy).then_inc(S("w_copied"), 1)
            s.activation(wkvaT[:, :], full(0)[0:A_KVL, PARTS:2 * PARTS], ACT.Copy).then_inc(S("w_copied"), 1)
            s.wait_ge(S("w_prod"), 1)
            s.activation(w_a[:, 0:DIM], full(1)[:, 0:DIM], ACT.Copy).then_inc(S("w_ready"), 1)
            s.activation(w_a[:, DIM:A_W].rearrange("p (c x) -> p c x", c=2),
                         full(1)[:, DIM:A_W].rearrange("p (x c) -> p c x", c=2), ACT.Copy).then_inc(S("w_ready"), 1)

            def a_xnT(b, src=full(7)):
                s.wait_ge(S("a_xnT"), ONE + b + 1)
                s.wait_ge(S("a_qkv"), ONE + b)
                s.activation(xnT[:, :], src[:, 0:SEQ], ACT.Copy).then_inc(S("a_xnT_out"), 1)

            def a_stack(b, n):
                s.wait_ge(S("a_parts"), ONE + b + 1)
                s.wait_ge(S("a_st"), ONE + b * NS)
                rows = A_HEADS * SPLIT
                s.activation(stack[:, n, 0:A_HEADS, :, :, :].rearrange("p h i j d -> p (h i) j d"),
                             parts[:, n, 0:A_HEADS, :, :].rearrange("p h i d -> p (h i) d").unsqueeze(2)
                             .broadcast_to([PARTS, rows, SPLIT, A_D]), ACT.Copy)
                s.activation(stack[:, n, A_HEADS:A_QK, :, :, :].rearrange("p h i j d -> p h i (j d)"),
                             parts[:, n, A_HEADS:A_QK, :, :].rearrange("p h j d -> p h (j d)").unsqueeze(2)
                             .broadcast_to([PARTS, A_KV, SPLIT, SPLIT * A_D]), ACT.Copy)\
                    .then_inc(S("a_stack"), 1)

            def a_stack_out(b, par, k, first=False):
                n, h0, hs = STACKS[k]
                s.wait_ge(S("a_st"), ONE + b * NS + k + 1)
                if not first:
                    s.wait_ge(S("a_p2"), ONE + (b - 2) * NK + (NK // 2 if h0 == 0 else NK))
                src = full(6 + k % 2).bitcast(BF16)[0:A_STACK, 0:hs * PARTS].rearrange("p (h q) -> p h q", h=hs)
                s.activation(qkT_a[par][0:A_STACK, h0:h0 + hs, n * PARTS:(n + 1) * PARTS], src, ACT.Copy)\
                    .then_inc(S("a_st_out"), 1)

            def a_mT_out(b, first=False):
                s.wait_ge(S("a_mT"), ONE + b + 1)
                if not first:
                    s.wait_ge(ld_m, b * M_LOADS)
                s.activation(mT[:, :], full(0).bitcast(BF16)[0:SPLIT * A_HEADS, 0:SEQ], ACT.Copy)\
                    .then_inc(S("a_mT_out"), 1)

            def a_exp(b, u):
                kt, h0, nh = USES_K[u]
                s.wait_ge(S("a_p2"), ONE + b * NK + u + 1)
                if u == 0:
                    s.wait_ge(S("a_pv"), ONE + b * A_KV)
                dst = pT_k0[:, h0:h0 + nh, :] if kt == 0 else pT_k1[:, h0:h0 + nh, :]
                s.activation(dst.rearrange("p h q -> p (h q)"), full(2 + u % 2), ACT.Exp, scale=A_SCALE)\
                    .then_inc(S("a_exp"), 1)

            def a_ov(b, k):
                s.wait_ge(S("a_pv"), ONE + b * A_KV + 2 * k + 2)
                s.wait_ge(S("a_back"), ONE + b)
                s.activation(ovT[:, 2 * k:2 * k + 2, :].rearrange("p g q -> p (g q)"), full(4 + k), ACT.Copy)\
                    .then_inc(S("a_ov"), 1)

            def a_oT(b):
                s.wait_ge(S("a_oT"), ONE + b + 1)
                s.wait_ge(S("a_y"), ONE + b)
                s.activation(oT_a[:, :], full(4)[:, 0:SEQ], ACT.Copy).then_inc(S("a_oT_out"), 1)

            def a_h0T(b):
                s.wait_ge(S("a_h0T"), ONE + b + 1)
                s.activation(xT[:, bass.ds(b, 1), :].rearrange("p o s -> p (o s)"), full(1)[:, 0:SEQ], ACT.Copy)\
                    .then_inc(S("a_h0T_out"), 1)

            def a_step(b, par, prev, one, two):
                if two:
                    a_xnT(b + 2)
                for u in range(NK):
                    a_exp(b, u)
                    if two and u in (4, 5):
                        a_stack(b + 2, u - 4)
                    if two and u in (9, 10):
                        a_stack_out(b + 2, par, u - 9)
                    if u == 10:
                        a_ov(b, 0)
                if two:
                    a_stack_out(b + 2, par, 2)
                a_ov(b, 1)
                if one:
                    a_mT_out(b + 1)
                if two:
                    a_stack_out(b + 2, par, 3)
                if prev:
                    a_h0T(b - 1)
                if two:
                    a_stack_out(b + 2, par, 4)
                    a_stack_out(b + 2, par, 5)
                a_oT(b)

            a_xnT(0)
            a_xnT(1, full(5))
            for n in range(TILES):
                a_stack(0, n)
            s.wait_ge(S("a_rows"), 1)
            for k in range(NS):
                a_stack_out(0, 0, k, first=True)
            for n in range(TILES):
                a_stack(1, n)
            for k in range(NS):
                a_stack_out(1, 1, k, first=True)
            a_mT_out(0, first=True)
            a_step(0, 0, False, True, True)
            with s.Fori(0, (BATCH - 4) // 2) as j:
                a_step(2 * j + 1, 1, True, True, True)
                a_step(2 * j + 2, 0, True, True, True)
            a_step(BATCH - 3, 1, True, True, True)
            a_step(BATCH - 2, 0, True, True, False)
            a_step(BATCH - 1, 1, True, False, False)
            a_h0T(BATCH - 1)

            def b_hT(i, b):
                s.wait_ge(S("b_vp"), ONE + 2 * i)
                src = xT[:, bass.ds(b, 1), :].rearrange("p o s -> p (o s)")
                s.activation(hT[0:64, :], src[0:64, :], ACT.Copy).then_inc(S("b_hT"), 1)
                s.activation(hT[64:128, 1:SEQ], src[64:128, 0:SEQ - 1], ACT.Copy).then_inc(S("b_hT"), 1)

            def b_sq(i, n, src=pj, back=0):
                s.wait_ge(S("b_qk"), ONE + 2 * i + n + 1)
                s.wait_ge(S("b_ss"), ONE + 2 * i - back)
                s.activation(sq[:, n, :, :].rearrange("p c n -> p (c n)"), src[:, :], ACT.Square).then_inc(S("b_sq"), 1)

            def b_v(x, par, src=pj, first=False):
                for n in range(TILES):
                    s.wait_ge(S("b_vp"), ONE + 2 * x + n + 1)
                    if n == 0:
                        s.wait_ge(S("b_pv"), ONE + done(x, PAIRS, first))
                    s.activation(v_b[par][:, n, :], src[:, n * INNER:(n + 1) * INNER], ACT.Copy).then_inc(S("b_v"), 1)

            def b_qkT(x, par, n, first=False):
                for c in range(2):
                    s.wait_ge(S("b_trT"), ONE + 4 * x + 2 * n + c + 1)
                    if n == 0 and c == 0:
                        s.wait_ge(S("b_sc"), ONE + done(x, NUB, first))
                    s.activation(qkT[par][:, c, :, n * PARTS:(n + 1) * PARTS],
                                 pj[:, c * 512:(c + 1) * 512].rearrange("p (a q) -> p a q", a=PAIRS),
                                 ACT.Copy).then_inc(S("b_trT_out"), 1)

            def b_exp(x, par, u, first=False):
                qt, heads = USES_B[u]
                s.wait_ge(S("b_sc"), ONE + x * NUB + u + 1)
                s.wait_ge(S("b_nm"), ONE + x * NUB + u + 1)
                if u == 0:
                    s.wait_ge(S("b_pT"), ONE + done(x, HEADS, first))
                nk = keys_b(qt)
                for n, h in enumerate(heads):
                    m = s.activation(p_slice_b(par, qt, h), sc_b[u % 3][:, n * nk:(n + 1) * nk], ACT.Exp,
                                     bias=nm_b[par][:, qt, h:h + 1], scale=r_q8[par][:, qt, h:h + 1],
                                     accum_out=sum_b[par][:, qt, h:h + 1])
                m.then_inc(S("b_exp"), 1)

            def b_pT_out(i, h):
                s.wait_ge(S("b_pT"), ONE + i * HEADS + h + 1)
                if h >= 4:
                    s.wait_ge(S("b_pv"), ONE + i * PAIRS + h // 2 - 1)
                s.activation(pT_b[:, h % 4, :], pt_b[h % 2][:, 0:PARTS + SEQ], ACT.Copy).then_inc(S("b_pT_act"), 1)

            def b_o(i, k):
                s.wait_ge(S("b_pv"), ONE + i * PAIRS + 2 * k + 2)
                s.wait_ge(S("b_y"), ONE + i)
                s.activation(oT_b[:, 2 * k:2 * k + 2, :], ov_b[:, :].rearrange("p (a q) -> p a q", a=2), ACT.Copy)\
                    .then_inc(S("b_o"), 1)

            def b_step(i, b, par, one, two):
                nxt = 1 - par
                b_exp(i, par, 4)
                if one:
                    b_v(i + 1, nxt)
                b_pT_out(i, 0)
                b_exp(i, par, 5)
                b_pT_out(i, 2)
                if one:
                    b_qkT(i + 1, nxt, 0)
                b_pT_out(i, 4)
                b_o(i, 0)
                if one:
                    b_qkT(i + 1, nxt, 1)
                if two:
                    b_hT(i + 2, b + 2)
                b_pT_out(i, 6)
                if one:
                    b_exp(i + 1, nxt, 0)
                if two:
                    b_sq(i + 2, 0)
                if one:
                    b_exp(i + 1, nxt, 1)
                b_o(i, 1)
                if one:
                    b_exp(i + 1, nxt, 2)
                if two:
                    b_sq(i + 2, 1)
                if one:
                    b_exp(i + 1, nxt, 3)

            def f_gate(i, c):
                h0, n = HCH[c]
                s.wait_ge(S("f_up"), ONE + i * (2 * NCH) + 2 * c + 1)
                s.wait_ge(S("f_act"), ONE + i * NCH)
                s.activation(gate[0:n, c, :], up[0][c % 2][0:n, :], ACT.Gelu, bias=b1[0:n, 1, c:c + 1])\
                    .then_inc(S("f_gate"), 1)

            def f_body(i):
                for c in range(NCH):
                    f_gate(i, c)

            with s.Fori(0, DEPTH) as l:
                i0 = l * BATCH
                s.wait_ge(S("b_zero"), 1)
                s.wait_ge(S("f_x"), ONE + l * GROUPS)
                s.wait_ge(S("a_h0T_out"), ONE + BATCH)
                b_sq(i0, 0, bank[0])
                b_sq(i0, 1, bank[1])
                b_hT(i0 + 1, 1)
                b_v(i0, 0, bank[2], first=True)
                b_sq(i0 + 1, 0, bank[3], back=1)
                b_qkT(i0, 0, 0, first=True)
                b_qkT(i0, 0, 1, first=True)
                b_exp(i0, 0, 0, first=True)
                b_sq(i0 + 1, 1)
                for u in range(1, 4):
                    b_exp(i0, 0, u)
                with s.Fori(0, (BATCH - 2) // 2) as j:
                    b_step(i0 + 2 * j, 2 * j, 0, True, True)
                    b_step(i0 + 2 * j + 1, 2 * j + 1, 1, True, True)
                b_step(i0 + (BATCH - 2), BATCH - 2, 0, True, False)
                b_step(i0 + (BATCH - 1), BATCH - 1, 1, False, False)
                s.wait_ge(ld_ffn, (l + 1) * (16 * FFN_LOADS))
                for g in range(GROUPS):
                    f_body(l * GROUPS + g)

            for g in range(GROUPS):
                s.wait_ge(S("last_sh"), g + 1)
                for n in range(GT):
                    m = s.activation(xl[:, g, n, :], full(g)[:, n * PARTS:(n + 1) * PARTS], ACT.Identity,
                                     bias=shl[:, g, n:n + 1], scale=rsl[:, g, n:n + 1])
                m.then_inc(S("last_n"), 1)

        @block.vector
        def _(v):
            for name in ("a_xn a_rope a_parts a_mx a_mp a_inv a_o a_yin a_ve2 a_h0 b_tab b_ss b_n2 b_rot b_r8 b_mx "
                         "b_nm b_inv b_p b_pT_dve b_x f_st f_mv f_hT f_ve f_y f_yT f_act f_x").split():
                v.sem_inc(S(name), ONE)
            v.memset(minus_half[:, :], -0.5).then_inc(S("half"), 1)
            own_x = Own(v, S("dve_ax"), 4)
            own_m = Own(v, S("dve_am"), 3)
            own_t = Own(v, S("dve_at"), 7)

            def bcast_heads(x, n, h, d):
                return x.unsqueeze(2).broadcast_to([PARTS, n, h, d])

            def a_stats(k, b0, b1):
                v.wait_ge(ld_x if k else ld_x0, 16)
                for b in range(b0, b1):
                    for n in range(TILES):
                        m = v.bn_stats(st[:, b, n, :], x_all[:, b, n, :])
                m.then_inc(S("a_stat"), 1)
                v.wait_ge(S("a_stat"), 2 * k + 1)
                for b in range(b0, b1):
                    for n in range(TILES):
                        m = v.bn_aggr(mv[:, b, n, :], st[:, b, n, :])
                m.then_inc(S("a_stat"), 1)
                v.wait_ge(S("a_stat"), 2 * k + 2)
                v.tensor_scalar(ve[:, b0:b1, :], mv[:, b0:b1, :, 1], EPS, None, ALU.add).then_inc(S("a_ve"), 1)

            def a_norm(b):
                one = bass.ds(b, 1)
                v.wait_ge(S("a_xnT"), ONE + b)
                for n in range(TILES):
                    m = v.tensor_scalar(xn[:, n, :], x_all[:, one, n, :].rearrange("p o d -> p (o d)"),
                                        mv[:, one, n, 0], rs1[:, one, n], ALU.subtract, ALU.mult)
                m.then_inc(S("a_xn"), 1)

            def a_rope(b, src=full(7)):
                v.wait_ge(S("a_qkv"), ONE + b + 1)
                v.wait_ge(S("a_v"), ONE + b)
                qkv = src[:, 0:TILES * A_W].rearrange("p (t w) -> p t w", t=TILES)
                w = A_QK * A_D
                qk = qkv[:, :, 0:w].rearrange("p t (h d) -> p t h d", d=A_D)
                v.tensor_tensor(rope_c[:, :, :, :], qk, bcast_heads(cos_a, TILES, A_QK, A_D), ALU.mult)
                for k in range(2):
                    v.tensor_tensor(rope_s[:, :, :, k::2], qk[:, :, :, 1 - k::2],
                                    bcast_heads(sin_a[:, :, k::2], TILES, A_QK, A_D // 2), ALU.mult)
                v.tensor_copy(v_new[:, :, :], qkv[:, :, w:A_W]).then_inc(S("a_rope"), 1)

            def a_split(b):
                own_x.begin(b)
                v.wait_ge(S("a_rope"), ONE + b + 1)
                v.wait_ge(S("a_stack"), ONE + b * TILES)
                own_x.step(v.tensor_tensor(rest[:, :, :, :], rope_c[:, :, :, :], rope_s[:, :, :, :], ALU.add))
                for i in range(SPLIT - 1):
                    own_x.step(v.tensor_copy(parts[:, :, :, i, :], rest[:, :, :, :]))
                    last = i == SPLIT - 2
                    m = v.tensor_tensor(parts[:, :, :, i + 1, :] if last else rest[:, :, :, :], rest[:, :, :, :],
                                        parts[:, :, :, i, :], ALU.subtract)
                    if last:
                        m.then_inc(S("a_parts"), 1)
                    else:
                        own_x.step(m)
                own_x.end()

            def a_max(b, u):
                qt, h0, nh = USES_Q[u]
                v.wait_ge(S("a_sc"), ONE + b * NQ + u + 1)
                if u == 0:
                    v.wait_ge(S("a_mp"), ONE + b)
                v.tensor_reduce(mx_a[:, qt, h0:h0 + nh], full(u % 2).rearrange("p (h k) -> p h k", h=nh),
                                AX.X, ALU.max).then_inc(S("a_mx"), 1)

            def a_split_m(b):
                own_m.begin(b)
                v.wait_ge(S("a_mx"), ONE + b * NQ + NQ)
                v.wait_ge(S("a_mT"), ONE + b)
                own_m.step(v.tensor_scalar(m_part[:, :, 0, :], mx_a[:, :, :], -1.0, None, ALU.mult))
                own_m.step(v.scalar_tensor_tensor(out=m_left[:, :, :], in0=mx_a[:, :, :], scalar=-1.0,
                                                  in1=m_part[:, :, 0, :], op0=ALU.mult, op1=ALU.subtract))
                own_m.step(v.tensor_copy(m_part[:, :, 1, :], m_left[:, :, :]))
                v.tensor_tensor(m_part[:, :, 2, :], m_left[:, :, :], m_part[:, :, 1, :], ALU.subtract)\
                    .then_inc(S("a_mp"), 1)

            def a_o(b):
                v.wait_ge(S("a_back"), ONE + b + 1)
                both = bank[2][:, :].rearrange("p (t h c) -> p t h c", t=TILES, c=A_COLS)
                v.reciprocal(inv_a[:, :, :], both[:, :, :, A_D]).then_inc(S("a_inv"), 1)
                v.wait_ge(S("a_inv"), ONE + b + 1)
                v.wait_ge(S("a_oT"), ONE + b)
                v.tensor_tensor(o_a[:, :, :].rearrange("p t (h d) -> p t h d", d=A_D), both[:, :, :, 0:A_D],
                                inv_a[:, :, :].unsqueeze(3).broadcast_to([PARTS, TILES, A_HEADS, A_D]), ALU.mult)\
                    .then_inc(S("a_o"), 1)

            def a_stats_of(b, k, src):
                for n in range(TILES):
                    m = v.bn_stats(st2[:, n, :], src[:, n, :])
                own_t.step(m)
                plain(v)
                for n in range(TILES):
                    m = v.bn_aggr(mv2[:, n, :], st2[:, n, :])
                own_t.step(m)
                v.tensor_scalar(ve2[:, :], mv2[:, :, 1], EPS, None, ALU.add).then_inc(S("a_ve2"), 1)

            def a_y(b):
                own_t.begin(b)
                v.wait_ge(S("a_y"), ONE + b + 1)
                v.tensor_tensor(y_a[:, :, :], full(4)[:, 0:TILES * DIM].rearrange("p (t d) -> p t d", t=TILES),
                                bout[:, :].unsqueeze(1).broadcast_to([PARTS, TILES, DIM]), ALU.add)\
                    .then_inc(S("a_yin"), 1)
                v.wait_ge(S("a_yin"), ONE + b + 1)
                a_stats_of(b, 0, y_a)

            def a_x1(b):
                v.wait_ge(S("a_rs2"), ONE + 2 * b + 1)
                v.wait_ge(S("a_h0T"), ONE + b)
                for n in range(TILES):
                    m = v.tensor_scalar(y_a[:, n, :], y_a[:, n, :], mv2[:, n, 0:1], rs2[:, n:n + 1],
                                        ALU.subtract, ALU.mult)
                own_t.step(m)
                x1 = x_all[:, bass.ds(b, 1), :, :].rearrange("p o t d -> p (o t) d")
                own_t.step(v.tensor_tensor(z_a[:, :, :], y_a[:, :, :], x1, ALU.add))
                a_stats_of(b, 1, z_a)
                own_t.step(v.tensor_tensor(x1, y_a[:, :, :], x1, ALU.add))

            def a_h0(b):
                v.wait_ge(S("a_rs2"), ONE + 2 * b + 2)
                for n in range(TILES):
                    m = v.tensor_scalar(z_a[:, n, :], z_a[:, n, :], mv2[:, n, 0:1], rs2[:, n:n + 1],
                                        ALU.subtract, ALU.mult)
                m.then_inc(S("a_h0"), 1)
                own_t.end()

            def a_step(b, prev, one, two):
                def maxima(u0, u1):
                    if one:
                        for u in range(u0, u1):
                            a_max(b + 1, u)

                if two:
                    a_norm(b + 2)
                if prev:
                    a_y(b - 1)
                maxima(0, 1)
                if two:
                    a_rope(b + 2)
                maxima(1, 3)
                if two:
                    a_split(b + 2)
                maxima(3, 5)
                if prev:
                    a_x1(b - 1)
                maxima(5, 8)
                if prev:
                    a_h0(b - 1)
                maxima(8, NQ)
                if one:
                    a_split_m(b + 1)
                a_o(b)

            a_stats(0, 0, 2)
            v.wait_ge(ld_ident, 16)
            v.tensor_copy(ident_h[:, :], ident).then_inc(S("ident_cast"), 1)
            v.wait_ge(S("a_rs"), 1)
            a_norm(0)
            for par in range(2):
                m = v.memset(qkT_a[par][64:A_STACK + SPLIT, A_HEADS:A_QK, :], 1.0)
            m.then_inc(S("a_rows"), 1)
            a_norm(1)
            v.wait_ge(ld_c, 16)
            a_rope(0)
            a_split(0)
            v.tensor_copy(ident_4[:, :, :], ident.unsqueeze(1).broadcast_to([PARTS, 4, PARTS]))
            v.tensor_copy(mask_a[:, :, :], const[:, C_MA:C_MB0].unsqueeze(1).broadcast_to([PARTS, 4, PARTS]))\
                .then_inc(S("mask_cast"), 1)
            a_rope(1, full(5))
            a_split(1)
            a_stats(1, 2, BATCH)
            v.wait_ge(S("a_rs"), 2)
            for par in range(2):
                v.memset(v_a[par][:, :, :, A_D:A_D + 1], 1.0)
                m = v.memset(v_a[par][:, :, :, A_D + 1:A_COLS], 0.0)
            m.then_inc(S("a_ones"), 1)
            for u in range(NQ):
                a_max(0, u)
            a_split_m(0)
            v.tensor_copy(mask_b0[:, :, :], const[:, C_MB0:C_MB1].unsqueeze(1).broadcast_to([PARTS, 4, PARTS]))
            v.tensor_copy(mask_b1[:, :, :], const[:, C_MB1:C_RA].unsqueeze(1).broadcast_to([PARTS, 2, B1K]))\
                .then_inc(S("b_masks"), 1)
            v.memset(hT[64:128, 0:1], 0.0)
            v.memset(hTf[64:128, :, 0:1], 0.0)
            for par in range(2):
                m = v.memset(p_b1[par][:, :, 0:WINDOW], 0.0)
            m.then_inc(S("b_zero"), 1)
            a_step(0, False, True, True)
            with v.Fori(1, BATCH - 2) as b:
                a_step(b, True, True, True)
            a_step(BATCH - 2, True, True, False)
            a_step(BATCH - 1, True, False, False)
            a_y(BATCH - 1)
            a_x1(BATCH - 1)
            a_h0(BATCH - 1)

            def l_tables(l):
                v.wait_ge(ld_att, l * 64 + 64)
                v.wait_ge(S("b_rot"), ONE + l * (BATCH * TILES))
                for n in range(TILES):
                    v.tensor_tensor(tab_c[:, n, :, :], rot_raw[:, 0, n, :, :], scales[:, :, :], ALU.mult)
                    for k in range(2):
                        o = slice(k * (HD // 2), (k + 1) * (HD // 2))
                        p = slice((1 - k) * (HD // 2), (2 - k) * (HD // 2))
                        m = v.tensor_tensor(tab_s[:, n, :, o], rot_raw[:, 1, n, :, o], scales[:, :, p], ALU.mult)
                m.then_inc(S("b_tab"), 1)
                v.wait_ge(S("b_tab"), ONE + l + 1)

            def b_norms(i, n):
                v.wait_ge(S("b_sq"), ONE + 2 * i + n + 1)
                v.wait_ge(S("b_r"), ONE + 2 * i)
                v.tensor_reduce(ss[:, n, :], sq[:, n, :, :].rearrange("p c (h d) -> p (c h) d", d=HD), AX.X, ALU.add)\
                    .then_inc(S("b_ss"), 1)
                v.wait_ge(S("b_ss"), ONE + 2 * i + n + 1)
                v.tensor_scalar(ss[:, n, :], ss[:, n, :], TINY, None, ALU.max).then_inc(S("b_n2"), 1)

            def b_rot(i, n, bank_qk=pj, first=False):
                v.wait_ge(S("b_trT"), ONE + 4 * i - (0 if first else 2 * (TILES - 1 - n)))
                v.wait_ge(S("b_sq"), ONE + 2 * i + n + 1)
                src = bank_qk[:, :].rearrange("p (c h d) -> p c h d", c=2, d=HD)
                v.tensor_tensor(rc[:, n, :, :].rearrange("p c (h d) -> p c h d", d=HD), src,
                                tab_c[:, n, :, :].unsqueeze(2).broadcast_to([PARTS, 2, HEADS, HD]), ALU.mult)
                dst = rs[:, n, :, :].rearrange("p c (h d) -> p c h d", d=HD)
                for k in range(2):
                    o = slice(k * (HD // 2), (k + 1) * (HD // 2))
                    p = slice((1 - k) * (HD // 2), (2 - k) * (HD // 2))
                    m = v.tensor_tensor(dst[:, :, :, o], src[:, :, :, p],
                                        tab_s[:, n, :, o].unsqueeze(2).broadcast_to([PARTS, 2, HEADS, HD // 2]), ALU.mult)
                m.then_inc(S("b_rot"), 1)

            def b_r8(x, par, first=False):
                v.wait_ge(S("b_r"), ONE + 2 * x + 2)
                v.wait_ge(S("b_exp"), ONE + done(x, NUB, first))
                v.tensor_scalar(r_q8[par][:, :, :], r_qk[:, :, 0:HEADS], QK_SCALE, None, ALU.mult)\
                    .then_inc(S("b_r8"), 1)

            def b_max(x, par, u):
                qt, heads = USES_B[u]
                nk = keys_b(qt)
                v.wait_ge(S("b_sc"), ONE + x * NUB + u + 1)
                hs = slice(heads[0], heads[-1] + 1, 2)
                v.tensor_reduce(mx_b[par][:, qt, hs],
                                sc_b[u % 3][:, 0:len(heads) * nk].rearrange("p (h k) -> p h k", k=nk),
                                AX.X, ALU.max).then_inc(S("b_mx"), 1)
                v.wait_ge(S("b_mx"), ONE + x * NUB + u + 1)
                v.scalar_tensor_tensor(out=nm_b[par][:, qt, hs], in0=mx_b[par][:, qt, hs], scalar=-1.0,
                                       in1=r_q8[par][:, qt, hs], op0=ALU.mult, op1=ALU.mult).then_inc(S("b_nm"), 1)

            def b_probs(i, par, k):
                v.wait_ge(S("b_exp"), ONE + i * NUB + (4 if k == 0 else 6))
                h0 = 4 * k
                v.reciprocal(inv_b[par][:, :, h0:h0 + 4], sum_b[par][:, :, h0:h0 + 4]).then_inc(S("b_inv"), 1)
                v.wait_ge(S("b_inv"), ONE + 2 * i + k + 1)
                for h in range(h0, h0 + 4):
                    for qt in range(2):
                        m = v.tensor_scalar(p_slice_b(par, qt, h), p_slice_b(par, qt, h),
                                            inv_b[par][:, qt, h:h + 1], None, ALU.mult)
                    m.then_inc(S("b_p"), 1)

            def b_pT_out(i, h):
                v.wait_ge(S("b_pT"), ONE + i * HEADS + h + 1)
                if h >= 4:
                    v.wait_ge(S("b_pv"), ONE + i * PAIRS + h // 2 - 1)
                v.tensor_copy(pT_b[:, h % 4, :], pt_b[h % 2][:, 0:PARTS + SEQ]).then_inc(S("b_pT_dve"), 1)

            def b_x(i, b):
                v.wait_ge(S("b_y"), ONE + i + 1)
                x = xT[:, bass.ds(b, 1), :].rearrange("p o s -> p (o s)")
                v.tensor_tensor(x, ov_b[:, 0:SEQ], x, ALU.add).then_inc(S("b_x"), 1)

            def b_step(i, b, par, one, two, group=None):
                nxt = 1 - par
                last = group is not None
                b_max(i, par, 4)
                b_probs(i, par, 0)
                b_max(i, par, 5)
                if last:
                    f_hT(group, 0)
                b_pT_out(i, 1)
                b_pT_out(i, 3)
                b_probs(i, par, 1)
                if last:
                    f_stats(group)
                b_pT_out(i, 5)
                if last:
                    f_norm(group)
                b_pT_out(i, 7)
                if one:
                    b_r8(i + 1, nxt)
                    b_max(i + 1, nxt, 0)
                    b_max(i + 1, nxt, 1)
                if last:
                    f_yT(group)
                if two:
                    b_rot(i + 2, 0)
                if one:
                    b_max(i + 1, nxt, 2)
                if two:
                    b_norms(i + 2, 0)
                if one:
                    b_max(i + 1, nxt, 3)
                if two:
                    b_rot(i + 2, 1)
                    b_norms(i + 2, 1)
                b_x(i, b)

            def f_hT(i, g):
                v.wait_ge(S("f_h"), ONE + i)
                plain(v)
                src = xT[:, bass.ds(g * 2, 2), :]
                v.tensor_copy(hTf[0:64, :, :], src[0:64, :, :])
                v.tensor_copy(hTf[64:128, :, 1:SEQ], src[64:128, :, 0:SEQ - 1]).then_inc(S("f_hT"), 1)

            def f_stats(i):
                v.wait_ge(S("f_h"), ONE + i + 1)
                for n in range(GT):
                    m = v.bn_stats(stf[:, n, :], lnf[0][:, n * PARTS:(n + 1) * PARTS])
                m.then_inc(S("f_st"), 1)
                v.wait_ge(S("f_st"), ONE + i + 1)
                plain(v)
                for n in range(GT):
                    m = v.bn_aggr(mvf[:, n, :], stf[:, n, :])
                m.then_inc(S("f_mv"), 1)
                v.wait_ge(S("f_mv"), ONE + i + 1)
                v.tensor_scalar(vef[:, :], mvf[:, :, 1], EPS, None, ALU.add).then_inc(S("f_ve"), 1)

            def f_norm(i):
                v.wait_ge(S("f_rs"), ONE + i + 1)
                v.wait_ge(S("f_ty"), ONE + i)
                for n in range(GT):
                    m = v.tensor_scalar(yf[:, n, :], lnf[0][:, n * PARTS:(n + 1) * PARTS], mvf[:, n, 0:1],
                                        rsf[:, n:n + 1], ALU.subtract, ALU.mult)
                m.then_inc(S("f_y"), 1)

            def f_yT(i):
                v.wait_ge(S("f_ty"), ONE + i + 1)
                v.wait_ge(S("f_up"), ONE + i * (2 * NCH))
                v.tensor_scalar(yfT[:, :], lnf[1], ln_g[:, 0:1], ln_b[:, 0:1], ALU.mult, ALU.add).then_inc(S("f_yT"), 1)

            def f_act(i, c):
                h0, n = HCH[c]
                v.wait_ge(S("f_up"), ONE + i * (2 * NCH) + 2 * c + 2)
                v.wait_ge(S("f_gate"), ONE + i * NCH + c + 1)
                v.wait_ge(S("f_down"), ONE + i)
                v.scalar_tensor_tensor(out=act[0:n, c, :], in0=up[1][c % 2][0:n, :], scalar=b1[0:n, 0, c:c + 1],
                                       in1=gate[0:n, c, :], op0=ALU.add, op1=ALU.mult).then_inc(S("f_act"), 1)

            def f_x(i, g):
                v.wait_ge(S("f_down"), ONE + i + 1)
                x = xT[:, bass.ds(g * 2, 2), :].rearrange("p o s -> p (o s)")
                v.scalar_tensor_tensor(out=x, in0=down[:, :], scalar=b2[:, 0:1], in1=x, op0=ALU.add, op1=ALU.add)\
                    .then_inc(S("f_x"), 1)

            def f_body(i, g, more):
                if more:
                    f_hT(i + 1, g + 1)
                f_act(i, 0)
                if more:
                    f_stats(i + 1)
                f_act(i, 1)
                if more:
                    f_norm(i + 1)
                f_act(i, 2)
                if more:
                    f_yT(i + 1)
                f_x(i, g)

            with v.Fori(0, DEPTH) as l:
                i0 = l * BATCH
                g0 = l * GROUPS
                v.wait_ge(S("a_h0T_out"), ONE + BATCH)
                v.wait_ge(S("f_x"), ONE + g0)
                v.wait_ge(S("b_vp"), ONE + TILES * i0)
                plain(v)
                v.tensor_copy(hT[0:64, :], xT[0:64, 0, :]).then_inc(S("b_hT"), 1)
                v.tensor_copy(hT[64:128, 1:SEQ], xT[64:128, 0, 0:SEQ - 1]).then_inc(S("b_hT"), 1)
                l_tables(l)
                for n in range(TILES):
                    b_rot(i0, n, bank[n], first=True)
                    b_norms(i0, n)
                    v.wait_ge(S("b_rot"), ONE + 2 * i0 + n + 1)
                    v.tensor_tensor(rc[:, n, :, :], rc[:, n, :, :], rs[:, n, :, :], ALU.add).then_inc(S("b_add"), 1)
                b_r8(i0, 0, first=True)
                b_rot(i0 + 1, 0, bank[3])
                b_norms(i0 + 1, 0)
                for u in range(3):
                    b_max(i0, 0, u)
                b_rot(i0 + 1, 1)
                b_norms(i0 + 1, 1)
                b_max(i0, 0, 3)
                with v.Fori(0, (BATCH - 2) // 2) as j:
                    b_step(i0 + 2 * j, 2 * j, 0, True, True)
                    b_step(i0 + 2 * j + 1, 2 * j + 1, 1, True, True)
                b_step(i0 + (BATCH - 2), BATCH - 2, 0, True, False)
                v.wait_ge(ld_ffn, (l + 1) * (16 * FFN_LOADS))
                b_step(i0 + (BATCH - 1), BATCH - 1, 1, False, False, g0)
                with v.Fori(0, GROUPS - 1) as g:
                    f_body(g0 + g, g, True)
                f_body(g0 + (GROUPS - 1), GROUPS - 1, False)

            def last_stats(g):
                v.wait_ge(S("last_t"), g + 1)
                for n in range(GT):
                    m = v.bn_stats(stl[:, g, n, :], full(g)[:, n * PARTS:(n + 1) * PARTS])
                m.then_inc(S("last_st"), 1)
                v.wait_ge(S("last_st"), g + 1)
                for n in range(GT):
                    m = v.bn_aggr(mvl[:, g, n, :], stl[:, g, n, :])
                m.then_inc(S("last_mv"), 1)
                v.wait_ge(S("last_mv"), g + 1)
                v.tensor_scalar(vel[:, g, :], mvl[:, g, :, 1], EPS, None, ALU.add).then_inc(S("last_ve"), 1)

            def last_shift(g):
                v.wait_ge(S("last_rs"), g + 1)
                v.scalar_tensor_tensor(out=shl[:, g, :], in0=mvl[:, g, :, 0], scalar=-1.0, in1=rsl[:, g, :],
                                       op0=ALU.mult, op1=ALU.mult).then_inc(S("last_sh"), 1)

            def last_sum(g):
                v.wait_ge(S("last_n"), g + 1)
                v.tensor_tensor(xl[:, g, :, :], xl[:, g, :, :],
                                x_all[:, 2 * g:2 * g + 2, :, :].rearrange("p b t d -> p (b t) d"), ALU.add)\
                    .then_inc(S("last_done"), 1)

            last_stats(0)
            for g in range(1, GROUPS):
                last_stats(g)
                last_shift(g - 1)
            last_sum(0)
            last_shift(GROUPS - 1)
            for g in range(1, GROUPS):
                last_sum(g)

        @block.gpsimd
        def _(g):
            for name in ("a_v a_rs2 b_r b_add b_qkr f_rs").split():
                g.sem_inc(S(name), ONE)
            g.wait_ge(S("half"), 1)

            def a_rs(k, b0, b1):
                g.wait_ge(S("a_ve"), k + 1)
                w = (b1 - b0) * TILES
                g.tensor_tensor(rs1[:, b0:b1, :].rearrange("p b t -> p (b t)"),
                                ve[:, b0:b1, :].rearrange("p b t -> p (b t)"), minus_half[:, 0:w], ALU.pow)\
                    .then_inc(S("a_rs"), 1)

            def a_v(b, par, first=False):
                g.wait_ge(S("a_rope"), ONE + b + 1)
                if not first:
                    g.wait_ge(S("a_pv"), ONE + (b - 1) * A_KV)
                plain(g)
                g.tensor_copy(v_a[par][:, :, :, 0:A_D], v_new[:, :, :].rearrange("p t (h d) -> p t h d", d=A_D))\
                    .then_inc(S("a_v"), 1)

            def a_rs2(b):
                for k in range(2):
                    g.wait_ge(S("a_ve2"), ONE + 2 * b + k + 1)
                    g.tensor_tensor(rs2[:, :], ve2[:, :], minus_half[:, 0:TILES], ALU.pow).then_inc(S("a_rs2"), 1)

            def a_step(b, par, prev, one):
                if one:
                    a_v(b + 1, 1 - par)
                if prev:
                    a_rs2(b - 1)

            a_rs(0, 0, 2)
            a_v(0, 0, first=True)
            a_rs(1, 2, BATCH)
            a_step(0, 0, False, True)
            with g.Fori(0, (BATCH - 2) // 2) as j:
                a_step(2 * j + 1, 1, True, True)
                a_step(2 * j + 2, 0, True, True)
            a_step(BATCH - 1, 1, True, False)
            a_rs2(BATCH - 1)

            def b_norm(i, n, first=False):
                if not first:
                    g.wait_ge(S("b_rot"), ONE + 2 * i + n + 1)
                    g.tensor_tensor(rc[:, n, :, :], rc[:, n, :, :], rs[:, n, :, :], ALU.add).then_inc(S("b_add"), 1)
                g.wait_ge(S("b_n2"), ONE + 2 * i + n + 1)
                g.wait_ge(S("b_r8"), ONE + i)
                g.tensor_tensor(r_qk[:, n, :], ss[:, n, :], minus_half[:, :], ALU.pow).then_inc(S("b_r"), 1)
                g.wait_ge(S("b_r"), ONE + 2 * i + n + 1)
                g.wait_ge(S("b_add"), ONE + 2 * i + n + 1)
                k = rc[:, n, 1, :].rearrange("p (h d) -> p h d", d=HD)
                g.tensor_tensor(k, k, r_qk[:, n, HEADS:2 * HEADS].unsqueeze(2).broadcast_to([PARTS, HEADS, HD]),
                                ALU.mult).then_inc(S("b_qkr"), 1)

            def f_rs(i):
                g.wait_ge(S("f_ve"), ONE + i + 1)
                g.tensor_tensor(rsf[:, :], vef[:, :], minus_half[:, 0:GT], ALU.pow).then_inc(S("f_rs"), 1)

            with g.Fori(0, DEPTH) as l:
                for n in range(TILES):
                    b_norm(l * BATCH, n, first=True)
                with g.Fori(1, BATCH) as b:
                    for n in range(TILES):
                        b_norm(l * BATCH + b, n)
                with g.Fori(0, GROUPS) as q:
                    f_rs(l * GROUPS + q)

            for q in range(GROUPS):
                g.wait_ge(S("last_ve"), q + 1)
                g.tensor_tensor(rsl[:, q, :], vel[:, q, :], minus_half[:, 0:GT], ALU.pow).then_inc(S("last_rs"), 1)


_INS = ["L0_attn_x", "L0_attn_Wqa", "L0_attn_Wqb", "L0_attn_Wkva", "L0_attn_Wkvb", "L0_attn_Wout", "L0_attn_bout",
        "L0_ffn_wqkv", "L0_ffn_q_scale", "L0_ffn_k_scale", "L0_ffn_wo", "L0_ffn_ln_g", "L0_ffn_ln_b", "L0_ffn_w1",
        "L0_ffn_b1", "L0_ffn_w2", "L0_ffn_b2"]


def kernel(**inputs):
    import numpy as _np
    import concourse.bacc as _bacc
    from concourse import mybir as _mybir
    from concourse.bass_utils import run_bass_kernel_spmd as _run

    nc = _bacc.Bacc("TRN2", target_bir_lowering=False, num_devices=1)
    arrays, args = {}, {}
    for name in _INS:
        x = _np.ascontiguousarray(inputs[name])
        arrays[f"in_{name}_dram"] = x
        args[name] = nc.dram_tensor(f"in_{name}_dram", x.shape, _mybir.dt.from_np(x.dtype), kind="ExternalInput").ap()
    arrays["consts_dram"] = shape_constants()
    args["consts"] = nc.dram_tensor("consts_dram", arrays["consts_dram"].shape, _mybir.dt.float32,
                                    kind="ExternalInput").ap()
    out = nc.dram_tensor("out_dram", (BATCH, SEQ, DIM), _mybir.dt.float32, kind="ExternalOutput").ap()
    build_program(nc, args, out)
    r = _run(nc, [arrays], core_ids=[0])
    return r.results[0]["out_dram"]
```
